# Optimizing a Trainium2 kernel written in Bass

```python
import numpy as np
import jax
import jax.numpy as jnp

def _softmax(x, axis=-1):
    return jax.nn.softmax(x, axis=axis)

def _gelu(x):
    return jax.nn.gelu(x, approximate=True)

def _silu(x):
    return jax.nn.silu(x)

def _sigmoid(x):
    return jax.nn.sigmoid(x)

def _layernorm(x, axis=-1, eps=1e-05):
    m = jnp.mean(x, axis=axis, keepdims=True)
    v = jnp.var(x, axis=axis, keepdims=True)
    return (x - m) / jnp.sqrt(v + eps)

def _scatter_add(tgt, idx, src, axis=0):
    return tgt.at[idx].add(src)

def _segment_sum(src, seg, n):
    return jax.ops.segment_sum(src, seg, n)
kernel_name = 'mk_adj_ffn_d1_adj_r2_f0e5ef'

def setup_inputs(seed: int=0):
    np.random.seed(seed)
    _w = jnp.asarray

    def _rec_inputs():
        import jax
        import jax.numpy as jnp
        _gk = jax.random.key(seed)
        x = -0.000929 + 1 * jax.random.normal(jax.random.fold_in(_gk, 1), (2048, 128), jnp.float32)
        _a = jax.random.bernoulli(jax.random.fold_in(_gk, 2), 0.0078125, (2048, 2048))
        adj = _a.astype(jnp.int32)
        return (x, adj)
    x, adj = _rec_inputs()

    def _L0_gnn_setup():
        import jax, jax.numpy as jnp
        import numpy as np
        N, IN_C, OUT_C, H, CF = (2048, 128, 128, 8, 6)
        D = OUT_C // H
        key = jax.random.key(seed)
        ks = jax.random.split(key, 8)
        x = jax.random.normal(ks[0], (N, IN_C), dtype=jnp.float32)
        positions = jax.random.normal(ks[1], (N, 3), dtype=jnp.float32)
        curv_feats = jax.random.normal(ks[2], (N, CF), dtype=jnp.float32)
        adj = jax.random.randint(ks[3], (N, N), 0, 2, dtype=jnp.int32)
        W = jax.random.normal(ks[4], (OUT_C, IN_C), dtype=jnp.float32) * 0.05
        a_l = jax.random.normal(ks[5], (H, D), dtype=jnp.float32) * 0.1
        a_r = jax.random.normal(ks[6], (H, D), dtype=jnp.float32) * 0.1
        Wc = jax.random.normal(ks[7], (H, CF), dtype=jnp.float32) * 0.1
        gate = jnp.asarray(0.1, dtype=jnp.float32)
        return {'x': x, 'positions': positions, 'curv_feats': curv_feats, 'adj': adj, 'W': W, 'a_l': a_l, 'a_r': a_r, 'Wc': Wc, 'gate': gate}
    _L0_gnn_all = _L0_gnn_setup()
    _L0_gnn_in = {k: v for k, v in _L0_gnn_all.items() if k in ('positions', 'curv_feats', 'W', 'a_l', 'a_r', 'Wc', 'gate')}
    del _L0_gnn_all

    def _L0_ffn_setup():
        import jax, jax.numpy as jnp
        import numpy as np
        B, T, C = (64, 192, 128)
        NH, NKV = (4, 2)
        HD = C // NH
        NREP = NH // NKV
        NE, TOPK = (8, 2)
        HID = int(8 / 3 * C)
        EPS_RMS = 1e-06

        def _rope_tables(t_len):
            inv_freq = 1.0 / 10000.0 ** (np.arange(0, HD, 2, dtype=np.float32) / HD)
            t = np.arange(t_len, dtype=np.float32)
            freqs = np.outer(t, inv_freq)
            emb = np.concatenate([freqs, freqs], axis=-1)
            return (jnp.asarray(np.cos(emb)), jnp.asarray(np.sin(emb)))

        def _rotate_half(x):
            h = x.shape[-1] // 2
            return jnp.concatenate([-x[..., h:], x[..., :h]], axis=-1)

        def _rmsnorm(v, w):
            return v * jax.lax.rsqrt(jnp.mean(v * v, axis=-1, keepdims=True) + EPS_RMS) * w
        key = jax.random.key(seed)
        ks = jax.random.split(key, 10)
        s = lambda k, shape: jax.random.normal(k, shape, jnp.float32) * 0.02
        return {'x': jax.random.normal(ks[0], (B, T, C), jnp.float32), 'ln1_w': jnp.ones((C,), jnp.float32), 'ln2_w': jnp.ones((C,), jnp.float32), 'wq': s(ks[1], (NH * HD, C)), 'wk': s(ks[2], (NKV * HD, C)), 'wv': s(ks[3], (NKV * HD, C)), 'wo': s(ks[4], (C, C)), 'router_w': s(ks[5], (NE, C)), 'w1': s(ks[6], (NE, HID, C)), 'w2': s(ks[7], (NE, C, HID)), 'w3': s(ks[8], (NE, HID, C))}
    _L0_ffn_all = _L0_ffn_setup()
    _L0_ffn_in = {k: v for k, v in _L0_ffn_all.items() if k in ('ln1_w', 'ln2_w', 'wq', 'wk', 'wv', 'wo', 'router_w', 'w1', 'w2', 'w3')}
    del _L0_ffn_all
    return {'x': x, 'adj': adj, 'L0_gnn_positions': _L0_gnn_in['positions'], 'L0_gnn_curv_feats': _L0_gnn_in['curv_feats'], 'L0_gnn_W': _L0_gnn_in['W'], 'L0_gnn_a_l': _L0_gnn_in['a_l'], 'L0_gnn_a_r': _L0_gnn_in['a_r'], 'L0_gnn_Wc': _L0_gnn_in['Wc'], 'L0_gnn_gate': _L0_gnn_in['gate'], 'L0_ffn_ln1_w': _L0_ffn_in['ln1_w'], 'L0_ffn_ln2_w': _L0_ffn_in['ln2_w'], 'L0_ffn_wq': _L0_ffn_in['wq'], 'L0_ffn_wk': _L0_ffn_in['wk'], 'L0_ffn_wv': _L0_ffn_in['wv'], 'L0_ffn_wo': _L0_ffn_in['wo'], 'L0_ffn_router_w': _L0_ffn_in['router_w'], 'L0_ffn_w1': _L0_ffn_in['w1'], 'L0_ffn_w2': _L0_ffn_in['w2'], 'L0_ffn_w3': _L0_ffn_in['w3']}

def reference(x, adj, L0_gnn_positions, L0_gnn_curv_feats, L0_gnn_W, L0_gnn_a_l, L0_gnn_a_r, L0_gnn_Wc, L0_gnn_gate, L0_ffn_ln1_w, L0_ffn_ln2_w, L0_ffn_wq, L0_ffn_wk, L0_ffn_wv, L0_ffn_wo, L0_ffn_router_w, L0_ffn_w1, L0_ffn_w2, L0_ffn_w3):
    import jax
    import jax.numpy as jnp

    def _L0_gnn_ref(x, positions, curv_feats, adj, W, a_l, a_r, Wc, gate):
        import jax, jax.numpy as jnp
        import numpy as np
        N, IN_C, OUT_C, H, CF = (2048, 128, 128, 8, 6)
        D = OUT_C // H
        n = x.shape[0]
        h = (x @ W.T).reshape(n, H, D)
        e_l = jnp.einsum('nhd,hd->nh', h, a_l)
        e_r = jnp.einsum('nhd,hd->nh', h, a_r)
        logits = jax.nn.leaky_relu(e_l[:, None, :] + e_r[None, :, :], negative_slope=0.2)
        curv_pair = jnp.abs(curv_feats[:, None, :] - curv_feats[None, :, :])
        curv_bias = jnp.einsum('ijf,hf->ijh', curv_pair, Wc)
        logits = logits + gate * curv_bias
        mask = (adj > 0)[:, :, None]
        logits = jnp.where(mask, logits, jnp.float32(-1000000000.0))
        attn = jax.nn.softmax(logits, axis=1)
        out = jnp.einsum('ijh,jhd->ihd', attn, h)
        return out.reshape(n, H * D)

    def _L0_ffn_ref(x, ln1_w, ln2_w, wq, wk, wv, wo, router_w, w1, w2, w3):
        import jax, jax.numpy as jnp
        import numpy as np
        B, T, C = (64, 192, 128)
        NH, NKV = (4, 2)
        HD = C // NH
        NREP = NH // NKV
        NE, TOPK = (8, 2)
        HID = int(8 / 3 * C)
        EPS_RMS = 1e-06

        def _rope_tables(t_len):
            inv_freq = 1.0 / 10000.0 ** (np.arange(0, HD, 2, dtype=np.float32) / HD)
            t = np.arange(t_len, dtype=np.float32)
            freqs = np.outer(t, inv_freq)
            emb = np.concatenate([freqs, freqs], axis=-1)
            return (jnp.asarray(np.cos(emb)), jnp.asarray(np.sin(emb)))

        def _rotate_half(x):
            h = x.shape[-1] // 2
            return jnp.concatenate([-x[..., h:], x[..., :h]], axis=-1)

        def _rmsnorm(v, w):
            return v * jax.lax.rsqrt(jnp.mean(v * v, axis=-1, keepdims=True) + EPS_RMS) * w
        Bx, Tx, Cx = x.shape
        h = _rmsnorm(x, ln1_w)
        q = (h @ wq.T).reshape(Bx, Tx, NH, HD).transpose(0, 2, 1, 3)
        k = (h @ wk.T).reshape(Bx, Tx, NKV, HD).transpose(0, 2, 1, 3)
        v = (h @ wv.T).reshape(Bx, Tx, NKV, HD).transpose(0, 2, 1, 3)
        cos, sin = _rope_tables(Tx)
        cos, sin = (cos[None, None], sin[None, None])
        q = q * cos + _rotate_half(q) * sin
        k = k * cos + _rotate_half(k) * sin
        k = jnp.repeat(k, NREP, axis=1)
        v = jnp.repeat(v, NREP, axis=1)
        scores = jnp.einsum('bhtd,bhsd->bhts', q, k) / jnp.sqrt(jnp.float32(HD))
        causal = jnp.tril(jnp.ones((Tx, Tx), dtype=bool))
        scores = jnp.where(causal[None, None], scores, jnp.float32(-1e+30))
        att = jax.nn.softmax(scores, axis=-1)
        y = jnp.einsum('bhts,bhsd->bhtd', att, v).transpose(0, 2, 1, 3).reshape(Bx, Tx, Cx)
        x = x + y @ wo.T
        flat = _rmsnorm(x, ln2_w).reshape(-1, Cx)
        probs = jax.nn.softmax(flat @ router_w.T, axis=-1)
        tp, ti = jax.lax.top_k(probs, TOPK)
        tp = tp / (jnp.sum(tp, axis=-1, keepdims=True) + 1e-09)
        weights = jnp.sum(tp[..., None] * jax.nn.one_hot(ti, NE, dtype=flat.dtype), axis=1)
        out = jnp.zeros_like(flat)
        for e in range(NE):
            hh = jax.nn.silu(flat @ w1[e].T) * (flat @ w3[e].T)
            out = out + weights[:, e:e + 1] * (hh @ w2[e].T)
        return x + out.reshape(Bx, Tx, Cx)
    x = x + _L0_gnn_ref(_layernorm(x, axis=-1), L0_gnn_positions, L0_gnn_curv_feats, adj, L0_gnn_W, L0_gnn_a_l, L0_gnn_a_r, L0_gnn_Wc, L0_gnn_gate)
    x = x + _L0_ffn_ref(_layernorm(x, axis=-1)[None], L0_ffn_ln1_w, L0_ffn_ln2_w, L0_ffn_wq, L0_ffn_wk, L0_ffn_wv, L0_ffn_wo, L0_ffn_router_w, L0_ffn_w1, L0_ffn_w2, L0_ffn_w3)[0]
    return x

_drawn_inputs = setup_inputs


def setup_inputs(seed=0):
    import zlib

    import numpy as np

    out = dict(_drawn_inputs(seed))
    spreads = {'L0_ffn_ln1_w': (1.0, 0.6), 'L0_ffn_ln2_w': (1.0, 0.6)}
    factors = {'L0_gnn_curv_feats': 8.0,
     'L0_gnn_a_l': 4.907,
     'L0_gnn_Wc': 8.0,
     'L0_ffn_wq': 8.0,
     'L0_ffn_wk': 8.0,
     'L0_ffn_wv': 8.0,
     'L0_ffn_wo': 8.0,
     'L0_ffn_router_w': 8.0,
     'L0_ffn_w1': 8.0,
     'L0_ffn_w2': 8.0,
     'L0_ffn_w3': 8.0}
    for name, (base, spread) in spreads.items():
        noise = np.random.default_rng([zlib.crc32(name.encode()), seed]).standard_normal(out[name].shape)
        drawn = base * np.exp(spread * noise) if base else spread * noise
        out[name] = jnp.asarray(drawn.astype(out[name].dtype))
    for name, factor in factors.items():
        out[name] = (out[name] * factor).astype(out[name].dtype)
    return out
```

```python
from contextlib import ExitStack

import numpy as np

import concourse.bass as bass
from concourse import mybir

F32 = mybir.dt.float32
F32R = mybir.dt.float32r
BF16 = mybir.dt.bfloat16
I32 = mybir.dt.int32
ALU = mybir.AluOpType
ACT = mybir.ActivationFunctionType
AX = mybir.AxisListType

P = 128
N = 2048
C = 128
NT = N // P
H, D, CF = 8, 16, 6
GI = P // H
GROUPS = N // GI
GPT = P // GI
FR = GI * CF
ER_ROW, CJ_ROW, PAD_ROW, MASK_ROW = FR, FR + H, FR + H + CF, P - GI
HALF = N // 2
LSLOTS = 4
HW = 32
AVG = 4
AVN = AVG * GI
TBANK = [0, 1, 2, 1]
MASKED = 1e9
SLOPE = 0.2
LN_EPS = 1e-5
RMS_EPS = 1e-6

NH, NKV, HD = 4, 2, 32
NREP = NH // NKV
ROPE_BASE = 10000.0
VW = 64
TC = 512
CUT = 1e30
NE, HID = 8, 341
HK = [(0, 128), (128, 128), (256, HID - 256)]


def constants():
    p = np.arange(P)
    c = {}
    c["ident"] = np.eye(P, dtype=np.float32)
    coef = np.zeros((P, P), np.float32)
    i_of, h_of = p // H, p % H
    for r in range(FR):
        coef[r] = 2.0 * (i_of == r // CF)
    for r in range(H):
        coef[ER_ROW + r] = SLOPE / (1 - SLOPE) * (h_of == r)
    coef[CJ_ROW:PAD_ROW] = -1.0
    for r in range(GI):
        coef[MASK_ROW + r] = MASKED * (i_of == r)
    c["coef"] = coef
    gated = np.zeros((P, 2), np.float32)
    gated[:FR, 0] = 1
    gated[CJ_ROW:PAD_ROW, 0] = 1
    gated[:, 1] = 1 - gated[:, 0]
    c["gated"] = gated
    c["headsel"] = (p[:, None] // D == h_of[None, :]).astype(np.float32)
    c["nodesel"] = ((1 - SLOPE) * (i_of[:, None] == np.arange(GI)[None, :])).astype(np.float32)
    inv = 1.0 / ROPE_BASE ** (np.arange(0, HD, 2, dtype=np.float32) / HD)
    freqs = np.outer(np.arange(N, dtype=np.float32), inv)
    emb = np.concatenate([freqs, freqs], axis=-1)
    sign = np.where(np.arange(HD) < HD // 2, -1.0, 1.0).astype(np.float32)
    c["cosT"] = np.tile(np.cos(emb).T, (NH, 1))
    c["sinT"] = np.tile((np.sin(emb) * sign).T, (NH, 1))
    c["causal_ts"] = np.where(p[None, :] > p[:, None], -CUT, 0.0).astype(np.float32)
    c["causal_st"] = c["causal_ts"].T
    c["descend"] = np.tile(np.arange(NE, 0, -1, dtype=np.float32), (P, 1))
    return c


class Names:

    def __init__(self, nc, ctx):
        self.nc, self.ctx = nc, ctx

    def sb(self, name, shape, dt=F32):
        return self.ctx.enter_context(self.nc.sbuf_tensor(name, shape, dt))

    def ps(self, name, shape, dt=F32):
        return self.ctx.enter_context(self.nc.psum_tensor(name, shape, dt))

    def sem(self, name):
        return self.ctx.enter_context(self.nc.semaphore(name))


def chain(engine, semaphore, start=0):
    count = [start]

    def link(instruction):
        instruction.then_inc(semaphore, 1)
        count[0] += 1
        engine.wait_ge(semaphore, count[0])
    return link


def bc(ap, n):
    return ap.rearrange("p (a o) -> p a o", o=1).to_broadcast([ap.shape[0], ap.shape[1], n])


def graph_setup(nc, d, x_sb, values, er08, cj, ci, el08, feat, wlog, ident):
    with ExitStack() as ctx:
        m = Names(nc, ctx)
        xc = m.sb("gs_xc", [P, NT, C])
        sq = m.sb("gs_sq", [P, NT, C])
        stat = m.sb("gs_stat", [P, 6, NT])
        xt = m.sb("gs_xt", [P, N])
        ht = m.sb("gs_ht", [P, N])
        wt = m.sb("gs_wt", [P, C])
        arl = m.sb("gs_arl", [P, 2])
        hsel = m.sb("gs_hsel", [P, P])
        ar = m.sb("gs_ar", [P, 2, P])
        nsel = m.sb("gs_nsel", [P, GI])
        val = m.sb("gs_val", [P, P])
        coef = m.sb("gs_coef", [P, P])
        gated = m.sb("gs_gated", [P, 2])
        gate = m.sb("gs_gate", [P, 1])
        eps = m.sb("gs_eps", [P, 1])
        ps = m.ps("gs_ps", [P, 8, 512])
        loaded_x, loaded = m.sem("gs_loaded_x"), m.sem("gs_loaded")
        fixed = m.sem("gs_fixed")
        centred, squared, var_ready, std_ready = m.sem("gs_centred"), m.sem("gs_sq_s"), m.sem("gs_var"), m.sem("gs_std")
        xn_ready, xt_ps, xt_ready = m.sem("gs_xn"), m.sem("gs_xt_ps"), m.sem("gs_xt_s")
        h_ps, h_ready, v_ps, v_done = m.sem("gs_h_ps"), m.sem("gs_h_s"), m.sem("gs_v_ps"), m.sem("gs_v_s")
        ar_ready, e_ps, er_done, el_mul, el_done = m.sem("gs_ar_s"), m.sem("gs_e_ps"), m.sem("gs_er_s"), m.sem("gs_elm"), m.sem("gs_el_s")
        spread, link_s = m.sem("gs_spread"), m.sem("gs_link")
        zeroed = m.sem("gs_zeroed")
        block = ctx.enter_context(nc.Block())

        @block.sync
        def _(sp):
            sp.dma_start(x_sb[:, :, :], d["x"].rearrange("(t p) c -> p t c", p=P)).then_inc(loaded_x, 16)
            for dst, name in ((ident, "ident"), (wt, "WT"), (arl, "a_rl"), (hsel, "headsel"), (nsel, "nodesel"),
                              (val, "curvw"), (coef, "coef"), (gated, "gated"), (ci, "curv_i")):
                sp.dma_start(dst[:, :], d[name]).then_inc(loaded, 16)
            sp.dma_start(gate[:, :], d["gate"].to_broadcast([P, 1])).then_inc(loaded, 16)
            for i in range(GI):
                sp.dma_start(cj[CF * i:CF * i + CF, :], d["curvT"]).then_inc(loaded, 16)
            sp.wait_ge(zeroed, 1)
            for b in range(2):
                sp.dma_start(feat[CJ_ROW:PAD_ROW, b, :], d["curvT"]).then_inc(spread, 16)
            sp.wait_ge(er_done, 4)
            for b in range(2):
                sp.dma_start(feat[ER_ROW:CJ_ROW, b, :], er08[0:H, :]).then_inc(spread, 16)
            sp.wait_ge(spread, 64)

        @block.gpsimd
        def _(pool):
            pool.memset(feat[96:P, :, :], 0.0).then_inc(zeroed, 1)

        @block.vector
        def _(dve):
            link = chain(dve, link_s)
            dve.memset(eps[:, :], LN_EPS).then_inc(fixed, 1)
            link(dve.memset(values[:, :, :, :], 0.0))
            link(dve.memset(values[:, :, :, D:D + 1], 1.0))
            dve.wait_ge(loaded_x, 16)
            link(dve.tensor_reduce(stat[:, 0, :], x_sb[:, :, :], AX.X, ALU.add))
            link(dve.tensor_scalar(stat[:, 1, :], stat[:, 0, :], 1.0 / C, None, ALU.mult))
            dve.tensor_tensor(xc[:, :, :], x_sb[:, :, :], bc(stat[:, 1, :], C), ALU.subtract).then_inc(centred, 1)
            dve.wait_ge(loaded, 16 * (10 + GI))
            for n in range(2):
                dve.tensor_scalar(ar[:, n, :], hsel[:, :], arl[:, n:n + 1], None, ALU.mult).then_inc(ar_ready, 1)
            link(dve.tensor_scalar(gated[:, 0:1], gated[:, 0:1], gate[:, 0:1], None, ALU.mult))
            link(dve.tensor_tensor(gate[:, :], gated[:, 0:1], gated[:, 1:2], ALU.add))
            link(dve.scalar_tensor_tensor(wlog[:, :], val[:, :], gate[:, 0:1], coef[:, :], ALU.mult, ALU.mult))
            dve.wait_ge(squared, 1)
            dve.tensor_reduce(stat[:, 2, :], sq[:, :, :], AX.X, ALU.add).then_inc(var_ready, 1)
            dve.wait_ge(std_ready, 1)
            link(dve.reciprocal(stat[:, 4, :], stat[:, 3, :]))
            dve.tensor_tensor(sq[:, :, :], xc[:, :, :], bc(stat[:, 4, :], C), ALU.mult).then_inc(xn_ready, 1)
            for q in range(4):
                dve.wait_ge(xt_ps, q + 1)
                dve.tensor_copy(xt[:, 512 * q:512 * q + 512], ps[:, q, :]).then_inc(xt_ready, 1)
            for q in range(4):
                dve.wait_ge(h_ps, q + 1)
                dve.tensor_copy(ht[:, 512 * q:512 * q + 512], ps[:, 4 + q, :]).then_inc(h_ready, 1)
            for q in range(4):
                dve.wait_ge(v_ps, q + 1)
                dve.tensor_copy(values[:, 4 * q:4 * q + 4, :, 0:D],
                                ps[:, q, :].rearrange("p (t h e) -> p t h e", t=4, h=H)).then_inc(v_done, 1)
            dve.wait_ge(e_ps, 8)
            dve.tensor_tensor(sq[:, :, :].rearrange("p t (g i) -> p (t g) i", i=GI),
                              ps[:, 0:4, :].rearrange("p q (g i) -> p (q g) i", i=GI),
                              nsel[:, :].rearrange("p (o i) -> p o i", o=1).to_broadcast([P, GROUPS, GI]),
                              ALU.mult).then_inc(el_mul, 1)
            dve.wait_ge(el_mul, 1)
            dve.tensor_reduce(el08[:, :], sq[:, :, :].rearrange("p t (g i) -> p (t g) i", i=GI), AX.X,
                              ALU.add).then_inc(el_done, 1)

        @block.scalar
        def _(act):
            act.wait_ge(centred, 1)
            act.activation(sq[:, :, :], xc[:, :, :], ACT.Square).then_inc(squared, 1)
            act.wait_ge(var_ready, 1)
            act.wait_ge(fixed, 1)
            act.activation(stat[:, 3, :], stat[:, 2, :], ACT.Sqrt, bias=eps[:, 0:1], scale=1.0 / C).then_inc(std_ready, 1)
            for q in range(4):
                act.wait_ge(e_ps, q + 1)
                act.mul(er08[:, 512 * q:512 * q + 512], ps[:, 4 + q, :], 1 - SLOPE).then_inc(er_done, 1)

        @block.tensor
        def _(pe):
            pe.wait_ge(loaded, 16 * (10 + GI))
            pe.wait_ge(xn_ready, 1)
            for q in range(4):
                for k in range(4):
                    mm = pe.transpose(ps[:, q, P * k:P * k + P], sq[:, 4 * q + k, :], ident[:, :])
                mm.then_inc(xt_ps, 1)
            for q in range(4):
                pe.wait_ge(xt_ready, q + 1)
                pe.matmul(ps[:, 4 + q, :], wt[:, :], xt[:, 512 * q:512 * q + 512], start=True, stop=True).then_inc(h_ps, 1)
            for q in range(4):
                for k in range(4):
                    t = 4 * q + k
                    mm = pe.matmul(ps[:, q, P * k:P * k + P], xt[:, P * t:P * t + P], wt[:, :], start=True, stop=True)
                mm.then_inc(v_ps, 1)
            pe.wait_ge(ar_ready, 2)
            pe.wait_ge(h_ready, 4)
            for q in range(4):
                pe.matmul(ps[:, 4 + q, :], ar[:, 0, :], ht[:, 512 * q:512 * q + 512], start=True, stop=True).then_inc(e_ps, 1)
            pe.wait_ge(v_done, 4)
            for q in range(4):
                pe.matmul(ps[:, q, :], ar[:, 1, :], ht[:, 512 * q:512 * q + 512], start=True, stop=True).then_inc(e_ps, 1)


def graph_attention(nc, d, x_sb, values, er08, cj, ci, el08, feat, wlog, ident):
    AHEAD = 2
    with ExitStack() as ctx:
        m = Names(nc, ctx)
        logits = m.sb("ga_logits", [P, LSLOTS, N])
        adj = m.sb("ga_adj", [P, N], I32)
        mask = m.sb("ga_mask", [P, N])
        probs_t = m.sb("ga_probs_t", [P, 2, NT, H, AVN])
        av_sb = m.sb("ga_av", [P, 2, P])
        mx = m.sb("ga_mx", [P, 4, LSLOTS])
        rden = m.sb("ga_rden", [P, H])
        gout = m.sb("ga_gout", [P, C])
        lps = m.ps("ga_lps", [P, 4, 512])
        tps = m.ps("ga_tps", [P, 3, 512])
        avp = m.ps("ga_avp", [P, 512])
        adj_in = m.sem("ga_adj_in")
        mask_ready = m.sem("ga_mask_ready")
        mask_in = [m.sem(f"ga_mask_in{b}") for b in range(2)]
        feat_ready = m.sem("ga_feat_ready")
        logit_half = m.sem("ga_logit_half")
        half_seen = m.sem("ga_half_seen")
        relu_ready = m.sem("ga_relu_ready")
        max_half = m.sem("ga_max_half")
        keep_ready = m.sem("ga_keep_ready")
        shift_ready = m.sem("ga_shift_ready")
        probs_ready = m.sem("ga_probs_ready")
        turned = m.sem("ga_turned")
        act_moved = m.sem("ga_act_moved")
        dve_moved = m.sem("ga_dve_moved")
        av_ready = m.sem("ga_av_ready")
        av_moved = m.sem("ga_av_moved")
        out_turned = m.sem("ga_out_turned")
        rden_ready = m.sem("ga_rden_ready")
        scaled = m.sem("ga_scaled")
        out_done = m.sem("ga_out_done")
        block = ctx.enter_context(nc.Block())
        av_view = avp[:, 0:2 * AVN].rearrange("p (q i) -> p q i", q=2)
        out_view = tps[:, 2, 0:2 * P].rearrange("p (h e) -> p h e", e=HW)

        def tiles(engine, body):
            body(0, True, False)
            with engine.Fori(1, NT - 1) as t:
                body(t, True, True)
            body(NT - 1, False, True)

        def moved(g, q):
            dst = probs_t[:, g // AVG % 2, 4 * q:4 * q + 4, :, GI * (g % AVG):GI * (g % AVG) + GI]
            src = tps[:, TBANK[q], :].rearrange("p (k i h) -> p k h i", k=4, h=H)
            return dst, src

        @block.sync
        def _(sp):
            adj_rows = d["adj"].rearrange("(t p) j -> t p j", p=P)

            def mask_rows(t, g):
                if not (isinstance(t, int) and t == 0 and g < 2):
                    sp.wait_ge(logit_half, 2 * (t * GPT + g - 1))
                sp.dma_start(feat[MASK_ROW:P, g % 2, :], mask[GI * g:GI * g + GI, :]).then_inc(mask_in[g % 2], 16)

            def tile_of_rows(t):
                sp.wait_ge(mask_ready, t + 1)
                if not (isinstance(t, int) and t == NT - 1):
                    nxt = t + 1 if isinstance(t, int) else sp.snap(t + 1)
                    sp.dma_start(adj[:, :], adj_rows[bass.ds(nxt, 1)].rearrange("o p j -> (o p) j")).then_inc(adj_in, 16)
                for g in range(GPT):
                    mask_rows(t, g)

            sp.dma_start(adj[:, :], adj_rows[0]).then_inc(adj_in, 16)
            tile_of_rows(0)
            with sp.Fori(1, NT - 1) as t:
                tile_of_rows(t)
            tile_of_rows(NT - 1)

        @block.vector
        def _(dve):
            def make_mask(t):
                dve.wait_ge(adj_in, 16 * (t + 1))
                if not (isinstance(t, int) and t == 0):
                    for b in range(2):
                        dve.wait_ge(mask_in[b], 16 * (GPT // 2) * t)
                dve.tensor_scalar(mask[:, :], adj[:, :], 0.0, 1.0, ALU.is_gt, ALU.subtract).then_inc(mask_ready, 1)

            def features(t, g):
                first = isinstance(t, int) and t == 0
                if not (first and g < 2):
                    dve.wait_ge(logit_half, 2 * (t * GPT + g - 1))
                col = t * GPT + g
                dve.tensor_scalar(feat[0:FR, g % 2, :], cj[:, :], ci[0:FR, bass.ds(col, 1)], 0.0,
                                  ALU.subtract, ALU.max).then_inc(feat_ready, 1)

            def add_half(t, g, half):
                s = g % LSLOTS
                if half == 0:
                    dve.wait_ge(relu_ready, t * GPT + g + 1)
                else:
                    dve.wait_ge(max_half, 2 * (t * GPT + g) + 1)
                dve.wait_ge(logit_half, 2 * (t * GPT + g) + half + 1)
                dve.sem_inc(half_seen, 1)
                part = logits[:, s, HALF * half:HALF * half + HALF]
                dve.tensor_tensor_reduce(part, lps[:, 2 * half:2 * half + 2, :].rearrange("p q n -> p (q n)"), part, 1.0,
                                         -3e38 if half == 0 else mx[:, 0, s:s + 1], ALU.add, ALU.max,
                                         mx[:, half, s:s + 1]).then_inc(max_half, 1)

            def shift(t, g):
                s = g % LSLOTS
                dve.wait_ge(max_half, 2 * (t * GPT + g) + 2)
                dve.tensor_scalar(mx[:, 2, s:s + 1], mx[:, 1, s:s + 1], -0.5 * MASKED, None, ALU.is_gt).then_inc(keep_ready, 1)
                dve.wait_ge(keep_ready, t * GPT + g + 1)
                dve.scalar_tensor_tensor(mx[:, 3, s:s + 1], mx[:, 1, s:s + 1], -1.0, mx[:, 2, s:s + 1],
                                         ALU.mult, ALU.mult).then_inc(shift_ready, 1)

            def move(t, g, q):
                dve.wait_ge(turned, 4 * (t * GPT + g) + q + 1)
                if not (isinstance(t, int) and t == 0 and g < 2 * AVG) and g % AVG == 0:
                    dve.wait_ge(av_ready, 2 * t + g // AVG - 1)
                dve.tensor_copy(*moved(g, q)).then_inc(dve_moved, 1)

            def output(t):
                dve.wait_ge(out_turned, t + 1)
                dve.reciprocal(rden[:, :], out_view[:, :, D]).then_inc(rden_ready, 1)
                dve.wait_ge(rden_ready, t + 1)
                dve.tensor_tensor(gout[:, :].rearrange("p (h e) -> p h e", e=D), out_view[:, :, 0:D], bc(rden[:, :], D),
                                  ALU.mult).then_inc(scaled, 1)
                dve.wait_ge(scaled, t + 1)
                xt = x_sb[:, bass.ds(t, 1), :].rearrange("p o c -> p (o c)")
                dve.tensor_tensor(xt, xt, gout[:, :], ALU.add).then_inc(out_done, 1)

            make_mask(0)
            features(0, 0)
            features(0, 1)
            for g in range(AHEAD):
                add_half(0, g, 0)
                add_half(0, g, 1)
                shift(0, g)
                if g == 0:
                    features(0, 2)

            def body(t, ahead, earlier):
                for g in range(GPT):
                    if g == AVG + 1 and earlier:
                        output(t - 1)
                    if g == GPT - AHEAD - 1 and ahead:
                        make_mask(t + 1)
                    u, v = divmod(g + AHEAD + 1, GPT)
                    if u == 0 or ahead:
                        features(t + u, v)
                    u, v = divmod(g + AHEAD, GPT)
                    if u == 0 or ahead:
                        add_half(t + u, v, 0)
                    move(t, g, 1)
                    if u == 0 or ahead:
                        add_half(t + u, v, 1)
                        shift(t + u, v)
                    move(t, g, 3)
            tiles(dve, body)
            output(NT - 1)

        @block.scalar
        def _(act):
            def relu_part(t, g):
                if not (isinstance(t, int) and t == 0 and g < LSLOTS):
                    act.wait_ge(turned, 4 * (t * GPT + g - LSLOTS + 1))
                act.activation(logits[:, g % LSLOTS, :], er08[:, :], ACT.Relu,
                               bias=el08[:, bass.ds(t * GPT + g, 1)]).then_inc(relu_ready, 1)

            def exponent(t, g):
                s = g % LSLOTS
                act.wait_ge(shift_ready, t * GPT + g + 1)
                act.activation(logits[:, s, :], logits[:, s, :], ACT.Exp, bias=mx[:, 3, s:s + 1],
                               scale=mx[:, 2, s:s + 1]).then_inc(probs_ready, 1)

            def move(t, g, q):
                act.wait_ge(turned, 4 * (t * GPT + g) + q + 1)
                if not (isinstance(t, int) and t == 0) and g % AVG == 0:
                    act.wait_ge(av_ready, 2 * t + g // AVG - 1)
                act.copy(*moved(g, q)).then_inc(act_moved, 1)

            def move_av(t, b):
                act.wait_ge(av_ready, 2 * t + b + 1)
                if b == 0 and not (isinstance(t, int) and t == 0):
                    act.wait_ge(out_turned, t)
                act.copy(av_sb[:, :, AVN * b:AVN * b + AVN], av_view).then_inc(av_moved, 1)

            for g in range(AHEAD + 1):
                relu_part(0, g)
            exponent(0, 0)

            def body(t, ahead, earlier):
                for g in range(GPT):
                    if g == AVG and earlier:
                        move_av(t - 1, 1)
                    u, v = divmod(g + 1, GPT)
                    if u == 0 or ahead:
                        exponent(t + u, v)
                    move(t, g, 0)
                    u, v = divmod(g + AHEAD + 1, GPT)
                    if u == 0 or ahead:
                        relu_part(t + u, v)
                    move(t, g, 2)
                    if g == GPT - 1:
                        move_av(t, 0)
            tiles(act, body)
            move_av(NT - 1, 1)

        @block.tensor
        def _(pe):
            def product(t, g, half):
                if half == 0:
                    pe.wait_ge(feat_ready, t * GPT + g + 1)
                    pe.wait_ge(mask_in[g % 2], 16 * (t * (GPT // 2) + g // 2 + 1))
                if not (isinstance(t, int) and t == 0 and g == 0):
                    pe.wait_ge(max_half, 2 * (t * GPT + g - 1) + half + 1)
                for q in (2 * half, 2 * half + 1):
                    mm = pe.matmul(lps[:, q, :], wlog[:, :], feat[:, g % 2, 512 * q:512 * q + 512], start=True, stop=True)
                mm.then_inc(logit_half, 1)

            def turn(t, g, q):
                if q == 0:
                    pe.wait_ge(probs_ready, t * GPT + g + 1)
                first = isinstance(t, int) and t == 0 and g == 0
                n = t * GPT + g
                if q == 3:
                    pe.wait_ge(dve_moved, 2 * n + 1)
                elif q == 1:
                    if not first:
                        pe.wait_ge(dve_moved, 2 * n)
                elif not first:
                    pe.wait_ge(act_moved, 2 * n - (1 if q == 0 else 0))
                if q == 2 and g == AVG + 1 and not (isinstance(t, int) and t == 0):
                    pe.wait_ge(scaled, t)
                for k in range(4):
                    j = 4 * q + k
                    mm = pe.transpose(tps[:, TBANK[q], P * k:P * k + P], logits[:, g % LSLOTS, P * j:P * j + P], ident[:, :])
                mm.then_inc(turned, 1)

            def value_product(t, b, k):
                n = 2 * t + b
                if k == 0:
                    pe.wait_ge(act_moved, 2 * AVG * (n + 1))
                    pe.wait_ge(dve_moved, 2 * AVG * (n + 1))
                    if not (isinstance(t, int) and t == 0 and b == 0):
                        pe.wait_ge(av_moved, n)
                for j in range(4 * k, 4 * k + 4):
                    for h in range(H):
                        r = HW * (h % 4)
                        mm = pe.matmul(avp[r:r + HW, AVN * (h // 4):AVN * (h // 4) + AVN],
                                       values[:, j, h, :], probs_t[:, b, j, h, :],
                                       start=(j == 0 and h < 4), stop=(j == NT - 1), skip_group_check=True)
                if k == 3:
                    mm.then_inc(av_ready, 1)

            def turn_out(t):
                pe.wait_ge(act_moved, 2 * (GPT * t + GPT + AVG + 1) if not (isinstance(t, int) and t == NT - 1) else 2 * GROUPS)
                pe.wait_ge(av_moved, 2 * t + 2)
                for q in range(2):
                    mm = pe.transpose(tps[:, 2, P * q:P * q + P], av_sb[:, q, :], ident[:, :])
                mm.then_inc(out_turned, 1)

            for g in range(AHEAD):
                product(0, g, 0)
                product(0, g, 1)

            def body(t, ahead, earlier):
                for g in range(GPT):
                    u, v = divmod(g + AHEAD, GPT)
                    more = u == 0 or ahead
                    if more:
                        product(t + u, v, 0)
                    turn(t, g, 0)
                    turn(t, g, 1)
                    if more:
                        product(t + u, v, 1)
                    turn(t, g, 2)
                    turn(t, g, 3)
                    if g == AVG and earlier:
                        turn_out(t - 1)
                    if g >= AVG:
                        value_product(t, 0, g - AVG)
                    elif earlier:
                        value_product(t - 1, 1, g)
            tiles(pe, body)
            for k in range(4):
                value_product(NT - 1, 1, k)
            turn_out(NT - 1)


def block_input(nc, d, x_sb, y, ident, qs, ks, vx):
    with ExitStack() as ctx:
        m = Names(nc, ctx)
        sq = m.sb("bi_sq", [P, NT, C])
        stat = m.sb("bi_stat", [P, 8, NT])
        eps = m.sb("bi_eps", [P, 2])
        ht = m.sb("bi_ht", [P, N])
        ln1 = m.sb("bi_ln1", [P, 1])
        wq = m.sb("bi_wq", [P, 2, NH * HD])
        wk = m.sb("bi_wk", [P, 2, NKV * HD])
        wv = m.sb("bi_wv", [P, NKV * HD])
        cos = m.sb("bi_cos", [P, N])
        sin = m.sb("bi_sin", [P, N])
        rot = m.sb("bi_rot", [P, 2, 2, TC])
        q_hi = m.sb("bi_q_hi", [P, N], F32R)
        q_lo = m.sb("bi_q_lo", [P, N], F32R)
        k_hi = m.sb("bi_k_hi", [NKV * HD, N], F32R)
        k_lo = m.sb("bi_k_lo", [NKV * HD, N], F32R)
        qf = m.sb("bi_qf", [P, N])
        kf = m.sb("bi_kf", [NKV * HD, N])
        ps = m.ps("bi_ps", [P, 8, 512])
        loaded, tables = m.sem("bi_loaded"), m.sem("bi_tables")
        link_s, fixed = m.sem("bi_link"), m.sem("bi_fixed")
        centred, squared, sum_ready, std_ready = m.sem("bi_centred"), m.sem("bi_squared"), m.sem("bi_sum"), m.sem("bi_std")
        y_ready, h_ready = m.sem("bi_y"), m.sem("bi_h")
        ht_ps, ht_ready = m.sem("bi_ht_ps"), m.sem("bi_ht_s")
        qk_ps, qk_used = m.sem("bi_qk_ps"), m.sem("bi_qk_used")
        v_ps = m.sem("bi_v_ps")
        rotated, q_done, split, stacked, v_done = m.sem("bi_rotated"), m.sem("bi_q_done"), m.sem("bi_split"), m.sem("bi_stacked"), m.sem("bi_v_done")
        block = ctx.enter_context(nc.Block())

        @block.sync
        def _(sp):
            sp.dma_start(ln1[:, :], d["ln1"]).then_inc(loaded, 16)
            for k in range(2):
                sp.dma_start(wq[:, k, :], d["wqT"][k]).then_inc(loaded, 16)
                sp.dma_start(wk[:, k, :], d["wkT"][k]).then_inc(loaded, 16)
            sp.dma_start(wv[:, :], d["wvT"]).then_inc(loaded, 16)
            sp.dma_start(cos[:, :], d["cosT"]).then_inc(tables, 16)
            sp.dma_start(sin[:, :], d["sinT"]).then_inc(tables, 16)
            sp.wait_ge(split, 2)
            for g in range(NKV):
                rows = slice(HD * g, HD * g + HD)
                for part, src in enumerate((k_hi, k_hi, k_lo)):
                    sp.dma_start(ks[HD * part:HD * part + HD, g, :].bitcast(F32), src[rows, :].bitcast(F32)).then_inc(stacked, 16)
            sp.wait_ge(split, 4)
            for h in range(NH):
                rows = slice(HD * h, HD * h + HD)
                for part, src in enumerate((q_hi, q_lo, q_hi)):
                    sp.dma_start(qs[HD * part:HD * part + HD, h, :].bitcast(F32), src[rows, :].bitcast(F32)).then_inc(stacked, 16)
            sp.wait_ge(stacked, 16 * 3 * (NKV + NH))

        @block.gpsimd
        def _(pool):
            pool.memset(ks[3 * HD:3 * HD + 1, :, :].bitcast(F32), 1.0).then_inc(fixed, 1)
            pool.wait_ge(fixed, 1)
            pool.memset(vx[:, :, :, :], 0.0).then_inc(fixed, 1)
            pool.wait_ge(fixed, 2)
            pool.memset(vx[:, :, :, HD:HD + 1], 1.0).then_inc(fixed, 1)

        @block.vector
        def _(dve):
            link = chain(dve, link_s)
            link(dve.memset(eps[:, 0:1], LN_EPS))
            link(dve.memset(eps[:, 1:2], RMS_EPS))
            link(dve.tensor_reduce(stat[:, 0, :], x_sb[:, :, :], AX.X, ALU.add))
            link(dve.tensor_scalar(stat[:, 1, :], stat[:, 0, :], 1.0 / C, None, ALU.mult))
            dve.tensor_tensor(y[:, :, :], x_sb[:, :, :], bc(stat[:, 1, :], C), ALU.subtract).then_inc(centred, 1)
            dve.wait_ge(squared, 1)
            dve.tensor_reduce(stat[:, 2, :], sq[:, :, :], AX.X, ALU.add).then_inc(sum_ready, 1)
            dve.wait_ge(std_ready, 1)
            link(dve.reciprocal(stat[:, 4, :], stat[:, 3, :]))
            dve.tensor_tensor(y[:, :, :], y[:, :, :], bc(stat[:, 4, :], C), ALU.mult).then_inc(y_ready, 1)
            dve.wait_ge(squared, 2)
            dve.tensor_reduce(stat[:, 5, :], sq[:, :, :], AX.X, ALU.add).then_inc(sum_ready, 1)
            dve.wait_ge(std_ready, 2)
            link(dve.reciprocal(stat[:, 7, :], stat[:, 6, :]))
            dve.tensor_tensor(sq[:, :, :], y[:, :, :], bc(stat[:, 7, :], C), ALU.mult).then_inc(h_ready, 1)
            dve.wait_ge(loaded, 96)
            for q in range(4):
                dve.wait_ge(ht_ps, q + 1)
                dve.tensor_scalar(ht[:, 512 * q:512 * q + 512], ps[:, q, :], ln1[:, 0:1], None, ALU.mult).then_inc(ht_ready, 1)
            dve.wait_ge(tables, 32)
            for q in range(4):
                cols = slice(512 * q, 512 * q + 512)
                for n, (rows, dst) in enumerate(((NKV * HD, kf), (NH * HD, qf))):
                    bank = 4 * ((q + 1) % 2) + 2 * n
                    u = 2 * q + n
                    dve.wait_ge(qk_ps, u + 1)
                    dve.tensor_tensor(rot[0:rows, n, 0, :], ps[0:rows, bank, :], cos[0:rows, cols], ALU.mult).then_inc(rotated, 1)
                    dve.tensor_tensor(rot[0:rows, n, 1, :], ps[0:rows, bank + 1, :], sin[0:rows, cols], ALU.mult).then_inc(qk_used, 1)
                    dve.wait_ge(rotated, u + 1)
                    dve.wait_ge(qk_used, u + 1)
                    dve.tensor_tensor(dst[:, cols], rot[0:rows, n, 0, :], rot[0:rows, n, 1, :], ALU.add).then_inc(q_done, 1)
                    dve.wait_ge(q_done, u + 1)
            for src, hi, lo in ((kf, k_hi, k_lo), (qf, q_hi, q_lo)):
                last = dve.tensor_copy(hi[:, :], src[:, :]).then_inc(split, 1)
                dve.wait_ge(split, 1 if src is kf else 3)
                dve.tensor_tensor(lo[:, :], src[:, :], hi[:, :].bitcast(F32), ALU.subtract).then_inc(split, 1)

        @block.scalar
        def _(act):
            act.wait_ge(centred, 1)
            act.activation(sq[:, :, :], y[:, :, :], ACT.Square).then_inc(squared, 1)
            act.wait_ge(sum_ready, 1)
            act.activation(stat[:, 3, :], stat[:, 2, :], ACT.Sqrt, bias=eps[:, 0:1], scale=1.0 / C).then_inc(std_ready, 1)
            act.wait_ge(y_ready, 1)
            act.activation(sq[:, :, :], y[:, :, :], ACT.Square).then_inc(squared, 1)
            act.wait_ge(sum_ready, 2)
            act.activation(stat[:, 6, :], stat[:, 5, :], ACT.Sqrt, bias=eps[:, 1:2], scale=1.0 / C).then_inc(std_ready, 1)
            act.wait_ge(fixed, 3)
            for q in range(2):
                act.wait_ge(v_ps, q + 1)
                act.copy(vx[:, 8 * q:8 * q + 8, :, 0:HD],
                         ps[:, 2 * q, :].rearrange("p (t g e) -> p t g e", t=8, g=NKV)).then_inc(v_done, 1)

        @block.tensor
        def _(pe):
            pe.wait_ge(h_ready, 1)
            for q in range(4):
                for k in range(4):
                    mm = pe.transpose(ps[:, q, P * k:P * k + P], sq[:, 4 * q + k, :], ident[:, :])
                mm.then_inc(ht_ps, 1)
            pe.wait_ge(loaded, 96)
            for q in range(4):
                pe.wait_ge(ht_ready, q + 1 if q == 0 else 4)
                for n, w in enumerate((wk, wq)):
                    bank = 4 * ((q + 1) % 2) + 2 * n
                    if q >= 2:
                        pe.wait_ge(qk_used, 2 * (q - 2) + n + 1)
                        pe.wait_ge(rotated, 2 * (q - 2) + n + 1)
                    for r in range(2):
                        mm = pe.matmul(ps[0:w.shape[2], bank + r, :], w[:, r, :], ht[:, 512 * q:512 * q + 512],
                                       start=True, stop=True)
                    mm.then_inc(qk_ps, 1)
            pe.wait_ge(qk_used, 8)
            pe.wait_ge(rotated, 8)
            for q in range(2):
                for k in range(8):
                    t = 8 * q + k
                    mm = pe.matmul(ps[:, 2 * q, 64 * k:64 * k + 64], ht[:, P * t:P * t + P], wv[:, :], start=True, stop=True)
                mm.then_inc(v_ps, 1)


def causal_attention(nc, d, qs, ks, vx, ident, u_sb):
    with ExitStack() as ctx:
        m = Names(nc, ctx)
        probs = m.sb("ca_probs", [P, 3, 2, TC])
        mx = m.sb("ca_mx", [P, NH, NT, 4])
        neg = m.sb("ca_neg", [P, NH, NT])
        negt = m.sb("ca_negt", [2 * NT, NKV, P], F32R)
        identb = m.sb("ca_identb", [P, P], BF16)
        cut = m.sb("ca_cut", [P, 2, P])
        cutb = m.sb("ca_cutb", [P, 2, TC], BF16)
        sps = m.ps("ca_sps", [P, 2, 512])
        tps = m.ps("ca_tps", [P, 2, 2, TC])
        ops = m.ps("ca_ops", [P, 2, TC])
        loaded, fixed, link_s = m.sem("ca_loaded"), m.sem("ca_fixed"), m.sem("ca_link")
        s_ready, s_maxed = m.sem("ca_s_ready"), m.sem("ca_s_maxed")
        neg_ready, neg_turned, neg_copied = m.sem("ca_neg_ready"), m.sem("ca_neg_turned"), m.sem("ca_neg_copied")
        neg_row = m.sem("ca_neg_row")
        t_ready, t_exp = m.sem("ca_t_ready"), m.sem("ca_t_exp")
        pv_done, o_moved = m.sem("ca_pv_done"), m.sem("ca_o_moved")
        block = ctx.enter_context(nc.Block())
        K = 3 * HD
        s_units = [[(h, tt, sc) for h in (2 * g, 2 * g + 1) for tt in range(NT) for sc in range(tt // 4 + 1)]
                   for g in range(NKV)]
        t_units = [[(tc, sj) for tc in range(N // TC) for sj in range(4 * tc + 4)] for g in range(NKV)]
        n_s, n_t = len(s_units[0]), len(t_units[0])

        @block.sync
        def _(sp):
            sp.dma_start(cut[:, 0, :], d["causal_ts"]).then_inc(loaded, 16)
            sp.dma_start(cut[:, 1, :], d["causal_st"]).then_inc(loaded, 16)
            for g in range(NKV):
                sp.wait_ge(neg_copied, g + 1)
                for h in range(2):
                    for t in range(NT):
                        sp.dma_start(qs[K:K + 1, 2 * g + h, P * t:P * t + P].bitcast(F32),
                                     negt[NT * h + t:NT * h + t + 1, g, :].bitcast(F32)).then_inc(neg_row, 16)

        @block.vector
        def _(dve):
            link = chain(dve, link_s)
            dve.wait_ge(loaded, 32)
            dve.tensor_copy(identb[:, :], ident[:, :]).then_inc(fixed, 1)
            link(dve.memset(cutb[:, :, :], 0.0))
            dve.tensor_copy(cutb[:, 0, TC - P:TC], cut[:, 0, :]).then_inc(fixed, 1)
            dve.tensor_copy(cutb[:, 1, 0:P], cut[:, 1, :]).then_inc(fixed, 1)
            link(dve.memset(mx[:, :, :, :], -3e38))

            def maximum(g, i):
                h, tt, sc = s_units[g][i]
                n = g * n_s + i
                w = min(512, P * (tt + 1) - 512 * sc)
                dve.wait_ge(s_ready, n + 1)
                dve.tensor_reduce(mx[:, h, tt, sc:sc + 1], sps[:, n % 2, 0:w], AX.X, ALU.max).then_inc(s_maxed, 1)

            def negate(g):
                dve.wait_ge(s_maxed, (g + 1) * n_s)
                heads = slice(2 * g, 2 * g + 2)
                dve.tensor_reduce(neg[:, heads, :], mx[:, heads, :, :], AX.X, ALU.max, negate=True).then_inc(neg_ready, 1)
                dve.wait_ge(neg_turned, g + 1)
                dve.tensor_copy(negt[:, g, :], sps[0:2 * NT, 0, 0:P]).then_inc(neg_copied, 1)

            def move_out(g, tc):
                dve.wait_ge(pv_done, g * n_t + 2 * (tc + 1) * (tc + 2))
                dve.tensor_copy(u_sb[:, g, TC * tc:TC * tc + TC], ops[:, tc % 2, :]).then_inc(o_moved, 1)

            for i in range(n_s):
                maximum(0, i)
            negate(0)
            for i, (tc, sj) in enumerate(t_units[0]):
                maximum(1, 2 * i)
                maximum(1, 2 * i + 1)
                if sj == 1 and tc:
                    move_out(0, tc - 1)
            negate(1)
            move_out(0, 3)
            for tc in range(4):
                move_out(1, tc)

        @block.scalar
        def _(act):
            for g in range(NKV):
                for i, (tc, sj) in enumerate(t_units[g]):
                    n = g * n_t + i
                    off = max(0, P * sj - TC * tc)
                    act.wait_ge(t_ready, n + 1)
                    if n >= 3:
                        act.wait_ge(pv_done, n - 2)
                    act.activation(probs[:, n % 3, :, off:TC], tps[:, n % 2, :, off:TC], ACT.Exp,
                                   scale=float(np.float32(1) / np.sqrt(np.float32(HD)))).then_inc(t_exp, 1)

        @block.tensor
        def _(pe):
            def by_target(g, i):
                h, tt, sc = s_units[g][i]
                n = g * n_s + i
                w = min(512, P * (tt + 1) - 512 * sc)
                diag = sc == tt // 4
                if n >= 2:
                    pe.wait_ge(s_maxed, n - 1)
                if g and i == 0:
                    pe.wait_ge(neg_copied, g)
                if diag:
                    pe.matmul(sps[:, n % 2, 0:w], identb[:, :], cutb[:, 0, 4 * P - w:4 * P], start=True, stop=False)
                mm = pe.matmul(sps[:, n % 2, 0:w], qs[0:K, h, P * tt:P * tt + P], ks[0:K, g, 512 * sc:512 * sc + w],
                               start=not diag, stop=True)
                mm.then_inc(s_ready, 1)

            def turn_negative(g):
                pe.wait_ge(neg_ready, g + 1)
                pe.transpose(sps[0:2 * NT, 0, 0:P], neg[:, 2 * g:2 * g + 2, :].rearrange("p h t -> p (h t)"),
                             ident[:, :]).then_inc(neg_turned, 1)

            def by_source(g, i):
                tc, sj = t_units[g][i]
                n = g * n_t + i
                off = max(0, P * sj - TC * tc)
                diag = sj >= 4 * tc
                if n >= 2:
                    pe.wait_ge(t_exp, n - 1)
                for h in range(2):
                    if diag:
                        pe.matmul(tps[:, n % 2, h, off:TC], identb[:, :], cutb[:, 1, 0:TC - off], start=True, stop=False)
                    mm = pe.matmul(tps[:, n % 2, h, off:TC], ks[0:K + 1, g, P * sj:P * sj + P],
                                   qs[0:K + 1, 2 * g + h, TC * tc + off:TC * tc + TC], start=not diag, stop=True)
                mm.then_inc(t_ready, 1)

            def values(g, i):
                tc, sj = t_units[g][i]
                n = g * n_t + i
                off = max(0, P * sj - TC * tc)
                last = sj == 4 * tc + 3
                pe.wait_ge(t_exp, n + 1)
                if sj == 0 and 4 * g + tc >= 2:
                    pe.wait_ge(o_moved, 4 * g + tc - 1)
                for h in range(2):
                    mm = pe.matmul(ops[VW * h:VW * h + VW, tc % 2, off:TC], vx[:, sj, g, :], probs[:, n % 3, h, off:TC],
                                   start=(sj == 0), stop=last, skip_group_check=True)
                mm.then_inc(pv_done, 1)

            pe.wait_ge(fixed, 3)
            for i in range(n_s):
                by_target(0, i)
            turn_negative(0)
            for g in range(NKV):
                pe.wait_ge(neg_row, 16 * 2 * NT * (g + 1))
                for i in range(n_t):
                    by_source(g, i)
                    if g == 0:
                        by_target(1, 2 * i)
                        by_target(1, 2 * i + 1)
                    if i:
                        values(g, i - 1)
                values(g, n_t - 1)
                if g == 0:
                    turn_negative(1)


def project(nc, d, y, u_sb):
    with ExitStack() as ctx:
        m = Names(nc, ctx)
        wo = m.sb("pj_wo", [P, 2, 256])
        parts = m.sb("pj_parts", [P, 2, NH, C])
        total = m.sb("pj_total", [P, 2, C])
        rden = m.sb("pj_rden", [P, 2, NH])
        ps = m.ps("pj_ps", [P, 2, NH, 256])
        loaded, made, inverted, scaled, summed, added = (m.sem(f"pj_{n}") for n in
                                                         ("loaded", "made", "inverted", "scaled", "summed", "added"))
        block = ctx.enter_context(nc.Block())

        @block.sync
        def _(sp):
            sp.dma_start(wo[:, :, :], d["woX"]).then_inc(loaded, 16)

        @block.vector
        def _(dve):
            for t in range(NT):
                b = t % 2
                dve.wait_ge(made, t + 1)
                dve.reciprocal(rden[:, b, :], ps[:, b, :, C]).then_inc(inverted, 1)
                dve.wait_ge(inverted, t + 1)
                if t >= 2:
                    dve.wait_ge(summed, t - 1)
                dve.tensor_tensor(parts[:, b, :, :], ps[:, b, :, 0:C], bc(rden[:, b, :], C), ALU.mult).then_inc(scaled, 1)
                dve.wait_ge(scaled, t + 1)
                if t >= 2:
                    dve.wait_ge(added, t - 1)
                dve.tensor_reduce(total[:, b, :], parts[:, b, :, :].rearrange("p h c -> p c h"), AX.X,
                                  ALU.add).then_inc(summed, 1)
                dve.wait_ge(summed, t + 1)
                dve.tensor_tensor(y[:, t, :], y[:, t, :], total[:, b, :], ALU.add).then_inc(added, 1)

        @block.tensor
        def _(pe):
            pe.wait_ge(loaded, 16)
            for t in range(NT):
                if t >= 2:
                    pe.wait_ge(scaled, t - 1)
                for h in range(NH):
                    r = VW * (h % 2)
                    mm = pe.matmul(ps[:, t % 2, 2 * (h % 2) + h // 2, 0:C + 2], u_sb[r:r + VW, h // 2, P * t:P * t + P],
                                   wo[r:r + VW, h // 2, 0:C + 2], start=True, stop=True)
                mm.then_inc(made, 1)


def experts(nc, d, out, x_sb, y, ident):
    UN = len(HK)
    with ExitStack() as ctx:
        m = Names(nc, ctx)
        sq = m.sb("ex_sq", [P, NT, C])
        stat = m.sb("ex_stat", [P, 3, NT])
        eps = m.sb("ex_eps", [P, 1])
        ft = m.sb("ex_ft", [P, N])
        ln2 = m.sb("ex_ln2", [P, 1])
        rw = m.sb("ex_rw", [P, NE])
        desc = m.sb("ex_desc", [P, NE])
        pr = m.sb("ex_pr", [P, NT, NE])
        r = m.sb("ex_r", [P, 6, NT, NE])
        rs = m.sb("ex_rs", [P, 8, NT])
        wgt = m.sb("ex_wgt", [P, NT, NE])
        w1 = m.sb("ex_w1", [P, 2, HID])
        w3 = m.sb("ex_w3", [P, 2, HID])
        w2 = m.sb("ex_w2", [P, 2, UN, C])
        gate = m.sb("ex_gate", [P, 2, TC])
        hid = m.sb("ex_hid", [P, 2, UN, TC])
        aps = m.ps("ex_aps", [P, 2, TC])
        bps = m.ps("ex_bps", [P, 2, TC])
        ops = m.ps("ex_ops", [P, 2, 4, C])
        xps = m.ps("ex_xps", [P, 2, 512])
        loaded, link_s = m.sem("ex_loaded"), m.sem("ex_link")
        squared, sum_ready, std_ready, f_ready = m.sem("ex_squared"), m.sem("ex_sum"), m.sem("ex_std"), m.sem("ex_f")
        ft_ps, ft_ready = m.sem("ex_ft_ps"), m.sem("ex_ft_s")
        r_ps, shifted, r_exp = m.sem("ex_r_ps"), m.sem("ex_shifted"), m.sem("ex_r_exp")
        w_in = [m.sem(f"ex_w_in{b}") for b in range(2)]
        ab_ready = m.sem("ex_ab_ready")
        gated = m.sem("ex_gated")
        hid_ready = m.sem("ex_hid_ready")
        o_ready = m.sem("ex_o_ready")
        combined = m.sem("ex_combined")
        x_ready, stored = m.sem("ex_x_ready"), m.sem("ex_stored")
        block = ctx.enter_context(nc.Block())
        NC_ = N // TC

        def pairs(engine, body):
            for b in range(2):
                body(b, b, False)
            with engine.Fori(1, NE // 2) as i:
                for b in range(2):
                    body(2 * i + b, b, True)

        @block.sync
        def _(sp):
            sp.dma_start(ln2[:, :], d["ln2"]).then_inc(loaded, 16)
            sp.dma_start(rw[:, :], d["routerT"]).then_inc(loaded, 16)
            sp.dma_start(desc[:, :], d["descend"]).then_inc(loaded, 16)

            def weights(e, b, earlier):
                if earlier:
                    sp.wait_ge(o_ready, NC_ * (e - 1))
                ex = e if isinstance(e, int) else sp.snap(e)
                one = bass.ds(ex, 1)
                for dst, name in ((w1, "w1T"), (w3, "w3T")):
                    sp.dma_start(dst[:, b, :], d[name][one].rearrange("o c k -> (o c) k")).then_inc(w_in[b], 16)
                for k, (k0, n) in enumerate(HK):
                    sp.dma_start(w2[0:n, b, k, :], d["w2T"][one, k0:k0 + n].rearrange("o k c -> (o k) c")).then_inc(w_in[b], 16)
            pairs(sp, weights)
            out_t = out.rearrange("(t p) c -> p t c", p=P)
            for q in range(NC_):
                sp.wait_ge(combined, 4 * NC_ * (NE - 1) + 4 * (q + 1))
                sp.dma_start(out_t[:, 4 * q:4 * q + 4, :], x_sb[:, 4 * q:4 * q + 4, :]).then_inc(stored, 16)
            sp.wait_ge(stored, 16 * NC_)

        @block.vector
        def _(dve):
            link = chain(dve, link_s)
            link(dve.memset(eps[:, :], RMS_EPS))
            dve.wait_ge(squared, 1)
            dve.tensor_reduce(stat[:, 0, :], sq[:, :, :], AX.X, ALU.add).then_inc(sum_ready, 1)
            dve.wait_ge(std_ready, 1)
            link(dve.reciprocal(stat[:, 2, :], stat[:, 1, :]))
            dve.tensor_tensor(sq[:, :, :], y[:, :, :], bc(stat[:, 2, :], C), ALU.mult).then_inc(f_ready, 1)
            dve.wait_ge(loaded, 48)
            for q in range(4):
                dve.wait_ge(ft_ps, q + 1)
                dve.tensor_scalar(ft[:, 512 * q:512 * q + 512], xps[:, q % 2, :], ln2[:, 0:1], None, ALU.mult).then_inc(ft_ready, 1)
            dve.tensor_tensor(x_sb[:, :, :], x_sb[:, :, :], y[:, :, :], ALU.add).then_inc(x_ready, 1)
            dve.wait_ge(r_ps, 1)
            link(dve.tensor_copy(r[:, 0, :, :], xps[:, 0, 0:NT * NE].rearrange("p (t e) -> p t e", e=NE)))
            link(dve.tensor_reduce(rs[:, 0, :], r[:, 0, :, :], AX.X, ALU.max))
            dve.tensor_tensor(r[:, 1, :, :], r[:, 0, :, :], bc(rs[:, 0, :], NE), ALU.subtract).then_inc(shifted, 1)
            dve.wait_ge(r_exp, 1)
            link(dve.tensor_reduce(rs[:, 1, :], r[:, 2, :, :], AX.X, ALU.add))
            link(dve.reciprocal(rs[:, 2, :], rs[:, 1, :]))
            link(dve.tensor_tensor(pr[:, :, :], r[:, 2, :, :], bc(rs[:, 2, :], NE), ALU.mult))
            marks = desc[:, :].rearrange("p (o e) -> p o e", o=1).to_broadcast([P, NT, NE])

            def first_largest(src, largest, mark, hot):
                link(dve.tensor_reduce(rs[:, largest, :], src, AX.X, ALU.max))
                link(dve.tensor_tensor(r[:, 0, :, :], src, bc(rs[:, largest, :], NE), ALU.is_ge))
                link(dve.tensor_tensor(r[:, 1, :, :], r[:, 0, :, :], marks, ALU.mult))
                link(dve.tensor_reduce(rs[:, mark, :], r[:, 1, :, :], AX.X, ALU.max))
                link(dve.tensor_tensor(r[:, hot, :, :], r[:, 1, :, :], bc(rs[:, mark, :], NE), ALU.is_equal))

            first_largest(pr[:, :, :], 3, 4, 3)
            link(dve.scalar_tensor_tensor(r[:, 5, :, :], r[:, 3, :, :], -2.0, pr[:, :, :], ALU.mult, ALU.add))
            first_largest(r[:, 5, :, :], 5, 4, 4)
            link(dve.scalar_tensor_tensor(rs[:, 6, :], rs[:, 3, :], 1e-9, rs[:, 5, :], ALU.add, ALU.add))
            link(dve.reciprocal(rs[:, 7, :], rs[:, 6, :]))
            link(dve.tensor_tensor(r[:, 0, :, :], r[:, 3, :, :], r[:, 4, :, :], ALU.add))
            link(dve.tensor_tensor(r[:, 1, :, :], r[:, 0, :, :], pr[:, :, :], ALU.mult))
            link(dve.tensor_tensor(wgt[:, :, :], r[:, 1, :, :], bc(rs[:, 7, :], NE), ALU.mult))
            dve.wait_ge(x_ready, 1)

            def combine(e, tc, no_wait=False):
                dve.wait_ge(o_ready, NC_ * e + tc + 1)
                if not isinstance(e, int) or e:
                    dve.wait_ge(combined, 4 * (NC_ * (e - 1) + tc + 1))
                for k in range(4):
                    t = 4 * tc + k
                    dve.scalar_tensor_tensor(x_sb[:, t, :], ops[:, tc % 2, k, :], wgt[:, t, bass.ds(e, 1)], x_sb[:, t, :],
                                             ALU.mult, ALU.add).then_inc(combined, 1)

            def body(e, b, earlier):
                for tc in range(NC_):
                    for k, (_, n) in enumerate(HK):
                        u = (NC_ * e + tc) * UN + k
                        dve.wait_ge(ab_ready, u + 1)
                        dve.wait_ge(gated, u + 1)
                        if k == 0 and not (isinstance(e, int) and e == 0 and tc < 2):
                            dve.wait_ge(o_ready, NC_ * e + tc - 1)
                        dve.tensor_tensor(hid[0:n, tc % 2, k, :], gate[0:n, (tc * UN + k) % 2, :],
                                          bps[0:n, (tc * UN + k) % 2, :], ALU.mult).then_inc(hid_ready, 1)
                    if tc:
                        combine(e, tc - 1)
                    elif earlier or b:
                        combine(e - 1, NC_ - 1)
            pairs(dve, body)
            combine(NE - 1, NC_ - 1)

        @block.scalar
        def _(act):
            act.activation(sq[:, :, :], y[:, :, :], ACT.Square).then_inc(squared, 1)
            act.wait_ge(sum_ready, 1)
            act.activation(stat[:, 1, :], stat[:, 0, :], ACT.Sqrt, bias=eps[:, 0:1], scale=1.0 / C).then_inc(std_ready, 1)
            act.wait_ge(shifted, 1)
            act.activation(r[:, 2, :, :], r[:, 1, :, :], ACT.Exp).then_inc(r_exp, 1)

            def body(e, b, earlier):
                for tc in range(NC_):
                    for k, (_, n) in enumerate(HK):
                        u = (NC_ * e + tc) * UN + k
                        act.wait_ge(ab_ready, u + 1)
                        if not (isinstance(e, int) and e == 0 and tc * UN + k < 2):
                            act.wait_ge(hid_ready, u - 1)
                        act.activation(gate[0:n, (tc * UN + k) % 2, :], aps[0:n, (tc * UN + k) % 2, :],
                                       ACT.Silu).then_inc(gated, 1)
            pairs(act, body)

        @block.tensor
        def _(pe):
            pe.wait_ge(f_ready, 1)
            for q in range(4):
                if q >= 2:
                    pe.wait_ge(ft_ready, q - 1)
                for k in range(4):
                    mm = pe.transpose(xps[:, q % 2, P * k:P * k + P], sq[:, 4 * q + k, :], ident[:, :])
                mm.then_inc(ft_ps, 1)
            pe.wait_ge(ft_ready, 4)
            pe.wait_ge(loaded, 48)
            for t in range(NT):
                mm = pe.matmul(xps[:, 0, NE * t:NE * t + NE], ft[:, P * t:P * t + P], rw[:, :], start=True, stop=True)
            mm.then_inc(r_ps, 1)

            def output(e, b, tc):
                n = NC_ * e + tc
                pe.wait_ge(hid_ready, UN * (n + 1))
                if not (isinstance(e, int) and e == 0 and tc < 2):
                    pe.wait_ge(combined, 4 * (n - 1))
                for t in range(4):
                    for k, (_, rows) in enumerate(HK):
                        mm = pe.matmul(ops[:, tc % 2, t, :], hid[0:rows, tc % 2, k, P * t:P * t + P], w2[0:rows, b, k, :],
                                       start=(k == 0), stop=(k == UN - 1))
                mm.then_inc(o_ready, 1)

            def body(e, b, earlier):
                if isinstance(e, int):
                    pe.wait_ge(w_in[b], 16 * (2 + UN))
                else:
                    pe.wait_ge(w_in[b], 8 * (2 + UN) * (e - b + 2))
                for tc in range(NC_):
                    for k, (k0, n) in enumerate(HK):
                        s = (tc * UN + k) % 2
                        u = (NC_ * e + tc) * UN + k
                        if not (isinstance(e, int) and e == 0 and tc * UN + k < 2):
                            pe.wait_ge(hid_ready, u - 1)
                        for w, dst in ((w1, aps), (w3, bps)):
                            mm = pe.matmul(dst[0:n, s, :], w[:, b, k0:k0 + n], ft[:, TC * tc:TC * tc + TC],
                                           start=True, stop=True)
                        mm.then_inc(ab_ready, 1)
                    if tc:
                        output(e, b, tc - 1)
                    elif earlier or b:
                        output(e - 1, 1 - b, NC_ - 1)
            pairs(pe, body)
            output(NE - 1, 1, NC_ - 1)


def program(nc, d, out, stop_after=None):
    with ExitStack() as ctx:
        m = Names(nc, ctx)
        x_sb = m.sb("x_sb", [P, NT, C])
        ident = m.sb("ident_sb", [P, P])
        with ExitStack() as gctx:
            g = Names(nc, gctx)
            values = g.sb("g_values", [P, NT, H, HW])
            er08 = g.sb("g_er08", [P, N])
            cj = g.sb("g_cj", [FR, N])
            ci = g.sb("g_ci", [FR, GROUPS])
            el08 = g.sb("g_el08", [P, GROUPS])
            feat = g.sb("g_feat", [P, 2, N])
            wlog = g.sb("g_wlog", [P, P])
            args = (nc, d, x_sb, values, er08, cj, ci, el08, feat, wlog, ident)
            graph_setup(*args)
            graph_attention(*args)
        if stop_after == "graph":
            done = m.sem("dbg")
            block = ctx.enter_context(nc.Block())

            @block.sync
            def _(sp):
                sp.dma_start(out.rearrange("(t p) c -> p t c", p=P), x_sb[:, :, :]).then_inc(done, 16)
                sp.wait_ge(done, 16)
            return
        y = m.sb("y_sb", [P, NT, C])
        with ExitStack() as actx:
            a = Names(nc, actx)
            u_sb = a.sb("u_sb", [P, NKV, N])
            with ExitStack() as qctx:
                q = Names(nc, qctx)
                qs = q.sb("q_stack", [3 * HD + 1, NH, N], F32R)
                ks = q.sb("k_stack", [3 * HD + 1, NKV, N], F32R)
                vx = q.sb("v_values", [P, NT, NKV, VW])
                block_input(nc, d, x_sb, y, ident, qs, ks, vx)
                causal_attention(nc, d, qs, ks, vx, ident, u_sb)
            project(nc, d, y, u_sb)
        experts(nc, d, out, x_sb, y, ident)


def lay_out(x, adj, L0_gnn_positions, L0_gnn_curv_feats, L0_gnn_W, L0_gnn_a_l, L0_gnn_a_r, L0_gnn_Wc, L0_gnn_gate,
            L0_ffn_ln1_w, L0_ffn_ln2_w, L0_ffn_wq, L0_ffn_wk, L0_ffn_wv, L0_ffn_wo, L0_ffn_router_w, L0_ffn_w1,
            L0_ffn_w2, L0_ffn_w3):
    a = np.asarray
    curv = a(L0_gnn_curv_feats)
    wc = a(L0_gnn_Wc)
    curvw = np.ones((P, P), np.float32)
    curvw[:FR] = np.tile(wc.T, (GI, GI))
    curvw[CJ_ROW:PAD_ROW] = np.tile(wc.T, (1, GI))
    arrays = {
        "x": a(x), "adj": a(adj),
        "WT": a(L0_gnn_W).T,
        "a_rl": np.stack([a(L0_gnn_a_r).reshape(-1), a(L0_gnn_a_l).reshape(-1)], 1),
        "curvw": curvw, "curvT": curv.T, "curv_i": curv.reshape(GROUPS, FR).T,
        "gate": a(L0_gnn_gate).reshape(1, 1),
        "ln1": a(L0_ffn_ln1_w).reshape(C, 1), "ln2": a(L0_ffn_ln2_w).reshape(C, 1),
        "wvT": a(L0_ffn_wv).T, "routerT": a(L0_ffn_router_w).T,
        "w1T": a(L0_ffn_w1).transpose(0, 2, 1), "w3T": a(L0_ffn_w3).transpose(0, 2, 1),
        "w2T": a(L0_ffn_w2).transpose(0, 2, 1),
    }
    for name, w in (("wqT", a(L0_ffn_wq)), ("wkT", a(L0_ffn_wk))):
        partner = w.reshape(-1, 2, HD // 2, C)[:, ::-1].reshape(w.shape)
        arrays[name] = np.stack([w.T, partner.T])
    wo = np.zeros((P, 2, 256), np.float32)
    for h in range(NH):
        r = VW * (h % 2)
        wo[r:r + HD, h // 2, 0:C] = a(L0_ffn_wo)[:, HD * h:HD * h + HD].T
        wo[r + HD, h // 2, C] = 1.0
    arrays["woX"] = wo
    arrays.update(constants())
    return {k: np.ascontiguousarray(v) for k, v in arrays.items()}


def kernel(**inputs):
    import concourse.bacc as bacc
    from concourse.bass_utils import run_bass_kernel_spmd

    nc = bacc.Bacc("TRN2", target_bir_lowering=False, num_devices=1)
    arrays = lay_out(**inputs)
    aps = {name: nc.dram_tensor(f"in_{name}", a.shape, mybir.dt.from_np(a.dtype), kind="ExternalInput").ap()
           for name, a in arrays.items()}
    out = nc.dram_tensor("out", (N, C), F32, kind="ExternalOutput").ap()
    program(nc, aps, out)
    r = run_bass_kernel_spmd(nc, [{f"in_{name}": a for name, a in arrays.items()}], core_ids=[0])
    return r.results[0]["out"]
```

```python
from contextlib import ExitStack

import numpy as np

import concourse.bass as bass
from concourse import mybir

F32 = mybir.dt.float32
F32R = mybir.dt.float32r
BF16 = mybir.dt.bfloat16
I32 = mybir.dt.int32
ALU = mybir.AluOpType
ACT = mybir.ActivationFunctionType
AX = mybir.AxisListType

P = 128
N = 2048
C = 128
NT = N // P
H, D, CF = 8, 16, 6
GI = P // H
GROUPS = N // GI
GPT = P // GI
FR = GI * CF
ER_ROW, CJ_ROW, PAD_ROW, MASK_ROW = FR, FR + H, FR + H + CF, P - GI
HALF = N // 2
LSLOTS = 4
HW = 32
AVG = 4
AVN = AVG * GI
TBANK = [0, 1, 2, 1]
MASKED = 1e9
SLOPE = 0.2
LN_EPS = 1e-5
RMS_EPS = 1e-6

NH, NKV, HD = 4, 2, 32
NREP = NH // NKV
ROPE_BASE = 10000.0
VW = 64
TC = 512
CUT = 1e30
LEAD, RATE = 28, 5
NE, HID = 8, 341
HK = [(0, 128), (128, 128), (256, HID - 256)]


def constants():
    p = np.arange(P)
    c = {}
    c["ident"] = np.eye(P, dtype=np.float32)
    coef = np.zeros((P, P), np.float32)
    i_of, h_of = p // H, p % H
    for r in range(FR):
        coef[r] = 2.0 * (i_of == r // CF)
    for r in range(H):
        coef[ER_ROW + r] = SLOPE / (1 - SLOPE) * (h_of == r)
    coef[CJ_ROW:PAD_ROW] = -1.0
    for r in range(GI):
        coef[MASK_ROW + r] = MASKED * (i_of == r)
    c["coef"] = coef
    gated = np.zeros((P, 2), np.float32)
    gated[:FR, 0] = 1
    gated[CJ_ROW:PAD_ROW, 0] = 1
    gated[:, 1] = 1 - gated[:, 0]
    c["gated"] = gated
    c["headsel"] = (p[:, None] // D == h_of[None, :]).astype(np.float32)
    c["nodesel"] = ((1 - SLOPE) * (i_of[:, None] == np.arange(GI)[None, :])).astype(np.float32)
    inv = 1.0 / ROPE_BASE ** (np.arange(0, HD, 2, dtype=np.float32) / HD)
    freqs = np.outer(np.arange(N, dtype=np.float32), inv)
    emb = np.concatenate([freqs, freqs], axis=-1)
    sign = np.where(np.arange(HD) < HD // 2, -1.0, 1.0).astype(np.float32)
    c["cosT"] = np.tile(np.cos(emb).T, (NH, 1))
    c["sinT"] = np.tile((np.sin(emb) * sign).T, (NH, 1))
    rows = NKV * HD
    for name in ("cos", "sin"):
        t = c[name + "T"][:rows].reshape(rows, 2, 2, TC)
        c[name + "K"] = t.transpose(2, 0, 1, 3).reshape(P, 2, TC)
    c["causal_ts"] = np.where(p[None, :] > p[:, None], -CUT, 0.0).astype(np.float32)
    c["causal_st"] = c["causal_ts"].T
    c["descend"] = np.tile(np.arange(NE, 0, -1, dtype=np.float32), (P, 1))
    return c


class Names:

    def __init__(self, nc, ctx):
        self.nc, self.ctx = nc, ctx

    def sb(self, name, shape, dt=F32):
        return self.ctx.enter_context(self.nc.sbuf_tensor(name, shape, dt))

    def ps(self, name, shape, dt=F32):
        return self.ctx.enter_context(self.nc.psum_tensor(name, shape, dt))

    def sem(self, name):
        return self.ctx.enter_context(self.nc.semaphore(name))


def chain(engine, semaphore, start=0):
    count = [start]

    def link(instruction):
        instruction.then_inc(semaphore, 1)
        count[0] += 1
        engine.wait_ge(semaphore, count[0])
    return link


def bc(ap, n):
    return ap.rearrange("p (a o) -> p a o", o=1).to_broadcast([ap.shape[0], ap.shape[1], n])


def moments(dve, link, st, out):
    even, odd = st[:, :, 1], st[:, :, 4]
    link(dve.tensor_tensor(out[:, 0, :], even, odd, ALU.add))
    link(dve.tensor_tensor(out[:, 1, :], even, odd, ALU.subtract))
    link(dve.tensor_tensor(out[:, 2, :], out[:, 1, :], out[:, 1, :], ALU.mult))
    link(dve.tensor_tensor(out[:, 3, :], st[:, :, 2], st[:, :, 5], ALU.add))
    link(dve.scalar_tensor_tensor(out[:, 1, :], out[:, 2, :], C / 4.0, out[:, 3, :], ALU.mult, ALU.add))
    link(dve.tensor_scalar(out[:, 0, :], out[:, 0, :], 0.5, None, ALU.mult))


def graph_setup(nc, d, x_sb, values, er08, cj, ci, el08, feat, wlog, ident, mask):
    with ExitStack() as ctx:
        m = Names(nc, ctx)
        st = m.sb("gs_st", [P, NT, 6])
        sq = m.sb("gs_sq", [P, NT, C])
        stat = m.sb("gs_stat", [P, 6, NT])
        xt = m.sb("gs_xt", [P, N])
        el_tmp = m.sb("gs_el_tmp", [P, N])
        ht = m.sb("gs_ht", [P, N])
        wt = m.sb("gs_wt", [P, C])
        arl = m.sb("gs_arl", [P, 2])
        hsel = m.sb("gs_hsel", [P, P])
        ar = m.sb("gs_ar", [P, 2, P])
        nsel = m.sb("gs_nsel", [P, GI])
        val = m.sb("gs_val", [P, P])
        coef = m.sb("gs_coef", [P, P])
        gated = m.sb("gs_gated", [P, 2])
        gate = m.sb("gs_gate", [P, 1])
        eps = m.sb("gs_eps", [P, 1])
        ps = m.ps("gs_ps", [P, 8, 512])
        loaded_x, loaded = [m.sem(f"gs_loaded_x{q}") for q in range(4)], m.sem("gs_loaded")
        adj_in, stats_done, mask_done = m.sem("gs_adj_in"), m.sem("gs_stats_done"), m.sem("gs_mask_done")
        fixed = m.sem("gs_fixed")
        var_ready, std_ready = m.sem("gs_var"), m.sem("gs_std")
        xn_ready, xt_ps, xt_ready = m.sem("gs_xn"), m.sem("gs_xt_ps"), m.sem("gs_xt_s")
        h_ps, h_ready, v_ps, v_done = m.sem("gs_h_ps"), m.sem("gs_h_s"), m.sem("gs_v_ps"), m.sem("gs_v_s")
        ar_ready, e_ps, er_done, el_mul, el_done = m.sem("gs_ar_s"), m.sem("gs_e_ps"), m.sem("gs_er_s"), m.sem("gs_elm"), m.sem("gs_el_s")
        spread, link_s = m.sem("gs_spread"), m.sem("gs_link")
        zeroed = m.sem("gs_zeroed")
        block = ctx.enter_context(nc.Block())

        @block.sync
        def _(sp):
            for q in range(4):
                sp.dma_start(x_sb[:, 4 * q:4 * q + 4, :],
                             d["x"].rearrange("(t p) c -> p t c", p=P)[:, 4 * q:4 * q + 4, :]).then_inc(loaded_x[q], 16)
            for dst, name in ((ident, "ident"), (wt, "WT"), (arl, "a_rl"), (hsel, "headsel"), (nsel, "nodesel"),
                              (val, "curvw"), (coef, "coef"), (gated, "gated"), (ci, "curv_i")):
                sp.dma_start(dst[:, :], d[name]).then_inc(loaded, 16)
            sp.dma_start(gate[:, :], d["gate"].to_broadcast([P, 1])).then_inc(loaded, 16)
            for i in range(GI):
                sp.dma_start(cj[CF * i:CF * i + CF, :], d["curvT"]).then_inc(loaded, 16)
            sp.dma_start(mask[:, 0, :].bitcast(I32), d["adj"].rearrange("(t p) j -> t p j", p=P)[0]).then_inc(adj_in, 16)
            sp.wait_ge(zeroed, 1)
            for b in range(2):
                sp.dma_start(feat[CJ_ROW:PAD_ROW, b, :], d["curvT"]).then_inc(spread, 16)
            sp.wait_ge(er_done, 4)
            for b in range(2):
                sp.dma_start(feat[ER_ROW:CJ_ROW, b, :], er08[0:H, :]).then_inc(spread, 16)
            sp.wait_ge(spread, 64)

        @block.gpsimd
        def _(pool):
            pool.memset(feat[96:P, :, :], 0.0).then_inc(zeroed, 1)
            pool.wait_ge(zeroed, 1)
            pool.memset(values[:, :, :, :], 0.0).then_inc(zeroed, 1)
            pool.wait_ge(zeroed, 2)
            pool.memset(values[:, :, :, D:D + 1], 1.0).then_inc(zeroed, 1)

        @block.vector
        def _(dve):
            link = chain(dve, link_s)
            dve.memset(eps[:, :], LN_EPS).then_inc(fixed, 1)
            for t in range(NT):
                if t % 4 == 0:
                    dve.wait_ge(loaded_x[t // 4], 16)
                dve.bn_stats(st[:, t, :], x_sb[:, t, :]).then_inc(stats_done, 1)
            dve.wait_ge(stats_done, NT)
            moments(dve, link, st, stat)
            dve.sem_inc(var_ready, 1)
            dve.wait_ge(loaded, 16 * (10 + GI))
            for n in range(2):
                dve.tensor_scalar(ar[:, n, :], hsel[:, :], arl[:, n:n + 1], None, ALU.mult).then_inc(ar_ready, 1)
            link(dve.tensor_scalar(gated[:, 0:1], gated[:, 0:1], gate[:, 0:1], None, ALU.mult))
            link(dve.tensor_tensor(gate[:, :], gated[:, 0:1], gated[:, 1:2], ALU.add))
            link(dve.scalar_tensor_tensor(wlog[:, :], val[:, :], gate[:, 0:1], coef[:, :], ALU.mult, ALU.mult))
            dve.wait_ge(std_ready, 1)
            link(dve.reciprocal(stat[:, 5, :], stat[:, 4, :]))
            for t in range(NT):
                dve.tensor_scalar(sq[:, t, :], x_sb[:, t, :], stat[:, 0, t:t + 1], stat[:, 5, t:t + 1], ALU.subtract,
                                  ALU.mult).then_inc(xn_ready, 1)
            for q in range(4):
                dve.wait_ge(xt_ps, q + 1)
                dve.tensor_copy(xt[:, 512 * q:512 * q + 512], ps[:, q, :]).then_inc(xt_ready, 1)
            for q in range(4):
                dve.wait_ge(h_ps, q + 1)
                dve.tensor_copy(ht[:, 512 * q:512 * q + 512], ps[:, 4 + q, :]).then_inc(h_ready, 1)
            el_cols = el_tmp[:, :].rearrange("p (g i) -> p g i", i=GI)
            dve.wait_ge(e_ps, 4)
            dve.tensor_tensor(el_cols, ps[:, 0:4, :].rearrange("p q (g i) -> p (q g) i", i=GI),
                              nsel[:, :].rearrange("p (o i) -> p o i", o=1).to_broadcast([P, GROUPS, GI]),
                              ALU.mult).then_inc(el_mul, 1)
            dve.wait_ge(el_mul, 1)
            dve.tensor_reduce(el08[:, :], el_cols, AX.X, ALU.add).then_inc(el_done, 1)
            dve.wait_ge(adj_in, 16)
            dve.tensor_scalar(mask[:, 0, :], mask[:, 0, :].bitcast(I32), 0.0, 1.0, ALU.is_gt, ALU.subtract).then_inc(mask_done, 1)
            dve.wait_ge(zeroed, 3)
            for q in range(4):
                dve.wait_ge(v_ps, q + 1)
                dve.tensor_copy(values[:, 4 * q:4 * q + 4, :, 0:D],
                                ps[:, q, :].rearrange("p (t h e) -> p t h e", t=4, h=H)).then_inc(v_done, 1)

        @block.scalar
        def _(act):
            act.wait_ge(fixed, 1)
            act.wait_ge(var_ready, 1)
            act.activation(stat[:, 4, :], stat[:, 1, :], ACT.Sqrt, bias=eps[:, 0:1], scale=1.0 / C).then_inc(std_ready, 1)
            for q in range(4):
                act.wait_ge(e_ps, 4 + q + 1)
                act.mul(er08[:, 512 * q:512 * q + 512], ps[:, 4 + q, :], 1 - SLOPE).then_inc(er_done, 1)

        @block.tensor
        def _(pe):
            pe.wait_ge(loaded, 16 * (10 + GI))
            for q in range(4):
                pe.wait_ge(xn_ready, 4 * q + 4)
                for k in range(4):
                    mm = pe.transpose(ps[:, q, P * k:P * k + P], sq[:, 4 * q + k, :], ident[:, :])
                mm.then_inc(xt_ps, 1)
            for q in range(4):
                pe.wait_ge(xt_ready, q + 1)
                pe.matmul(ps[:, 4 + q, :], wt[:, :], xt[:, 512 * q:512 * q + 512], start=True, stop=True).then_inc(h_ps, 1)
            pe.wait_ge(ar_ready, 2)
            for n in (1, 0):
                for q in range(4):
                    if n:
                        pe.wait_ge(h_ready, q + 1)
                    bank = q if n else 4 + q
                    pe.matmul(ps[:, bank, :], ar[:, n, :], ht[:, 512 * q:512 * q + 512], start=True, stop=True).then_inc(e_ps, 1)
            pe.wait_ge(el_mul, 1)
            for q in range(4):
                for k in range(4):
                    t = 4 * q + k
                    mm = pe.matmul(ps[:, q, P * k:P * k + P], xt[:, P * t:P * t + P], wt[:, :], start=True, stop=True)
                mm.then_inc(v_ps, 1)


def graph_attention(nc, d, x_sb, values, er08, cj, ci, el08, feat, wlog, ident, mask, gstat):
    AHEAD = 2
    PARTS = [range(3 * k, 3 * k + 3) for k in range(4)] + [range(12, NT)]
    LEAST = [2, 3, 4, 5]
    with ExitStack() as ctx:
        m = Names(nc, ctx)
        logits = m.sb("ga_logits", [P, LSLOTS, N])
        probs_t = m.sb("ga_probs_t", [P, 3, NT, H, AVN])
        av_sb = m.sb("ga_av", [P, 2, P])
        mx = m.sb("ga_mx", [P, 4, LSLOTS])
        rden = m.sb("ga_rden", [P, H])
        gout = m.sb("ga_gout", [P, C])
        lps = m.ps("ga_lps", [P, 4, 512])
        tps = m.ps("ga_tps", [P, 3, 512])
        avp = m.ps("ga_avp", [P, 512])
        adj_in = m.sem("ga_adj_in")
        adj_seen = m.sem("ga_adj_seen")
        mask_ready = m.sem("ga_mask_ready")
        mask_in = [m.sem(f"ga_mask_in{b}") for b in range(2)]
        feat_ready = m.sem("ga_feat_ready")
        logit_half = m.sem("ga_logit_half")
        half_seen = m.sem("ga_half_seen")
        relu_ready = m.sem("ga_relu_ready")
        max_half = m.sem("ga_max_half")
        keep_ready = m.sem("ga_keep_ready")
        shift_ready = m.sem("ga_shift_ready")
        probs_ready = m.sem("ga_probs_ready")
        turned = m.sem("ga_turned")
        act_moved = m.sem("ga_act_moved")
        dve_moved = m.sem("ga_dve_moved")
        av_part = m.sem("ga_av_part")
        av_moved = m.sem("ga_av_moved")
        out_turned = m.sem("ga_out_turned")
        rden_ready = m.sem("ga_rden_ready")
        scaled = m.sem("ga_scaled")
        out_done = m.sem("ga_out_done")
        stats_done = m.sem("ga_stats_done")
        block = ctx.enter_context(nc.Block())
        av_view = avp[:, 0:2 * P].rearrange("p (q s i) -> p q s i", q=2, s=2)
        out_view = avp[:, 2 * P:4 * P].rearrange("p (h e) -> p h e", e=HW)

        def tiles(engine, body):
            body(0, False, True, False)
            with engine.Fori(0, NT // 2 - 1) as pair:
                body(engine.snap(2 * pair + 1), True, True, True)
                body(engine.snap(2 * pair + 2), False, True, True)
            body(NT - 1, True, False, True)

        def moved(odd, g, q):
            dst = probs_t[:, 1 if g >= AVG else 2 * odd, 4 * q:4 * q + 4, :, GI * (g % AVG):GI * (g % AVG) + GI]
            src = tps[:, TBANK[q], :].rearrange("p (k i h) -> p k h i", k=4, h=H)
            return dst, src

        @block.sync
        def _(sp):
            adj_rows = d["adj"].rearrange("(t p) j -> t p j", p=P)

            def mask_rows(t, odd, g):
                if not (isinstance(t, int) and t == 0 and g < 2):
                    sp.wait_ge(logit_half, 2 * (t * GPT + g - 1))
                sp.dma_start(feat[MASK_ROW:P, g % 2, :], mask[GI * g:GI * g + GI, odd, :]).then_inc(mask_in[g % 2], 16)

            def tile_of_rows(t, odd, ahead, earlier):
                if earlier:
                    sp.wait_ge(mask_ready, t)
                for g in range(GPT):
                    mask_rows(t, odd, g)
                    if g == 1 and ahead:
                        nxt = t + 1 if isinstance(t, int) else sp.snap(t + 1)
                        sp.dma_start(mask[:, 1 - odd, :].bitcast(I32),
                                     adj_rows[bass.ds(nxt, 1)].rearrange("o p j -> (o p) j")).then_inc(adj_in, 16)
            tiles(sp, tile_of_rows)

        @block.gpsimd
        def _(pool):
            def body(t, odd, ahead, earlier):
                if ahead:
                    pool.wait_ge(adj_in, 16 * (t + 1))
                    pool.sem_inc(adj_seen, 1)
                    pool.tensor_scalar(mask[:, 1 - odd, :], mask[:, 1 - odd, :].bitcast(I32), 0.0, 1.0, ALU.is_gt,
                                       ALU.subtract).then_inc(mask_ready, 1)
                if earlier:
                    add(t - 1)

            def add(t):
                xt = x_sb[:, bass.ds(t, 1), :].rearrange("p o c -> p (o c)")
                pool.wait_ge(scaled, t + 1)
                pool.tensor_tensor(xt, xt, gout[:, :], ALU.add).then_inc(out_done, 1)
            tiles(pool, body)
            add(NT - 1)

        @block.vector
        def _(dve):
            def features(t, g):
                first = isinstance(t, int) and t == 0
                if not (first and g < 2):
                    dve.wait_ge(logit_half, 2 * (t * GPT + g - 1))
                col = t * GPT + g
                dve.tensor_scalar(feat[0:FR, g % 2, :], cj[:, :], ci[0:FR, bass.ds(col, 1)], 0.0,
                                  ALU.subtract, ALU.max).then_inc(feat_ready, 1)

            def add_half(t, g, half):
                s = g % LSLOTS
                if half == 0:
                    dve.wait_ge(relu_ready, t * GPT + g + 1)
                else:
                    dve.wait_ge(max_half, 2 * (t * GPT + g) + 1)
                dve.wait_ge(logit_half, 2 * (t * GPT + g) + half + 1)
                dve.sem_inc(half_seen, 1)
                part = logits[:, s, HALF * half:HALF * half + HALF]
                dve.tensor_tensor_reduce(part, lps[:, 2 * half:2 * half + 2, :].rearrange("p q n -> p (q n)"), part, 1.0,
                                         -3e38 if half == 0 else mx[:, 0, s:s + 1], ALU.add, ALU.max,
                                         mx[:, half, s:s + 1]).then_inc(max_half, 1)

            def shift(t, g):
                s = g % LSLOTS
                dve.wait_ge(max_half, 2 * (t * GPT + g) + 2)
                dve.tensor_scalar(mx[:, 2, s:s + 1], mx[:, 1, s:s + 1], -0.5 * MASKED, None, ALU.is_gt).then_inc(keep_ready, 1)
                dve.wait_ge(keep_ready, t * GPT + g + 1)
                dve.scalar_tensor_tensor(mx[:, 3, s:s + 1], mx[:, 1, s:s + 1], -1.0, mx[:, 2, s:s + 1],
                                         ALU.mult, ALU.mult).then_inc(shift_ready, 1)

            def move(t, odd, g, q):
                dve.wait_ge(turned, 4 * (t * GPT + g) + q + 1)
                if not (isinstance(t, int) and t == 0) and g == AVG:
                    dve.wait_ge(av_part, len(PARTS) * (t - 1) + LEAST[q])
                dve.tensor_copy(*moved(odd, g, q)).then_inc(dve_moved, 1)

            def output(t):
                dve.wait_ge(out_turned, t + 1)
                dve.reciprocal(rden[:, :], out_view[:, :, D]).then_inc(rden_ready, 1)
                dve.wait_ge(rden_ready, t + 1)
                dve.tensor_tensor(gout[:, :].rearrange("p (h e) -> p h e", e=D), out_view[:, :, 0:D], bc(rden[:, :], D),
                                  ALU.mult).then_inc(scaled, 1)

            features(0, 0)
            features(0, 1)
            for g in range(AHEAD):
                add_half(0, g, 0)
                add_half(0, g, 1)
                shift(0, g)
                if g == 0:
                    features(0, 2)

            def body(t, odd, ahead, earlier):
                for g in range(GPT):
                    if g == AVG + 2 and earlier:
                        output(t - 1)
                    if g == GPT - 1 and earlier:
                        dve.wait_ge(out_done, t)
                    u, v = divmod(g + AHEAD + 1, GPT)
                    if u == 0 or ahead:
                        features(t + u, v)
                    u, v = divmod(g + AHEAD, GPT)
                    if u == 0 or ahead:
                        add_half(t + u, v, 0)
                    move(t, odd, g, 1)
                    if u == 0 or ahead:
                        add_half(t + u, v, 1)
                        shift(t + u, v)
                    move(t, odd, g, 3)
            tiles(dve, body)
            for t in range(NT):
                if t == NT - 1:
                    output(t)
                dve.wait_ge(out_done, t + 1)
                dve.bn_stats(gstat[:, t, :], x_sb[:, t, :]).then_inc(stats_done, 1)

        @block.scalar
        def _(act):
            def relu_part(t, g):
                if not (isinstance(t, int) and t == 0 and g < LSLOTS):
                    act.wait_ge(turned, 4 * (t * GPT + g - LSLOTS + 1))
                act.activation(logits[:, g % LSLOTS, :], er08[:, :], ACT.Relu,
                               bias=el08[:, bass.ds(t * GPT + g, 1)]).then_inc(relu_ready, 1)

            def exponent(t, g):
                s = g % LSLOTS
                act.wait_ge(shift_ready, t * GPT + g + 1)
                act.activation(logits[:, s, :], logits[:, s, :], ACT.Exp, bias=mx[:, 3, s:s + 1],
                               scale=mx[:, 2, s:s + 1]).then_inc(probs_ready, 1)

            def move(t, odd, g, q):
                act.wait_ge(turned, 4 * (t * GPT + g) + q + 1)
                if not (isinstance(t, int) and t == 0) and g == AVG:
                    act.wait_ge(av_part, len(PARTS) * (t - 1) + LEAST[q])
                act.copy(*moved(odd, g, q)).then_inc(act_moved, 1)

            def move_av(parts, swapped):
                act.wait_ge(av_part, parts)
                for b in range(2):
                    half = 1 - b if swapped else b
                    act.copy(av_sb[:, :, AVN * half:AVN * half + AVN], av_view[:, :, b, :]).then_inc(av_moved, 1)

            for g in range(AHEAD + 1):
                relu_part(0, g)
            exponent(0, 0)

            def body(t, odd, ahead, earlier):
                for g in range(GPT):
                    if g == AVG + 1 and earlier:
                        move_av(len(PARTS) * t, not odd)
                    if g == GPT - 1 and earlier:
                        act.wait_ge(out_turned, t)
                    u, v = divmod(g + 1, GPT)
                    if u == 0 or ahead:
                        exponent(t + u, v)
                    move(t, odd, g, 0)
                    u, v = divmod(g + AHEAD + 1, GPT)
                    if u == 0 or ahead:
                        relu_part(t + u, v)
                    move(t, odd, g, 2)
            tiles(act, body)
            move_av(len(PARTS) * (NT - 1) + 1, False)

        @block.tensor
        def _(pe):
            def product(t, g, half):
                if half == 0:
                    pe.wait_ge(feat_ready, t * GPT + g + 1)
                    pe.wait_ge(mask_in[g % 2], 16 * (t * (GPT // 2) + g // 2 + 1))
                if not (isinstance(t, int) and t == 0 and g == 0):
                    pe.wait_ge(max_half, 2 * (t * GPT + g - 1) + half + 1)
                for q in (2 * half, 2 * half + 1):
                    mm = pe.matmul(lps[:, q, :], wlog[:, :], feat[:, g % 2, 512 * q:512 * q + 512], start=True, stop=True)
                mm.then_inc(logit_half, 1)

            def turn(t, g, q):
                if q == 0:
                    pe.wait_ge(probs_ready, t * GPT + g + 1)
                first = isinstance(t, int) and t == 0 and g == 0
                n = t * GPT + g
                if q == 3:
                    pe.wait_ge(dve_moved, 2 * n + 1)
                elif q == 1:
                    if not first:
                        pe.wait_ge(dve_moved, 2 * n)
                elif not first:
                    pe.wait_ge(act_moved, 2 * n - (1 if q == 0 else 0))
                for k in range(4):
                    j = 4 * q + k
                    mm = pe.transpose(tps[:, TBANK[q], P * k:P * k + P], logits[:, g % LSLOTS, P * j:P * j + P], ident[:, :])
                mm.then_inc(turned, 1)

            def value_product(t, odd, k):
                if k == 0:
                    pe.wait_ge(act_moved, 2 * GPT * (t + 1))
                    pe.wait_ge(dve_moved, 2 * GPT * (t + 1))
                for j in PARTS[k]:
                    for h in range(H):
                        r = HW * (h % 4)
                        mm = pe.matmul(avp[r:r + HW, P * (h // 4):P * (h // 4) + P],
                                       values[:, j, h, :], probs_t[:, odd:odd + 2, j, h, :],
                                       start=(j == 0 and h < 4), stop=(j == NT - 1), skip_group_check=True)
                mm.then_inc(av_part, 1)

            def half_product(b, js):
                if js[0] == 0:
                    pe.wait_ge(act_moved, 2 * (GROUPS - GPT + AVG * (b + 1)))
                    pe.wait_ge(dve_moved, 2 * (GROUPS - GPT + AVG * (b + 1)))
                for j in js:
                    for h in range(H):
                        r, col = HW * (h % 4), P * (h // 4) + AVN * b
                        mm = pe.matmul(avp[r:r + HW, col:col + AVN], values[:, j, h, :], probs_t[:, 2 - b, j, h, :],
                                       start=(b == 0 and j == 0 and h < 4), stop=(j == NT - 1), skip_group_check=True)
                return mm

            def turn_out(t):
                pe.wait_ge(av_moved, 2 * t + 2)
                for q in range(2):
                    mm = pe.transpose(avp[:, P * (2 + q):P * (2 + q) + P], av_sb[:, q, :], ident[:, :])
                mm.then_inc(out_turned, 1)

            for g in range(AHEAD):
                product(0, g, 0)
                product(0, g, 1)

            def body(t, odd, ahead, earlier):
                for g in range(GPT):
                    u, v = divmod(g + AHEAD, GPT)
                    more = u == 0 or ahead
                    if more:
                        product(t + u, v, 0)
                    turn(t, g, 0)
                    turn(t, g, 1)
                    if g == len(PARTS) - 1 and earlier:
                        value_product(t - 1, not odd, g)
                    if more:
                        product(t + u, v, 1)
                    turn(t, g, 2)
                    turn(t, g, 3)
                    if g < len(PARTS) - 1 and earlier:
                        value_product(t - 1, not odd, g)
                    if g == AVG + 1 and earlier:
                        turn_out(t - 1)
                    if g == GPT - 1 and ahead and earlier:
                        pe.wait_ge(scaled, t)
                    if g >= GPT - 2 and not ahead:
                        if g == GPT - 2:
                            pe.wait_ge(scaled, t)
                        half_product(0, range(8 * (g - GPT + 2), 8 * (g - GPT + 2) + 8))
            tiles(pe, body)
            half_product(1, range(NT)).then_inc(av_part, 1)
            turn_out(NT - 1)


def block_input(nc, d, x_sb, y, ident, gstat, qs, ks, vx, identb, cutb, k_in, q_in):
    KR = NKV * HD
    with ExitStack() as ctx:
        m = Names(nc, ctx)
        h = m.sb("bi_h", [P, NT, C])
        stat = m.sb("bi_stat", [P, 10, NT])
        eps = m.sb("bi_eps", [P, 2])
        ht = m.sb("bi_ht", [P, N])
        ln1 = m.sb("bi_ln1", [P, 1])
        wq = m.sb("bi_wq", [P, 2, NH * HD])
        wk = m.sb("bi_wk", [P, 2, KR])
        wv = m.sb("bi_wv", [P, KR])
        cos = m.sb("bi_cos", [P, N])
        sin = m.sb("bi_sin", [P, N])
        cosk = m.sb("bi_cosk", [P, 2, TC])
        sink = m.sb("bi_sink", [P, 2, TC])
        rot = m.sb("bi_rot", [P, 2, 2, TC])
        full = m.sb("bi_full", [P, 2, TC])
        cut = m.sb("bi_cut", [P, 2, P])
        q_hi, q_lo = m.sb("bi_q_hi", [P, 4, TC], F32R), m.sb("bi_q_lo", [P, 4, TC], F32R)
        k_hi, k_lo = m.sb("bi_k_hi", [P, 2, TC], F32R), m.sb("bi_k_lo", [P, 2, TC], F32R)
        ps = m.ps("bi_ps", [P, 8, 512])
        loaded, tables, cut_in = m.sem("bi_loaded"), m.sem("bi_tables"), m.sem("bi_cut_in")
        link_s, fixed = m.sem("bi_link"), m.sem("bi_fixed")
        sum_ready, std_ready, scale_ready = m.sem("bi_sum"), m.sem("bi_std"), m.sem("bi_scale")
        y_done, h_ready = m.sem("bi_y"), m.sem("bi_h_s")
        ht_ps, ht_ready, v_ps, v_done = m.sem("bi_ht_ps"), m.sem("bi_ht_s"), m.sem("bi_v_ps"), m.sem("bi_v_s")
        unit_ps = m.sem("bi_unit_ps")
        by_cos, by_sin, rotated = m.sem("bi_by_cos"), m.sem("bi_by_sin"), m.sem("bi_rotated")
        high, low = m.sem("bi_high"), m.sem("bi_low")
        block = ctx.enter_context(nc.Block())
        units = [(c, i) for c in range(2) for i in range(3)]

        def tables_of(c, i):
            if i == 0:
                return cosk[:, c, :], sink[:, c, :], k_hi[:, c, :], k_lo[:, c, :]
            q = 2 * c + i - 1
            cols = slice(TC * q, TC * q + TC)
            return cos[:, cols], sin[:, cols], q_hi[:, q, :], q_lo[:, q, :]

        @block.sync
        def _(sp):
            sp.dma_start(ln1[:, :], d["ln1"]).then_inc(loaded, 16)
            for k in range(2):
                sp.dma_start(wq[:, k, :], d["wqT"][k]).then_inc(loaded, 16)
                sp.dma_start(wk[:, k, :], d["wkT"][k]).then_inc(loaded, 16)
            sp.dma_start(wv[:, :], d["wvT"]).then_inc(loaded, 16)
            sp.dma_start(cosk[:, :, :], d["cosK"]).then_inc(tables, 16)
            sp.dma_start(sink[:, :, :], d["sinK"]).then_inc(tables, 16)
            sp.dma_start(cos[:, :], d["cosT"]).then_inc(tables, 16)
            sp.dma_start(sin[:, :], d["sinT"]).then_inc(tables, 16)
            sp.dma_start(cut[:, 0, :], d["causal_ts"]).then_inc(cut_in, 16)
            sp.dma_start(cut[:, 1, :], d["causal_st"]).then_inc(cut_in, 16)
            for c in range(2):
                sp.wait_ge(low, 3 * c + 1)
                for j in range(2):
                    for g in range(NKV):
                        rows, cols = slice(KR * j + HD * g, KR * j + HD * g + HD), slice(TC * (2 * c + j), TC * (2 * c + j) + TC)
                        for part, src in enumerate((k_hi, k_hi, k_lo)):
                            sp.dma_start(ks[HD * part:HD * part + HD, g, cols].bitcast(F32),
                                         src[rows, c, :].bitcast(F32)).then_inc(k_in[c], 16)
                sp.wait_ge(low, 3 * c + 3)
                for h_ in range(NH):
                    rows, cols = slice(HD * h_, HD * h_ + HD), slice(2 * TC * c, 2 * TC * c + 2 * TC)
                    for part, src in enumerate((q_hi, q_lo, q_hi)):
                        sp.dma_start(qs[HD * part:HD * part + HD, h_, cols].bitcast(F32),
                                     src[rows, 2 * c:2 * c + 2, :].rearrange("p q n -> p (q n)").bitcast(F32)).then_inc(q_in[c], 16)

        @block.gpsimd
        def _(pool):
            link = chain(pool, fixed)
            link(pool.memset(ks[3 * HD:3 * HD + 1, :, :].bitcast(F32), 1.0))
            link(pool.memset(vx[:, :, :, :], 0.0))
            link(pool.memset(vx[:, :, :, HD:HD + 1], 1.0))
            link(pool.memset(cutb[:, :, :], 0.0))
            link(pool.tensor_copy(identb[:, :], ident[:, :]))
            pool.wait_ge(cut_in, 32)
            link(pool.tensor_copy(cutb[:, 0, TC - P:TC], cut[:, 0, :]))
            link(pool.tensor_copy(cutb[:, 1, 0:P], cut[:, 1, :]))
            pool.wait_ge(scale_ready, 1)
            for t in range(NT):
                if t:
                    pool.wait_ge(y_done, t)
                pool.tensor_scalar(y[:, t, :], x_sb[:, t, :], stat[:, 0, t:t + 1], stat[:, 5, t:t + 1], ALU.subtract,
                                   ALU.mult).then_inc(y_done, 1)

        @block.vector
        def _(dve):
            link = chain(dve, link_s)
            link(dve.memset(eps[:, 0:1], LN_EPS))
            link(dve.memset(eps[:, 1:2], RMS_EPS))
            moments(dve, link, gstat, stat)
            dve.sem_inc(sum_ready, 1)
            dve.wait_ge(std_ready, 1)
            link(dve.reciprocal(stat[:, 5, :], stat[:, 4, :]))
            link(dve.tensor_tensor(stat[:, 6, :], stat[:, 1, :], stat[:, 5, :], ALU.mult))
            dve.tensor_tensor(stat[:, 7, :], stat[:, 6, :], stat[:, 5, :], ALU.mult).then_inc(sum_ready, 1)
            dve.wait_ge(std_ready, 2)
            link(dve.reciprocal(stat[:, 9, :], stat[:, 8, :]))
            dve.tensor_tensor(stat[:, 6, :], stat[:, 5, :], stat[:, 9, :], ALU.mult).then_inc(scale_ready, 1)
            dve.wait_ge(scale_ready, 1)
            for t in range(NT):
                dve.tensor_scalar(h[:, t, :], x_sb[:, t, :], stat[:, 0, t:t + 1], stat[:, 6, t:t + 1], ALU.subtract,
                                  ALU.mult).then_inc(h_ready, 1)
            dve.wait_ge(tables, 64)
            for u, (c, i) in enumerate(units):
                cs, sn, hi, lo = tables_of(c, i)
                bank, s = 2 + 2 * (u % 3), u % 2
                dve.wait_ge(unit_ps, u + 1)
                if u >= 2:
                    dve.wait_ge(rotated, u - 1)
                dve.tensor_tensor(rot[:, s, 0, :], ps[:, bank, :], cs, ALU.mult).then_inc(by_cos, 1)
                dve.tensor_tensor(rot[:, s, 1, :], ps[:, bank + 1, :], sn, ALU.mult).then_inc(by_sin, 1)
                if u:
                    pc, pi = units[u - 1]
                    _, _, phi, plo = tables_of(pc, pi)
                    dve.wait_ge(high, u)
                    dve.tensor_tensor(plo, full[:, 1 - s, :], phi.bitcast(F32), ALU.subtract).then_inc(low, 1)
                dve.wait_ge(by_cos, u + 1)
                dve.wait_ge(by_sin, u + 1)
                if u >= 2:
                    dve.wait_ge(low, u - 1)
                dve.tensor_tensor(full[:, s, :], rot[:, s, 0, :], rot[:, s, 1, :], ALU.add).then_inc(rotated, 1)
            _, _, phi, plo = tables_of(*units[-1])
            dve.wait_ge(high, len(units))
            dve.tensor_tensor(plo, full[:, 1, :], phi.bitcast(F32), ALU.subtract).then_inc(low, 1)

        @block.scalar
        def _(act):
            act.wait_ge(sum_ready, 1)
            act.activation(stat[:, 4, :], stat[:, 1, :], ACT.Sqrt, bias=eps[:, 0:1], scale=1.0 / C).then_inc(std_ready, 1)
            act.wait_ge(sum_ready, 2)
            act.activation(stat[:, 8, :], stat[:, 7, :], ACT.Sqrt, bias=eps[:, 1:2], scale=1.0 / C).then_inc(std_ready, 1)
            act.wait_ge(loaded, 96)
            for q in range(4):
                act.wait_ge(ht_ps, q + 1)
                act.activation(ht[:, TC * q:TC * q + TC], ps[:, q % 2, :], ACT.Copy, scale=ln1[:, 0:1]).then_inc(ht_ready, 1)
            for u, (c, i) in enumerate(units):
                act.wait_ge(rotated, u + 1)
                act.copy(tables_of(c, i)[2], full[:, u % 2, :]).then_inc(high, 1)
            act.wait_ge(fixed, 3)
            for q in range(2):
                act.wait_ge(v_ps, q + 1)
                act.copy(vx[:, 8 * q:8 * q + 8, :, 0:HD],
                         ps[:, q, :].rearrange("p (t g e) -> p t g e", t=8, g=NKV)).then_inc(v_done, 1)

        @block.tensor
        def _(pe):
            for q in range(4):
                pe.wait_ge(h_ready, 4 * q + 4)
                if q >= 2:
                    pe.wait_ge(ht_ready, q - 1)
                for k in range(4):
                    mm = pe.transpose(ps[:, q % 2, P * k:P * k + P], h[:, 4 * q + k, :], ident[:, :])
                mm.then_inc(ht_ps, 1)
            pe.wait_ge(loaded, 96)
            for u, (c, i) in enumerate(units):
                bank = 2 + 2 * (u % 3)
                pe.wait_ge(ht_ready, 2 * c + (2 if i != 1 else 1))
                if u >= 3:
                    pe.wait_ge(by_cos, u - 2)
                    pe.wait_ge(by_sin, u - 2)
                for r in range(2):
                    if i == 0:
                        for j in range(2):
                            q = 2 * c + j
                            mm = pe.matmul(ps[KR * j:KR * j + KR, bank + r, :], wk[:, r, :], ht[:, TC * q:TC * q + TC],
                                           start=True, stop=True)
                    else:
                        q = 2 * c + i - 1
                        mm = pe.matmul(ps[:, bank + r, :], wq[:, r, :], ht[:, TC * q:TC * q + TC], start=True, stop=True)
                mm.then_inc(unit_ps, 1)
            for q in range(2):
                for k in range(8):
                    t = 8 * q + k
                    mm = pe.matmul(ps[:, q, KR * k:KR * k + KR], ht[:, P * t:P * t + P], wv[:, :], start=True, stop=True)
                mm.then_inc(v_ps, 1)


def causal_attention(nc, d, qs, ks, vx, ident, u_sb, identb, cutb, k_in, q_in):
    K = 3 * HD
    chunks = [(g, tc) for g in range(NKV) for tc in range(N // TC)]
    tiles_c = TC // P
    ahead, rows_of = [], {}
    for c, (g, tc) in enumerate(chunks):
        for h in (2 * g, 2 * g + 1):
            for tt in range(tiles_c * tc, tiles_c * tc + tiles_c):
                for sc in range(tc + 1):
                    ahead.append((c, h, tt, sc))
        rows_of[c] = len(ahead)
    turn_after = {rows_of[c] + 1: c for c in rows_of}
    steps = []
    for i, unit in enumerate(ahead):
        steps.append(unit)
        if i in turn_after:
            steps.append((turn_after[i], None, None, None))
    steps.append((len(chunks) - 1, None, None, None))
    last_of = {c: max(i for i, u in enumerate(steps) if u[0] == c and u[1] is not None) for c in range(len(chunks))}
    halves_from = [min(i for i, u in enumerate(steps) if u[0] == c) for c in (0, N // TC // 2)]
    units = [(c, sj) for c, (g, tc) in enumerate(chunks) for sj in range(tiles_c * (tc + 1))]
    end_of = {c: max(i for i, u in enumerate(units) if u[0] == c) for c in range(len(chunks))}

    def due(n):
        return min(len(steps), LEAD + (RATE * n + 1) // 2)

    with ExitStack() as ctx:
        m = Names(nc, ctx)
        probs = m.sb("ca_probs", [P, 3, 2, TC])
        mx = m.sb("ca_mx", [P, len(chunks), 2, tiles_c, NT // tiles_c])
        neg = m.sb("ca_neg", [P, len(chunks), 2, tiles_c])
        negt = m.sb("ca_negt", [2 * tiles_c, len(chunks), P], F32R)
        sps = m.ps("ca_sps", [P, 2, 512])
        tps = m.ps("ca_tps", [P, 2, 2, TC])
        ops = m.ps("ca_ops", [P, 2, TC])
        link_s = m.sem("ca_link")
        s_ready, s_used = m.sem("ca_s_ready"), m.sem("ca_s_used")
        neg_ready = m.sem("ca_neg_ready")
        neg_copied = m.sem("ca_neg_copied")
        neg_row = [m.sem(f"ca_neg_row{c}") for c in range(len(chunks))]
        t_ready, t_exp = m.sem("ca_t_ready"), m.sem("ca_t_exp")
        pv_done, o_moved = m.sem("ca_pv_done"), m.sem("ca_o_moved")
        block = ctx.enter_context(nc.Block())

        @block.sync
        def _(sp):
            for c, (g, tc) in enumerate(chunks):
                sp.wait_ge(neg_copied, c + 1)
                for h in range(2):
                    dst = qs[K:K + 1, 2 * g + h, TC * tc:TC * tc + TC]
                    sp.dma_start(dst.bitcast(F32), negt[tiles_c * h:tiles_c * h + tiles_c, c, :].bitcast(F32)).then_inc(neg_row[c], 16)

        @block.vector
        def _(dve):
            link = chain(dve, link_s)
            link(dve.memset(mx[:, :, :, :, :], -3e38))

            def take(n):
                c, h, tt, sc = steps[n]
                g, tc = chunks[c]
                dve.wait_ge(s_ready, n + 1)
                if h is None:
                    dve.tensor_copy(negt[:, c, :], sps[0:2 * tiles_c, n % 2, 0:P]).then_inc(s_used, 1)
                    dve.wait_ge(s_used, n + 1)
                    dve.sem_inc(neg_copied, 1)
                    return
                w = min(512, P * (tt + 1) - 512 * sc)
                dve.tensor_reduce(mx[:, c, h - 2 * g, tt - tiles_c * tc, sc:sc + 1], sps[:, n % 2, 0:w], AX.X,
                                  ALU.max).then_inc(s_used, 1)
                if n == last_of[c]:
                    dve.wait_ge(s_used, n + 1)
                    dve.tensor_reduce(neg[:, c, :, :], mx[:, c, :, :, :], AX.X, ALU.max, negate=True).then_inc(neg_ready, 1)

            def move_out(c):
                dve.wait_ge(pv_done, end_of[c] + 1)
                dve.tensor_copy(u_sb[:, chunks[c][0], TC * chunks[c][1]:TC * chunks[c][1] + TC], ops[:, c % 2, :]).then_inc(o_moved, 1)

            for n in range(due(0)):
                take(n)
            for u, (c, sj) in enumerate(units):
                for n in range(due(u), due(u + 1)):
                    take(n)
                if sj == 1 and c:
                    move_out(c - 1)
            move_out(len(chunks) - 1)

        @block.scalar
        def _(act):
            for u, (c, sj) in enumerate(units):
                off = max(0, P * sj - TC * chunks[c][1])
                act.wait_ge(t_ready, u + 1)
                if u >= 3:
                    act.wait_ge(pv_done, u - 2)
                act.activation(probs[:, u % 3, :, off:TC], tps[:, u % 2, :, off:TC], ACT.Exp,
                               scale=float(np.float32(1) / np.sqrt(np.float32(HD)))).then_inc(t_exp, 1)

        @block.tensor
        def _(pe):
            def by_target(n):
                c, h, tt, sc = steps[n]
                g, tc = chunks[c]
                if n >= 2:
                    pe.wait_ge(s_used, n - 1)
                if h is None:
                    pe.wait_ge(neg_ready, c + 1)
                    pe.transpose(sps[0:2 * tiles_c, n % 2, 0:P], neg[:, c, :, :].rearrange("p h t -> p (h t)"),
                                 ident[:, :]).then_inc(s_ready, 1)
                    return
                if n in halves_from:
                    pe.wait_ge(k_in[tc // 2], 16 * 3 * 2 * NKV)
                    pe.wait_ge(q_in[tc // 2], 16 * 3 * NH)
                w = min(512, P * (tt + 1) - 512 * sc)
                diag = sc == tc
                if diag:
                    pe.matmul(sps[:, n % 2, 0:w], identb[:, :], cutb[:, 0, TC - w:TC], start=True, stop=False)
                pe.matmul(sps[:, n % 2, 0:w], qs[0:K, h, P * tt:P * tt + P], ks[0:K, g, 512 * sc:512 * sc + w],
                          start=not diag, stop=True).then_inc(s_ready, 1)

            def by_source(u):
                c, sj = units[u]
                g, tc = chunks[c]
                off = max(0, P * sj - TC * tc)
                diag = sj >= tiles_c * tc
                if u >= 2:
                    pe.wait_ge(t_exp, u - 1)
                if sj == 0:
                    pe.wait_ge(neg_row[c], 32)
                for h in range(2):
                    if diag:
                        pe.matmul(tps[:, u % 2, h, off:TC], identb[:, :], cutb[:, 1, 0:TC - off], start=True, stop=False)
                    mm = pe.matmul(tps[:, u % 2, h, off:TC], ks[0:K + 1, g, P * sj:P * sj + P],
                                   qs[0:K + 1, 2 * g + h, TC * tc + off:TC * tc + TC], start=not diag, stop=True)
                mm.then_inc(t_ready, 1)

            def values(u):
                c, sj = units[u]
                g, tc = chunks[c]
                off = max(0, P * sj - TC * tc)
                pe.wait_ge(t_exp, u + 1)
                if sj == 0 and c >= 2:
                    pe.wait_ge(o_moved, c - 1)
                for h in range(2):
                    mm = pe.matmul(ops[VW * h:VW * h + VW, c % 2, off:TC], vx[:, sj, g, :], probs[:, u % 3, h, off:TC],
                                   start=(sj == 0), stop=(u == end_of[c]), skip_group_check=True)
                mm.then_inc(pv_done, 1)

            for n in range(due(0)):
                by_target(n)
            for u in range(len(units)):
                by_source(u)
                for n in range(due(u), due(u + 1)):
                    by_target(n)
                if u:
                    values(u - 1)
            values(len(units) - 1)


def project(nc, d, y, u_sb, ystat):
    with ExitStack() as ctx:
        m = Names(nc, ctx)
        wo = m.sb("pj_wo", [P, 2, 256])
        parts = m.sb("pj_parts", [P, 2, NH, C])
        total = m.sb("pj_total", [P, 2, C])
        rden = m.sb("pj_rden", [P, 2, NH])
        ps = m.ps("pj_ps", [P, 2, NH, 256])
        loaded, made, inverted, scaled, summed, added, stats = (m.sem(f"pj_{n}") for n in (
            "loaded", "made", "inverted", "scaled", "summed", "added", "stats"))
        block = ctx.enter_context(nc.Block())

        @block.sync
        def _(sp):
            sp.dma_start(wo[:, :, :], d["woX"]).then_inc(loaded, 16)

        @block.vector
        def _(dve):
            def invert(t):
                dve.wait_ge(made, t + 1)
                dve.reciprocal(rden[:, t % 2, :], ps[:, t % 2, :, C]).then_inc(inverted, 1)

            def scale(t):
                dve.wait_ge(inverted, t + 1)
                dve.tensor_tensor(parts[:, t % 2, :, :], ps[:, t % 2, :, 0:C], bc(rden[:, t % 2, :], C), ALU.mult).then_inc(scaled, 1)

            def add_heads(t):
                dve.wait_ge(scaled, t + 1)
                dve.tensor_reduce(total[:, t % 2, :], parts[:, t % 2, :, :].rearrange("p h c -> p c h"), AX.X,
                                  ALU.add).then_inc(summed, 1)

            def add_y(t):
                dve.wait_ge(summed, t + 1)
                dve.tensor_tensor(y[:, t, :], y[:, t, :], total[:, t % 2, :], ALU.add).then_inc(added, 1)

            def statistics(t):
                dve.wait_ge(added, t + 1)
                dve.bn_stats(ystat[:, t, :], y[:, t, :]).then_inc(stats, 1)

            for t in range(NT + 1):
                if t < NT:
                    invert(t)
                if t:
                    add_heads(t - 1)
                if t < NT:
                    scale(t)
                if t:
                    add_y(t - 1)
                if t >= 2:
                    statistics(t - 2)
            statistics(NT - 1)

        @block.tensor
        def _(pe):
            pe.wait_ge(loaded, 16)
            for t in range(NT):
                if t >= 2:
                    pe.wait_ge(scaled, t - 1)
                for h in range(NH):
                    r = VW * (h % 2)
                    mm = pe.matmul(ps[:, t % 2, 2 * (h % 2) + h // 2, 0:C + 2], u_sb[r:r + VW, h // 2, P * t:P * t + P],
                                   wo[r:r + VW, h // 2, 0:C + 2], start=True, stop=True)
                mm.then_inc(made, 1)


def experts(nc, d, out, x_sb, y, ident, ystat):
    UN, NCH = len(HK), N // TC
    W1, W3, W2 = 0, HID, 2 * HID
    WCOLS = 2 * HID + UN * C
    scratch = nc.dram_tensor("routing_rows", (NE, N), F32).ap()
    with ExitStack() as ctx:
        m = Names(nc, ctx)
        sq = m.sb("ex_sq", [P, NT, C])
        stat = m.sb("ex_stat", [P, 8, NT])
        eps = m.sb("ex_eps", [P, 1])
        ft = m.sb("ex_ft", [P, N])
        f_hi = m.sb("ex_f_hi", [P, N], F32R)
        f_lo = m.sb("ex_f_lo", [P, N], F32R)
        ln2 = m.sb("ex_ln2", [P, 1])
        rw = m.sb("ex_rw", [P, NE])
        desc = m.sb("ex_desc", [P, NE])
        pr = m.sb("ex_pr", [P, NT, NE])
        r = m.sb("ex_r", [P, 6, NT, NE])
        rs = m.sb("ex_rs", [P, 8, NT])
        wgt = m.sb("ex_wgt", [P, NT, NE])
        wgt_t = m.sb("ex_wgt_t", [P, P])
        raw = m.sb("ex_raw", [P, 2, WCOLS])
        w_hi = m.sb("ex_w_hi", [P, 2, WCOLS], F32R)
        w_lo = m.sb("ex_w_lo", [P, 2, WCOLS], F32R)
        wrow = m.sb("ex_wrow", [P, 2, N])
        gate = m.sb("ex_gate", [P, 2, TC])
        hid = m.sb("ex_hid", [P, 2, TC])
        h_hi = m.sb("ex_h_hi", [P, 2, UN, TC], F32R)
        h_lo = m.sb("ex_h_lo", [P, 2, UN, TC], F32R)
        part = m.sb("ex_part", [P, 2, TC])
        acc = m.sb("ex_acc", [P, N])
        aps = m.ps("ex_aps", [P, 2, TC])
        bps = m.ps("ex_bps", [P, 2, TC])
        ops = m.ps("ex_ops", [P, 2, TC])
        xps = m.ps("ex_xps", [P, 2, 512])
        loaded, link_s, zeroed = m.sem("ex_loaded"), m.sem("ex_link"), m.sem("ex_zeroed")
        sum_ready, std_ready, f_ready = m.sem("ex_sum"), m.sem("ex_std"), m.sem("ex_f")
        ft_ps, ft_ready, f_high, f_split = m.sem("ex_ft_ps"), m.sem("ex_ft_s"), m.sem("ex_f_high"), m.sem("ex_f_split")
        r_ps, shifted, r_exp = m.sem("ex_r_ps"), m.sem("ex_shifted"), m.sem("ex_r_exp")
        wgt_ready, wgt_ps, wgt_rows, wgt_dram = m.sem("ex_wgt_s"), m.sem("ex_wgt_ps"), m.sem("ex_wgt_rows"), m.sem("ex_wgt_dram")
        w_in = [m.sem(f"ex_w_in{b}") for b in range(2)]
        row_in = [m.sem(f"ex_row_in{b}") for b in range(2)]
        w_high, w_low = m.sem("ex_w_high"), m.sem("ex_w_low")
        ab_ready = m.sem("ex_ab_ready")
        gated = m.sem("ex_gated")
        multiplied = m.sem("ex_multiplied")
        high, low = m.sem("ex_high"), m.sem("ex_low")
        o_ready = m.sem("ex_o_ready")
        weighted, combined = m.sem("ex_weighted"), m.sem("ex_combined")
        acc_ps, x_ready, total, stored = m.sem("ex_acc_ps"), m.sem("ex_x_ready"), m.sem("ex_total"), m.sem("ex_stored")
        block = ctx.enter_context(nc.Block())

        def pairs(engine, body):
            for b in range(2):
                body(b, b)
            with engine.Fori(1, NE // 2 - 1) as i:
                for b in range(2):
                    body(2 * i + b, b)
            for b in range(2):
                body(NE - 2 + b, b)

        def is_at(e, value):
            return isinstance(e, int) and e == value

        @block.sync
        def _(sp):
            sp.dma_start(ln2[:, :], d["ln2"]).then_inc(loaded, 16)
            sp.dma_start(rw[:, :], d["routerT"]).then_inc(loaded, 16)
            sp.dma_start(desc[:, :], d["descend"]).then_inc(loaded, 16)

            def weights(e, b):
                if not (isinstance(e, int) and e < 2):
                    sp.wait_ge(w_low, e - 1)
                one = bass.ds(e if isinstance(e, int) else sp.snap(e), 1)
                sp.dma_start(raw[:, b, :], d["experts"][one].rearrange("o p k -> (o p) k")).then_inc(w_in[b], 16)

            def row(e, b):
                if not (isinstance(e, int) and e < 2):
                    sp.wait_ge(weighted, NCH * (e - 1))
                one = bass.ds(e if isinstance(e, int) else sp.snap(e), 1)
                sp.dma_start(wrow[:, b, :], scratch[one].to_broadcast([P, N])).then_inc(row_in[b], 16)

            for b in range(2):
                weights(b, b)
            sp.wait_ge(wgt_rows, 1)
            sp.dma_start(scratch.rearrange("e (t p) -> t e p", p=P), wgt_t[:, :]).then_inc(wgt_dram, 16)
            sp.wait_ge(wgt_dram, 16)
            for b in range(2):
                row(b, b)
            with sp.Fori(1, NE // 2) as i:
                for b in range(2):
                    weights(2 * i + b, b)
                    row(2 * i + b, b)
            out_t = out.rearrange("(t p) c -> p t c", p=P)
            for q in range(NCH):
                sp.wait_ge(total, q + 1)
                sp.dma_start(out_t[:, 4 * q:4 * q + 4, :], x_sb[:, 4 * q:4 * q + 4, :]).then_inc(stored, 16)
            sp.wait_ge(stored, 16 * NCH)

        @block.gpsimd
        def _(pool):
            pool.memset(acc[:, :], 0.0).then_inc(zeroed, 1)
            pool.wait_ge(zeroed, 1)
            pool.tensor_tensor(x_sb[:, :, :], x_sb[:, :, :], y[:, :, :], ALU.add).then_inc(x_ready, 1)

        @block.vector
        def _(dve):
            link = chain(dve, link_s)
            link(dve.memset(eps[:, :], RMS_EPS))
            moments(dve, link, ystat, stat)
            link(dve.tensor_tensor(stat[:, 2, :], stat[:, 0, :], stat[:, 0, :], ALU.mult))
            dve.scalar_tensor_tensor(stat[:, 3, :], stat[:, 2, :], float(C), stat[:, 1, :], ALU.mult, ALU.add).then_inc(sum_ready, 1)
            dve.wait_ge(std_ready, 1)
            link(dve.reciprocal(stat[:, 5, :], stat[:, 4, :]))
            for t in range(NT):
                dve.tensor_scalar(sq[:, t, :], y[:, t, :], stat[:, 5, t:t + 1], None, ALU.mult).then_inc(f_ready, 1)
            for q in range(4):
                cols = slice(512 * q, 512 * q + 512)
                dve.wait_ge(f_high, q + 1)
                dve.tensor_tensor(f_lo[:, cols], ft[:, cols], f_hi[:, cols].bitcast(F32), ALU.subtract).then_inc(f_split, 1)

            def split_low(e, b):
                dve.wait_ge(w_high, e + 1)
                dve.tensor_tensor(w_lo[:, b, :], raw[:, b, :], w_hi[:, b, :].bitcast(F32), ALU.subtract).then_inc(w_low, 1)

            split_low(0, 0)

            def routing():
                dve.wait_ge(r_ps, 1)
                link(dve.tensor_copy(r[:, 0, :, :], xps[:, 0, 0:NT * NE].rearrange("p (t e) -> p t e", e=NE)))
                link(dve.tensor_reduce(rs[:, 0, :], r[:, 0, :, :], AX.X, ALU.max))
                dve.tensor_tensor(r[:, 1, :, :], r[:, 0, :, :], bc(rs[:, 0, :], NE), ALU.subtract).then_inc(shifted, 1)
                dve.wait_ge(r_exp, 1)
                link(dve.tensor_reduce(rs[:, 1, :], r[:, 2, :, :], AX.X, ALU.add))
                link(dve.reciprocal(rs[:, 2, :], rs[:, 1, :]))
                link(dve.tensor_tensor(pr[:, :, :], r[:, 2, :, :], bc(rs[:, 2, :], NE), ALU.mult))
                marks = desc[:, :].rearrange("p (o e) -> p o e", o=1).to_broadcast([P, NT, NE])

                def first_largest(src, largest, mark, hot):
                    link(dve.tensor_reduce(rs[:, largest, :], src, AX.X, ALU.max))
                    link(dve.tensor_tensor(r[:, 0, :, :], src, bc(rs[:, largest, :], NE), ALU.is_ge))
                    link(dve.tensor_tensor(r[:, 1, :, :], r[:, 0, :, :], marks, ALU.mult))
                    link(dve.tensor_reduce(rs[:, mark, :], r[:, 1, :, :], AX.X, ALU.max))
                    link(dve.tensor_tensor(r[:, hot, :, :], r[:, 1, :, :], bc(rs[:, mark, :], NE), ALU.is_equal))

                first_largest(pr[:, :, :], 3, 4, 3)
                link(dve.scalar_tensor_tensor(r[:, 5, :, :], r[:, 3, :, :], -2.0, pr[:, :, :], ALU.mult, ALU.add))
                first_largest(r[:, 5, :, :], 5, 4, 4)
                link(dve.scalar_tensor_tensor(rs[:, 6, :], rs[:, 3, :], 1e-9, rs[:, 5, :], ALU.add, ALU.add))
                link(dve.reciprocal(rs[:, 7, :], rs[:, 6, :]))
                link(dve.tensor_tensor(r[:, 0, :, :], r[:, 3, :, :], r[:, 4, :, :], ALU.add))
                link(dve.tensor_tensor(r[:, 1, :, :], r[:, 0, :, :], pr[:, :, :], ALU.mult))
                dve.tensor_tensor(wgt[:, :, :], r[:, 1, :, :], bc(rs[:, 7, :], NE), ALU.mult).then_inc(wgt_ready, 1)

            def routing_rows():
                dve.wait_ge(wgt_ps, 1)
                dve.tensor_copy(wgt_t[:, :], xps[:, 1, 0:P]).then_inc(wgt_rows, 1)

            def combine(e, b, tc):
                n = NCH * e + tc
                cols = slice(TC * tc, TC * tc + TC)
                if tc == 0:
                    dve.wait_ge(row_in[b], 16 * (e // 2 + 1) if isinstance(e, int) else 8 * (e - b + 2))
                dve.wait_ge(o_ready, n + 1)
                if not (is_at(e, 0) and tc < 2):
                    dve.wait_ge(combined, n - 1)
                dve.tensor_tensor(part[:, tc % 2, :], ops[:, tc % 2, :], wrow[:, b, cols], ALU.mult).then_inc(weighted, 1)
                dve.wait_ge(weighted, n + 1)
                if not is_at(e, 0):
                    dve.wait_ge(combined, n - NCH + 1)
                dve.tensor_tensor(acc[:, cols], acc[:, cols], part[:, tc % 2, :], ALU.add).then_inc(combined, 1)

            def multiply(e, tc, k):
                u = (NCH * e + tc) * UN + k
                rows, s = HK[k][1], (tc * UN + k) % 2
                dve.wait_ge(gated, u + 1)
                if not (is_at(e, 0) and tc == 0 and k < 2):
                    dve.wait_ge(low, u - 1)
                dve.tensor_tensor(hid[0:rows, s, :], gate[0:rows, s, :], bps[0:rows, s, :], ALU.mult).then_inc(multiplied, 1)

            def split_hidden(e, tc, k):
                u = (NCH * e + tc) * UN + k
                rows, s = HK[k][1], (tc * UN + k) % 2
                dve.wait_ge(high, u + 1)
                dve.tensor_tensor(h_lo[0:rows, tc % 2, k, :], hid[0:rows, s, :], h_hi[0:rows, tc % 2, k, :].bitcast(F32),
                                  ALU.subtract).then_inc(low, 1)

            def body(e, b):
                for tc in range(NCH):
                    for k in range(UN):
                        multiply(e, tc, k)
                        if k:
                            split_hidden(e, tc, k - 1)
                        elif tc:
                            split_hidden(e, tc - 1, UN - 1)
                        elif not is_at(e, 0):
                            split_hidden(e - 1, NCH - 1, UN - 1)
                        if is_at(e, 0) and tc == 1 and k == 0:
                            routing_rows()
                    if is_at(e, 0) and tc == 0:
                        routing()
                        dve.wait_ge(zeroed, 1)
                    if tc:
                        combine(e, b, tc - 1)
                    elif not is_at(e, 0):
                        combine(e - 1, 1 - b, NCH - 1)
                    if tc == 1 and not is_at(e, NE - 1):
                        split_low(e + 1, 1 - b)
            pairs(dve, body)
            split_hidden(NE - 1, NCH - 1, UN - 1)
            combine(NE - 1, 1, NCH - 1)
            dve.wait_ge(x_ready, 1)
            for q in range(NCH):
                dve.wait_ge(acc_ps, q + 1)
                xq = x_sb[:, 4 * q:4 * q + 4, :].rearrange("p t c -> p (t c)")
                dve.tensor_tensor(xq, xq, xps[:, q % 2, :], ALU.add).then_inc(total, 1)

        @block.scalar
        def _(act):
            def split_high(e, b):
                act.wait_ge(w_in[b], 16 * (e // 2 + 1) if isinstance(e, int) else 8 * (e - b + 2))
                if not (isinstance(e, int) and e < 2):
                    act.wait_ge(o_ready, NCH * (e - 1))
                act.copy(w_hi[:, b, :], raw[:, b, :]).then_inc(w_high, 1)

            act.wait_ge(sum_ready, 1)
            act.activation(stat[:, 4, :], stat[:, 3, :], ACT.Sqrt, bias=eps[:, 0:1], scale=1.0 / C).then_inc(std_ready, 1)
            act.wait_ge(loaded, 48)
            for q in range(4):
                cols = slice(512 * q, 512 * q + 512)
                act.wait_ge(ft_ps, q + 1)
                act.activation(ft[:, cols], xps[:, q % 2, :], ACT.Copy, scale=ln2[:, 0:1]).then_inc(ft_ready, 1)
                act.wait_ge(ft_ready, q + 1)
                act.copy(f_hi[:, cols], ft[:, cols]).then_inc(f_high, 1)
            split_high(0, 0)

            def silu(e, tc, k):
                u = (NCH * e + tc) * UN + k
                rows, s = HK[k][1], (tc * UN + k) % 2
                act.wait_ge(ab_ready, u + 1)
                if not (is_at(e, 0) and tc == 0 and k < 2):
                    act.wait_ge(multiplied, u - 1)
                act.activation(gate[0:rows, s, :], aps[0:rows, s, :], ACT.Silu).then_inc(gated, 1)

            def round_hidden(e, tc, k):
                n = NCH * e + tc
                rows, s = HK[k][1], (tc * UN + k) % 2
                act.wait_ge(multiplied, n * UN + k + 1)
                if k == 0 and not (is_at(e, 0) and tc < 2):
                    act.wait_ge(o_ready, n - 1)
                act.copy(h_hi[0:rows, tc % 2, k, :], hid[0:rows, s, :]).then_inc(high, 1)

            def body(e, b):
                for tc in range(NCH):
                    for k in range(UN):
                        silu(e, tc, k)
                        if k:
                            round_hidden(e, tc, k - 1)
                        elif tc:
                            round_hidden(e, tc - 1, UN - 1)
                        elif not is_at(e, 0):
                            round_hidden(e - 1, NCH - 1, UN - 1)
                    if is_at(e, 0) and tc == 0:
                        act.wait_ge(shifted, 1)
                        act.activation(r[:, 2, :, :], r[:, 1, :, :], ACT.Exp).then_inc(r_exp, 1)
                    if tc == 1 and not is_at(e, NE - 1):
                        split_high(e + 1, 1 - b)
            pairs(act, body)
            round_hidden(NE - 1, NCH - 1, UN - 1)

        @block.tensor
        def _(pe):
            for q in range(4):
                pe.wait_ge(f_ready, 4 * q + 4)
                if q >= 2:
                    pe.wait_ge(ft_ready, q - 1)
                for k in range(4):
                    mm = pe.transpose(xps[:, q % 2, P * k:P * k + P], sq[:, 4 * q + k, :], ident[:, :])
                mm.then_inc(ft_ps, 1)
            pe.wait_ge(ft_ready, 4)
            pe.wait_ge(loaded, 48)
            for t in range(NT):
                mm = pe.matmul(xps[:, 0, NE * t:NE * t + NE], ft[:, P * t:P * t + P], rw[:, :], start=True, stop=True)
            mm.then_inc(r_ps, 1)

            def product(dst, terms):
                for i, (col, width, b, rows, hi, lo) in enumerate(terms):
                    for j, (w, x) in enumerate(((w_hi, hi), (w_hi, lo), (w_lo, hi))):
                        mm = pe.matmul(dst, w[0:rows, b, col:col + width], x, start=(i == 0 and j == 0),
                                       stop=(i == len(terms) - 1 and j == 2))
                return mm

            def hidden(e, b, tc, k):
                u = (NCH * e + tc) * UN + k
                (k0, rows), s = HK[k], (tc * UN + k) % 2
                cols = slice(TC * tc, TC * tc + TC)
                if not (is_at(e, 0) and tc == 0 and k < 2):
                    pe.wait_ge(multiplied, u - 1)
                product(aps[0:rows, s, :], [(W1 + k0, rows, b, P, f_hi[:, cols], f_lo[:, cols])])
                product(bps[0:rows, s, :], [(W3 + k0, rows, b, P, f_hi[:, cols], f_lo[:, cols])]).then_inc(ab_ready, 1)

            def output(e, b, tc):
                n = NCH * e + tc
                pe.wait_ge(low, UN * (n + 1))
                if not (is_at(e, 0) and tc < 2):
                    pe.wait_ge(weighted, n - 1)
                product(ops[:, tc % 2, :], [(W2 + C * k, C, b, rows, h_hi[0:rows, tc % 2, k, :], h_lo[0:rows, tc % 2, k, :])
                                            for k, (_, rows) in enumerate(HK)]).then_inc(o_ready, 1)

            def body(e, b):
                pe.wait_ge(w_low, e + 1)
                for tc in range(NCH):
                    if is_at(e, 0):
                        pe.wait_ge(f_split, tc + 1)
                    for k in range(UN):
                        hidden(e, b, tc, k)
                        if is_at(e, 0) and tc == 1 and k == 0:
                            pe.wait_ge(wgt_ready, 1)
                            pe.transpose(xps[:, 1, 0:P], wgt[:, :, :].rearrange("p t e -> p (t e)"), ident[:, :]).then_inc(wgt_ps, 1)
                    if tc:
                        output(e, b, tc - 1)
                    elif not is_at(e, 0):
                        output(e - 1, 1 - b, NCH - 1)
            pairs(pe, body)
            output(NE - 1, 1, NCH - 1)
            for q in range(NCH):
                pe.wait_ge(combined, NCH * (NE - 1) + q + 1)
                if q >= 2:
                    pe.wait_ge(total, q - 1)
                for k in range(4):
                    j = 4 * q + k
                    mm = pe.transpose(xps[:, q % 2, P * k:P * k + P], acc[:, P * j:P * j + P], ident[:, :])
                mm.then_inc(acc_ps, 1)


def program(nc, d, out, stop_after=None):
    with ExitStack() as ctx:
        m = Names(nc, ctx)
        x_sb = m.sb("x_sb", [P, NT, C])
        ident = m.sb("ident_sb", [P, P])
        gstat = m.sb("gstat", [P, NT, 6])
        with ExitStack() as gctx:
            g = Names(nc, gctx)
            values = g.sb("g_values", [P, NT, H, HW])
            er08 = g.sb("g_er08", [P, N])
            cj = g.sb("g_cj", [FR, N])
            ci = g.sb("g_ci", [FR, GROUPS])
            el08 = g.sb("g_el08", [P, GROUPS])
            feat = g.sb("g_feat", [P, 2, N])
            wlog = g.sb("g_wlog", [P, P])
            mask = g.sb("g_mask", [P, 2, N])
            args = (nc, d, x_sb, values, er08, cj, ci, el08, feat, wlog, ident, mask)
            graph_setup(*args)
            graph_attention(*args, gstat)
        if stop_after == "graph":
            done = m.sem("dbg")
            block = ctx.enter_context(nc.Block())

            @block.sync
            def _(sp):
                sp.dma_start(out.rearrange("(t p) c -> p t c", p=P), x_sb[:, :, :]).then_inc(done, 16)
                sp.wait_ge(done, 16)
            return
        y = m.sb("y_sb", [P, NT, C])
        ystat = m.sb("ystat", [P, NT, 6])
        with ExitStack() as actx:
            a = Names(nc, actx)
            u_sb = a.sb("u_sb", [P, NKV, N])
            with ExitStack() as qctx:
                q = Names(nc, qctx)
                qs = q.sb("q_stack", [3 * HD + 1, NH, N], F32R)
                ks = q.sb("k_stack", [3 * HD + 1, NKV, N], F32R)
                vx = q.sb("v_values", [P, NT, NKV, VW])
                identb = q.sb("identb", [P, P], BF16)
                cutb = q.sb("cutb", [P, 2, TC], BF16)
                k_in = [q.sem(f"k_in{c}") for c in range(2)]
                q_in = [q.sem(f"q_in{c}") for c in range(2)]
                shared = (identb, cutb, k_in, q_in)
                block_input(nc, d, x_sb, y, ident, gstat, qs, ks, vx, *shared)
                causal_attention(nc, d, qs, ks, vx, ident, u_sb, *shared)
            project(nc, d, y, u_sb, ystat)
        experts(nc, d, out, x_sb, y, ident, ystat)


def lay_out(x, adj, L0_gnn_positions, L0_gnn_curv_feats, L0_gnn_W, L0_gnn_a_l, L0_gnn_a_r, L0_gnn_Wc, L0_gnn_gate,
            L0_ffn_ln1_w, L0_ffn_ln2_w, L0_ffn_wq, L0_ffn_wk, L0_ffn_wv, L0_ffn_wo, L0_ffn_router_w, L0_ffn_w1,
            L0_ffn_w2, L0_ffn_w3):
    a = np.asarray
    curv = a(L0_gnn_curv_feats)
    wc = a(L0_gnn_Wc)
    curvw = np.ones((P, P), np.float32)
    curvw[:FR] = np.tile(wc.T, (GI, GI))
    curvw[CJ_ROW:PAD_ROW] = np.tile(wc.T, (1, GI))
    arrays = {
        "x": a(x), "adj": a(adj),
        "WT": a(L0_gnn_W).T,
        "a_rl": np.stack([a(L0_gnn_a_r).reshape(-1), a(L0_gnn_a_l).reshape(-1)], 1),
        "curvw": curvw, "curvT": curv.T, "curv_i": curv.reshape(GROUPS, FR).T,
        "gate": a(L0_gnn_gate).reshape(1, 1),
        "ln1": a(L0_ffn_ln1_w).reshape(C, 1), "ln2": a(L0_ffn_ln2_w).reshape(C, 1),
        "wvT": a(L0_ffn_wv).T, "routerT": a(L0_ffn_router_w).T,
    }
    w2t = np.zeros((NE, len(HK) * P, C), np.float32)
    w2t[:, :HID] = a(L0_ffn_w2).transpose(0, 2, 1)
    w2t = w2t.reshape(NE, len(HK), P, C).transpose(0, 2, 1, 3).reshape(NE, P, len(HK) * C)
    arrays["experts"] = np.concatenate([a(L0_ffn_w1).transpose(0, 2, 1), a(L0_ffn_w3).transpose(0, 2, 1), w2t], 2)
    for name, w in (("wqT", a(L0_ffn_wq)), ("wkT", a(L0_ffn_wk))):
        partner = w.reshape(-1, 2, HD // 2, C)[:, ::-1].reshape(w.shape)
        arrays[name] = np.stack([w.T, partner.T])
    wo = np.zeros((P, 2, 256), np.float32)
    for h in range(NH):
        r = VW * (h % 2)
        wo[r:r + HD, h // 2, 0:C] = a(L0_ffn_wo)[:, HD * h:HD * h + HD].T
        wo[r + HD, h // 2, C] = 1.0
    arrays["woX"] = wo
    arrays.update(constants())
    return {k: np.ascontiguousarray(v) for k, v in arrays.items()}


def kernel(**inputs):
    import concourse.bacc as bacc
    from concourse.bass_utils import run_bass_kernel_spmd

    nc = bacc.Bacc("TRN2", target_bir_lowering=False, num_devices=1)
    arrays = lay_out(**inputs)
    aps = {name: nc.dram_tensor(f"in_{name}", a.shape, mybir.dt.from_np(a.dtype), kind="ExternalInput").ap()
           for name, a in arrays.items()}
    out = nc.dram_tensor("out", (N, C), F32, kind="ExternalOutput").ap()
    program(nc, aps, out)
    r = run_bass_kernel_spmd(nc, [{f"in_{name}": a for name, a in arrays.items()}], core_ids=[0])
    return r.results[0]["out"]
```

```python
from contextlib import ExitStack

import numpy as np

import concourse.bass as bass
from concourse import mybir

F32 = mybir.dt.float32
F32R = mybir.dt.float32r
BF16 = mybir.dt.bfloat16
I32 = mybir.dt.int32
ALU = mybir.AluOpType
ACT = mybir.ActivationFunctionType
AX = mybir.AxisListType

P = 128
N = 2048
C = 128
NT = N // P
H, D, CF = 8, 16, 6
GI = P // H
GROUPS = N // GI
GPT = P // GI
FR = GI * CF
ER_ROW, CJ_ROW, PAD_ROW, MASK_ROW = FR, FR + H, FR + H + CF, P - GI
HALF = N // 2
LSLOTS = 4
HV = D + 1
HW = 32
AVG = 4
AVN = AVG * GI
TBANK = [0, 1, 2, 1]
MASKED = 1e9
SLOPE = 0.2
LN_EPS = 1e-5
RMS_EPS = 1e-6

NH, NKV, HD = 4, 2, 32
NREP = NH // NKV
ROPE_BASE = 10000.0
VW = 64
TC = 512
CUT = 1e30
SLACK = 6
NE, HID = 8, 341
WCOLS = 2 * HID + 3 * C
HK = [(0, 128), (128, 128), (256, HID - 256)]


def constants():
    p = np.arange(P)
    c = {}
    c["ident"] = np.eye(P, dtype=np.float32)
    coef = np.zeros((P, P), np.float32)
    i_of, h_of = p // H, p % H
    for r in range(FR):
        coef[r] = 2.0 * (i_of == r // CF)
    for r in range(H):
        coef[ER_ROW + r] = SLOPE / (1 - SLOPE) * (h_of == r)
    coef[CJ_ROW:PAD_ROW] = -1.0
    for r in range(GI):
        coef[MASK_ROW + r] = MASKED * (i_of == r)
    c["coef"] = coef
    gated = np.zeros((P, 2), np.float32)
    gated[:FR, 0] = 1
    gated[CJ_ROW:PAD_ROW, 0] = 1
    gated[:, 1] = 1 - gated[:, 0]
    c["gated"] = gated
    c["headsel"] = (p[:, None] // D == h_of[None, :]).astype(np.float32)
    c["nodesel"] = ((1 - SLOPE) * (i_of[:, None] == np.arange(GI)[None, :])).astype(np.float32)
    inv = 1.0 / ROPE_BASE ** (np.arange(0, HD, 2, dtype=np.float32) / HD)
    freqs = np.outer(np.arange(N, dtype=np.float32), inv)
    emb = np.concatenate([freqs, freqs], axis=-1)
    sign = np.where(np.arange(HD) < HD // 2, -1.0, 1.0).astype(np.float32)
    c["cosT"] = np.tile(np.cos(emb).T, (NH, 1))
    c["sinT"] = np.tile((np.sin(emb) * sign).T, (NH, 1))
    rows = NKV * HD
    for name in ("cos", "sin"):
        t = c[name + "T"][:rows].reshape(rows, 2, 2, TC)
        c[name + "K"] = t.transpose(2, 0, 1, 3).reshape(P, 2, TC)
    c["causal_ts"] = np.where(p[None, :] > p[:, None], -CUT, 0.0).astype(np.float32)
    c["causal_st"] = c["causal_ts"].T
    c["descend"] = np.tile(np.arange(NE, 0, -1, dtype=np.float32), (P, 1))
    return c


class Names:

    def __init__(self, nc, ctx):
        self.nc, self.ctx = nc, ctx

    def sb(self, name, shape, dt=F32):
        return self.ctx.enter_context(self.nc.sbuf_tensor(name, shape, dt))

    def ps(self, name, shape, dt=F32):
        return self.ctx.enter_context(self.nc.psum_tensor(name, shape, dt))

    def sem(self, name):
        return self.ctx.enter_context(self.nc.semaphore(name))


def chain(engine, semaphore, start=0):
    count = [start]

    def link(instruction):
        instruction.then_inc(semaphore, 1)
        count[0] += 1
        engine.wait_ge(semaphore, count[0])
    return link


def bc(ap, n):
    return ap.rearrange("p (a o) -> p a o", o=1).to_broadcast([ap.shape[0], ap.shape[1], n])


def moments(dve, link, st, out):
    even, odd = st[:, :, 1], st[:, :, 4]
    link(dve.tensor_tensor(out[:, 0, :], even, odd, ALU.add))
    link(dve.tensor_tensor(out[:, 1, :], even, odd, ALU.subtract))
    link(dve.tensor_tensor(out[:, 2, :], out[:, 1, :], out[:, 1, :], ALU.mult))
    link(dve.tensor_tensor(out[:, 3, :], st[:, :, 2], st[:, :, 5], ALU.add))
    link(dve.scalar_tensor_tensor(out[:, 1, :], out[:, 2, :], C / 4.0, out[:, 3, :], ALU.mult, ALU.add))
    link(dve.tensor_scalar(out[:, 0, :], out[:, 0, :], 0.5, None, ALU.mult))


def graph_setup(nc, d, x_sb, values, er08, cj, ci, el08, feat, wlog, ident, mask):
    with ExitStack() as ctx:
        m = Names(nc, ctx)
        st = m.sb("gs_st", [P, NT, 6])
        sq = m.sb("gs_sq", [P, NT, C])
        stat = m.sb("gs_stat", [P, 6, NT])
        xt = m.sb("gs_xt", [P, N])
        el_tmp = m.sb("gs_el_tmp", [P, N])
        ht = m.sb("gs_ht", [P, N])
        wt = m.sb("gs_wt", [P, C])
        arl = m.sb("gs_arl", [P, 2])
        hsel = m.sb("gs_hsel", [P, P])
        ar = m.sb("gs_ar", [P, 2, P])
        nsel = m.sb("gs_nsel", [P, GI])
        val = m.sb("gs_val", [P, P])
        coef = m.sb("gs_coef", [P, P])
        gated = m.sb("gs_gated", [P, 2])
        gate = m.sb("gs_gate", [P, 1])
        eps = m.sb("gs_eps", [P, 1])
        ps = m.ps("gs_ps", [P, 8, 512])
        by_head = values[:, :, 0:HV * H].rearrange("p t (h e) -> p t h e", e=HV)
        loaded_x, loaded = [m.sem(f"gs_loaded_x{q}") for q in range(4)], m.sem("gs_loaded")
        first_in, cj_in = m.sem("gs_first_in"), m.sem("gs_cj_in")
        adj_in, stats_done, mask_done = m.sem("gs_adj_in"), m.sem("gs_stats_done"), m.sem("gs_mask_done")
        fixed = m.sem("gs_fixed")
        var_ready, std_ready = m.sem("gs_var"), m.sem("gs_std")
        xn_ready, xt_ps, xt_ready = m.sem("gs_xn"), m.sem("gs_xt_ps"), m.sem("gs_xt_s")
        h_ps, h_ready, v_ps, v_done = m.sem("gs_h_ps"), m.sem("gs_h_s"), m.sem("gs_v_ps"), m.sem("gs_v_s")
        ar_ready, e_ps, er_done, el_mul, el_done = m.sem("gs_ar_s"), m.sem("gs_e_ps"), m.sem("gs_er_s"), m.sem("gs_elm"), m.sem("gs_el_s")
        spread, link_s = m.sem("gs_spread"), m.sem("gs_link")
        zeroed = m.sem("gs_zeroed")
        block = ctx.enter_context(nc.Block())

        @block.sync
        def _(sp):
            for q in range(4):
                sp.dma_start(x_sb[:, 4 * q:4 * q + 4, :],
                             d["x"].rearrange("(t p) c -> p t c", p=P)[:, 4 * q:4 * q + 4, :]).then_inc(loaded_x[q], 16)
            for dst, name in ((ident, "ident"), (wt, "WT")):
                sp.dma_start(dst[:, :], d[name]).then_inc(first_in, 16)
            for dst, name in ((arl, "a_rl"), (hsel, "headsel"), (nsel, "nodesel"),
                              (val, "curvw"), (coef, "coef"), (gated, "gated"), (ci, "curv_i")):
                sp.dma_start(dst[:, :], d[name]).then_inc(loaded, 16)
            sp.dma_start(gate[:, :], d["gate"].to_broadcast([P, 1])).then_inc(loaded, 16)
            for i in range(GI):
                sp.dma_start(cj[CF * i:CF * i + CF, :], d["curvT"]).then_inc(cj_in, 16)
            sp.dma_start(mask[:, 0, :].bitcast(I32), d["adj"].rearrange("(t p) j -> t p j", p=P)[0]).then_inc(adj_in, 16)
            sp.wait_ge(zeroed, 1)
            for b in range(2):
                sp.dma_start(feat[CJ_ROW:PAD_ROW, b, :], d["curvT"]).then_inc(spread, 16)
            sp.wait_ge(er_done, 4)
            for b in range(2):
                sp.dma_start(feat[ER_ROW:CJ_ROW, b, :], er08[0:H, :]).then_inc(spread, 16)
            sp.wait_ge(spread, 64)
            sp.wait_ge(cj_in, 16 * GI)

        @block.gpsimd
        def _(pool):
            pool.memset(feat[96:P, :, :], 0.0).then_inc(zeroed, 1)
            pool.wait_ge(zeroed, 1)
            pool.memset(values[:, :, :], 0.0).then_inc(zeroed, 1)
            pool.wait_ge(zeroed, 2)
            pool.memset(by_head[:, :, :, D:D + 1], 1.0).then_inc(zeroed, 1)

        @block.vector
        def _(dve):
            link = chain(dve, link_s)
            dve.memset(eps[:, :], LN_EPS).then_inc(fixed, 1)
            for t in range(NT):
                if t % 4 == 0:
                    dve.wait_ge(loaded_x[t // 4], 16)
                dve.bn_stats(st[:, t, :], x_sb[:, t, :]).then_inc(stats_done, 1)
            dve.wait_ge(stats_done, NT)
            moments(dve, link, st, stat)
            dve.sem_inc(var_ready, 1)
            dve.wait_ge(std_ready, 1)
            link(dve.reciprocal(stat[:, 5, :], stat[:, 4, :]))
            for t in range(NT):
                dve.tensor_scalar(sq[:, t, :], x_sb[:, t, :], stat[:, 0, t:t + 1], stat[:, 5, t:t + 1], ALU.subtract,
                                  ALU.mult).then_inc(xn_ready, 1)
            for q in range(4):
                dve.wait_ge(xt_ps, q + 1)
                dve.tensor_copy(xt[:, 512 * q:512 * q + 512], ps[:, q, :]).then_inc(xt_ready, 1)
            dve.wait_ge(loaded, 16 * 8)
            for n in range(2):
                dve.tensor_scalar(ar[:, n, :], hsel[:, :], arl[:, n:n + 1], None, ALU.mult).then_inc(ar_ready, 1)
            link(dve.tensor_scalar(gated[:, 0:1], gated[:, 0:1], gate[:, 0:1], None, ALU.mult))
            link(dve.tensor_tensor(gate[:, :], gated[:, 0:1], gated[:, 1:2], ALU.add))
            link(dve.scalar_tensor_tensor(wlog[:, :], val[:, :], gate[:, 0:1], coef[:, :], ALU.mult, ALU.mult))
            for q in range(4):
                dve.wait_ge(h_ps, q + 1)
                dve.tensor_copy(ht[:, 512 * q:512 * q + 512], ps[:, 4 + q, :]).then_inc(h_ready, 1)
            el_cols = el_tmp[:, :].rearrange("p (g i) -> p g i", i=GI)
            dve.wait_ge(e_ps, 4)
            dve.tensor_tensor(el_cols, ps[:, 0:4, :].rearrange("p q (g i) -> p (q g) i", i=GI),
                              nsel[:, :].rearrange("p (o i) -> p o i", o=1).to_broadcast([P, GROUPS, GI]),
                              ALU.mult).then_inc(el_mul, 1)
            dve.wait_ge(el_mul, 1)
            dve.tensor_reduce(el08[:, :], el_cols, AX.X, ALU.add).then_inc(el_done, 1)
            dve.wait_ge(adj_in, 16)
            dve.tensor_scalar(mask[:, 0, :], mask[:, 0, :].bitcast(I32), 0.0, 1.0, ALU.is_gt, ALU.subtract).then_inc(mask_done, 1)
            dve.wait_ge(zeroed, 3)
            for q in range(4):
                dve.wait_ge(v_ps, q + 1)
                dve.tensor_copy(by_head[:, 4 * q:4 * q + 4, :, 0:D],
                                ps[:, q, :].rearrange("p (t h e) -> p t h e", t=4, h=H)).then_inc(v_done, 1)

        @block.scalar
        def _(act):
            act.wait_ge(fixed, 1)
            act.wait_ge(var_ready, 1)
            act.activation(stat[:, 4, :], stat[:, 1, :], ACT.Sqrt, bias=eps[:, 0:1], scale=1.0 / C).then_inc(std_ready, 1)
            for q in range(4):
                act.wait_ge(e_ps, 4 + q + 1)
                act.mul(er08[:, 512 * q:512 * q + 512], ps[:, 4 + q, :], 1 - SLOPE).then_inc(er_done, 1)

        @block.tensor
        def _(pe):
            pe.wait_ge(first_in, 32)
            for q in range(4):
                pe.wait_ge(xn_ready, 4 * q + 4)
                for k in range(4):
                    mm = pe.transpose(ps[:, q, P * k:P * k + P], sq[:, 4 * q + k, :], ident[:, :])
                mm.then_inc(xt_ps, 1)
            for q in range(4):
                pe.wait_ge(xt_ready, q + 1)
                pe.matmul(ps[:, 4 + q, :], wt[:, :], xt[:, 512 * q:512 * q + 512], start=True, stop=True).then_inc(h_ps, 1)
            pe.wait_ge(ar_ready, 2)
            for n in (1, 0):
                for q in range(4):
                    if n:
                        pe.wait_ge(h_ready, q + 1)
                    bank = q if n else 4 + q
                    pe.matmul(ps[:, bank, :], ar[:, n, :], ht[:, 512 * q:512 * q + 512], start=True, stop=True).then_inc(e_ps, 1)
            pe.wait_ge(el_mul, 1)
            for q in range(4):
                for k in range(4):
                    t = 4 * q + k
                    mm = pe.matmul(ps[:, q, P * k:P * k + P], xt[:, P * t:P * t + P], wt[:, :], start=True, stop=True)
                mm.then_inc(v_ps, 1)


def graph_attention(nc, d, x_sb, values, er08, cj, ci, el08, feat, wlog, ident, mask, gstat):
    AHEAD = 2
    PARTS = [range(3 * k, 3 * k + 3) for k in range(4)] + [range(12, NT)]
    LEAST = [2, 3, 4, 5]
    SPLIT = range(AHEAD + 1, AHEAD + len(PARTS))
    with ExitStack() as ctx:
        m = Names(nc, ctx)
        logits = m.sb("ga_logits", [P, LSLOTS, N])
        probs_t = m.sb("ga_probs_t", [P, 3, NT, H, AVN])
        av_sb = m.sb("ga_av", [P, 2, P])
        mx = m.sb("ga_mx", [P, 4, LSLOTS])
        rden = m.sb("ga_rden", [P, H])
        gout = m.sb("ga_gout", [P, C])
        w_hi, w_lo = m.sb("ga_w_hi", [P, P], F32R), m.sb("ga_w_lo", [P, P], F32R)
        f_hi, f_lo = m.sb("ga_f_hi", [P, HALF], F32R), m.sb("ga_f_lo", [P, HALF], F32R)
        lps = m.ps("ga_lps", [P, 4, 512])
        tps = m.ps("ga_tps", [P, 3, 512])
        avp = m.ps("ga_avp", [P, 512])
        adj_in = m.sem("ga_adj_in")
        adj_seen = m.sem("ga_adj_seen")
        mask_ready = m.sem("ga_mask_ready")
        mask_in = [m.sem(f"ga_mask_in{b}") for b in range(2)]
        w_split = m.sem("ga_w_split")
        f_high = m.sem("ga_f_high")
        f_low = m.sem("ga_f_low")
        feat_ready = m.sem("ga_feat_ready")
        logit_half = m.sem("ga_logit_half")
        half_seen = m.sem("ga_half_seen")
        relu_ready = m.sem("ga_relu_ready")
        max_half = m.sem("ga_max_half")
        keep_ready = m.sem("ga_keep_ready")
        shift_ready = m.sem("ga_shift_ready")
        probs_ready = m.sem("ga_probs_ready")
        turned = m.sem("ga_turned")
        act_moved = m.sem("ga_act_moved")
        dve_moved = m.sem("ga_dve_moved")
        av_part = m.sem("ga_av_part")
        av_moved = m.sem("ga_av_moved")
        out_turned = m.sem("ga_out_turned")
        rden_ready = m.sem("ga_rden_ready")
        scaled = m.sem("ga_scaled")
        out_done = m.sem("ga_out_done")
        stats_done = m.sem("ga_stats_done")
        block = ctx.enter_context(nc.Block())
        av_view = avp[:, 0:2 * P].rearrange("p (q s i) -> p q s i", q=2, s=2)
        out_view = avp[:, 2 * P:4 * P].rearrange("p (h e) -> p h e", e=HW)

        def tiles(engine, body):
            body(0, False, True, False)
            with engine.Fori(0, NT // 2 - 1) as pair:
                body(engine.snap(2 * pair + 1), True, True, True)
                body(engine.snap(2 * pair + 2), False, True, True)
            body(NT - 1, True, False, True)

        def moved(odd, g, q):
            dst = probs_t[:, 1 if g >= AVG else 2 * odd, 4 * q:4 * q + 4, :, GI * (g % AVG):GI * (g % AVG) + GI]
            src = tps[:, TBANK[q], :].rearrange("p (k i h) -> p k h i", k=4, h=H)
            return dst, src

        @block.sync
        def _(sp):
            adj_rows = d["adj"].rearrange("(t p) j -> t p j", p=P)

            def mask_rows(t, odd, g):
                if not (isinstance(t, int) and t == 0 and g < 2):
                    sp.wait_ge(logit_half, 2 * (t * GPT + g - 1))
                sp.dma_start(feat[MASK_ROW:P, g % 2, :], mask[GI * g:GI * g + GI, odd, :]).then_inc(mask_in[g % 2], 16)

            def tile_of_rows(t, odd, ahead, earlier):
                if earlier:
                    sp.wait_ge(mask_ready, t)
                for g in range(GPT):
                    mask_rows(t, odd, g)
                    if g == 1 and ahead:
                        nxt = t + 1 if isinstance(t, int) else sp.snap(t + 1)
                        sp.dma_start(mask[:, 1 - odd, :].bitcast(I32),
                                     adj_rows[bass.ds(nxt, 1)].rearrange("o p j -> (o p) j")).then_inc(adj_in, 16)
            tiles(sp, tile_of_rows)

        @block.gpsimd
        def _(pool):
            def body(t, odd, ahead, earlier):
                if ahead:
                    pool.wait_ge(adj_in, 16 * (t + 1))
                    pool.sem_inc(adj_seen, 1)
                    pool.tensor_scalar(mask[:, 1 - odd, :], mask[:, 1 - odd, :].bitcast(I32), 0.0, 1.0, ALU.is_gt,
                                       ALU.subtract).then_inc(mask_ready, 1)
                if earlier:
                    add(t - 1)

            def add(t):
                xt = x_sb[:, bass.ds(t, 1), :].rearrange("p o c -> p (o c)")
                pool.wait_ge(scaled, t + 1)
                pool.tensor_tensor(xt, xt, gout[:, :], ALU.add).then_inc(out_done, 1)
            tiles(pool, body)
            add(NT - 1)

        @block.vector
        def _(dve):
            def features(t, g):
                first = isinstance(t, int) and t == 0
                if not (first and g < 2):
                    dve.wait_ge(logit_half, 2 * (t * GPT + g - 1))
                col = t * GPT + g
                dve.tensor_scalar(feat[0:FR, g % 2, :], cj[:, :], ci[0:FR, bass.ds(col, 1)], 0.0,
                                  ALU.subtract, ALU.max).then_inc(feat_ready, 1)

            def low_part(t, g):
                dve.wait_ge(f_high, len(SPLIT) * t + g - SPLIT[0] + 1)
                dve.sem_inc(half_seen, 1)
                dve.tensor_tensor(f_lo[:, :], feat[:, g % 2, HALF:N], f_hi[:, :].bitcast(F32), ALU.subtract).then_inc(f_low, 1)

            def add_half(t, g, half):
                s = g % LSLOTS
                if half == 0:
                    dve.wait_ge(relu_ready, t * GPT + g + 1)
                else:
                    dve.wait_ge(max_half, 2 * (t * GPT + g) + 1)
                dve.wait_ge(logit_half, 2 * (t * GPT + g) + half + 1)
                dve.sem_inc(half_seen, 1)
                part = logits[:, s, HALF * half:HALF * half + HALF]
                dve.tensor_tensor_reduce(part, lps[:, 2 * half:2 * half + 2, :].rearrange("p q n -> p (q n)"), part, 1.0,
                                         -3e38 if half == 0 else mx[:, 0, s:s + 1], ALU.add, ALU.max,
                                         mx[:, half, s:s + 1]).then_inc(max_half, 1)

            def shift(t, g):
                s = g % LSLOTS
                dve.wait_ge(max_half, 2 * (t * GPT + g) + 2)
                dve.tensor_scalar(mx[:, 2, s:s + 1], mx[:, 1, s:s + 1], -0.5 * MASKED, None, ALU.is_gt).then_inc(keep_ready, 1)
                dve.wait_ge(keep_ready, t * GPT + g + 1)
                dve.scalar_tensor_tensor(mx[:, 3, s:s + 1], mx[:, 1, s:s + 1], -1.0, mx[:, 2, s:s + 1],
                                         ALU.mult, ALU.mult).then_inc(shift_ready, 1)

            def move(t, odd, g, q):
                dve.wait_ge(turned, 4 * (t * GPT + g) + q + 1)
                if not (isinstance(t, int) and t == 0) and g == AVG:
                    dve.wait_ge(av_part, len(PARTS) * (t - 1) + LEAST[q])
                dve.tensor_copy(*moved(odd, g, q)).then_inc(dve_moved, 1)

            def output(t):
                dve.wait_ge(out_turned, t + 1)
                dve.reciprocal(rden[:, :], out_view[:, :, D]).then_inc(rden_ready, 1)
                dve.wait_ge(rden_ready, t + 1)
                dve.tensor_tensor(gout[:, :].rearrange("p (h e) -> p h e", e=D), out_view[:, :, 0:D], bc(rden[:, :], D),
                                  ALU.mult).then_inc(scaled, 1)

            features(0, 0)
            features(0, 1)
            dve.wait_ge(w_split, 1)
            dve.tensor_tensor(w_lo[:, :], wlog[:, :], w_hi[:, :].bitcast(F32), ALU.subtract).then_inc(w_split, 1)
            for g in range(AHEAD):
                add_half(0, g, 0)
                add_half(0, g, 1)
                shift(0, g)
                if g == 0:
                    features(0, 2)

            def body(t, odd, ahead, earlier):
                for g in range(GPT):
                    if g == AVG + 2 and earlier:
                        output(t - 1)
                    if g == GPT - 1 and earlier:
                        dve.wait_ge(out_done, t)
                    u, v = divmod(g + AHEAD + 1, GPT)
                    if u == 0 or ahead:
                        features(t + u, v)
                    u, v = divmod(g + AHEAD, GPT)
                    if u == 0 or ahead:
                        add_half(t + u, v, 0)
                    move(t, odd, g, 1)
                    if u == 0 or ahead:
                        add_half(t + u, v, 1)
                        shift(t + u, v)
                    move(t, odd, g, 3)
                    u, v = divmod(g + AHEAD + 1, GPT)
                    if v in SPLIT and (u == 0 or ahead):
                        low_part(t + u, v)
            tiles(dve, body)
            for t in range(NT):
                if t == NT - 1:
                    output(t)
                dve.wait_ge(out_done, t + 1)
                dve.bn_stats(gstat[:, t, :], x_sb[:, t, :]).then_inc(stats_done, 1)

        @block.scalar
        def _(act):
            def relu_part(t, g):
                if not (isinstance(t, int) and t == 0 and g < LSLOTS):
                    act.wait_ge(turned, 4 * (t * GPT + g - LSLOTS + 1))
                act.activation(logits[:, g % LSLOTS, :], er08[:, :], ACT.Relu,
                               bias=el08[:, bass.ds(t * GPT + g, 1)]).then_inc(relu_ready, 1)

            def high_part(t, g):
                act.wait_ge(feat_ready, t * GPT + g + 1)
                act.wait_ge(mask_in[g % 2], 16 * (t * (GPT // 2) + g // 2 + 1))
                act.wait_ge(logit_half, 2 * (t * GPT + g))
                act.copy(f_hi[:, :], feat[:, g % 2, HALF:N]).then_inc(f_high, 1)

            def exponent(t, g):
                s = g % LSLOTS
                act.wait_ge(shift_ready, t * GPT + g + 1)
                act.activation(logits[:, s, :], logits[:, s, :], ACT.Exp, bias=mx[:, 3, s:s + 1],
                               scale=mx[:, 2, s:s + 1]).then_inc(probs_ready, 1)

            def move(t, odd, g, q):
                act.wait_ge(turned, 4 * (t * GPT + g) + q + 1)
                if not (isinstance(t, int) and t == 0) and g == AVG:
                    act.wait_ge(av_part, len(PARTS) * (t - 1) + LEAST[q])
                act.copy(*moved(odd, g, q)).then_inc(act_moved, 1)

            def move_av(parts, swapped):
                act.wait_ge(av_part, parts)
                for b in range(2):
                    half = 1 - b if swapped else b
                    act.copy(av_sb[:, :, AVN * half:AVN * half + AVN], av_view[:, :, b, :]).then_inc(av_moved, 1)

            act.copy(w_hi[:, :], wlog[:, :]).then_inc(w_split, 1)
            for g in range(AHEAD + 1):
                relu_part(0, g)
            exponent(0, 0)

            def body(t, odd, ahead, earlier):
                for g in range(GPT):
                    if g == AVG + 1 and earlier:
                        move_av(len(PARTS) * t, not odd)
                    if g == GPT - 1 and earlier:
                        act.wait_ge(out_turned, t)
                    u, v = divmod(g + 1, GPT)
                    if u == 0 or ahead:
                        exponent(t + u, v)
                    move(t, odd, g, 0)
                    u, v = divmod(g + AHEAD + 1, GPT)
                    if u == 0 or ahead:
                        relu_part(t + u, v)
                    move(t, odd, g, 2)
                    if v in SPLIT and (u == 0 or ahead):
                        high_part(t + u, v)
            tiles(act, body)
            move_av(len(PARTS) * (NT - 1) + 1, False)

        @block.tensor
        def _(pe):
            def product(t, g, half):
                if half == 0:
                    pe.wait_ge(feat_ready, t * GPT + g + 1)
                    pe.wait_ge(mask_in[g % 2], 16 * (t * (GPT // 2) + g // 2 + 1))
                if not (isinstance(t, int) and t == 0 and g == 0):
                    pe.wait_ge(max_half, 2 * (t * GPT + g - 1) + half + 1)
                if half == 1 and g in SPLIT:
                    pe.wait_ge(f_low, len(SPLIT) * t + g - SPLIT[0] + 1)
                for q in (2 * half, 2 * half + 1):
                    cols = slice(512 * q, 512 * q + 512)
                    if half == 1 and g in SPLIT:
                        part = slice(512 * (q - 2), 512 * (q - 2) + 512)
                        hi, lo = f_hi[:, part], f_lo[:, part]
                        for i, (w, f) in enumerate(((w_hi, hi), (w_hi, lo), (w_lo, hi))):
                            mm = pe.matmul(lps[:, q, :], w[:, :], f, start=(i == 0), stop=(i == 2))
                    else:
                        mm = pe.matmul(lps[:, q, :], wlog[:, :], feat[:, g % 2, cols], start=True, stop=True)
                mm.then_inc(logit_half, 1)

            def turn(t, g, q):
                if q == 0:
                    pe.wait_ge(probs_ready, t * GPT + g + 1)
                first = isinstance(t, int) and t == 0 and g == 0
                n = t * GPT + g
                if q == 3:
                    pe.wait_ge(dve_moved, 2 * n + 1)
                elif q == 1:
                    if not first:
                        pe.wait_ge(dve_moved, 2 * n)
                elif not first:
                    pe.wait_ge(act_moved, 2 * n - (1 if q == 0 else 0))
                for k in range(4):
                    j = 4 * q + k
                    mm = pe.transpose(tps[:, TBANK[q], P * k:P * k + P], logits[:, g % LSLOTS, P * j:P * j + P], ident[:, :])
                mm.then_inc(turned, 1)

            def value_product(t, odd, k):
                if k == 0:
                    pe.wait_ge(act_moved, 2 * GPT * (t + 1))
                    pe.wait_ge(dve_moved, 2 * GPT * (t + 1))
                for j in PARTS[k]:
                    for h in range(H):
                        r = HW * (h % 4)
                        mm = pe.matmul(avp[r:r + HW, P * (h // 4):P * (h // 4) + P],
                                       values[:, j, HV * h:HV * h + HW], probs_t[:, odd:odd + 2, j, h, :],
                                       start=(j == 0 and h < 4), stop=(j == NT - 1), skip_group_check=True)
                mm.then_inc(av_part, 1)

            def half_product(b, js):
                if js[0] == 0:
                    pe.wait_ge(act_moved, 2 * (GROUPS - GPT + AVG * (b + 1)))
                    pe.wait_ge(dve_moved, 2 * (GROUPS - GPT + AVG * (b + 1)))
                for j in js:
                    for h in range(H):
                        r, col = HW * (h % 4), P * (h // 4) + AVN * b
                        mm = pe.matmul(avp[r:r + HW, col:col + AVN], values[:, j, HV * h:HV * h + HW], probs_t[:, 2 - b, j, h, :],
                                       start=(b == 0 and j == 0 and h < 4), stop=(j == NT - 1), skip_group_check=True)
                return mm

            def turn_out(t):
                pe.wait_ge(av_moved, 2 * t + 2)
                for q in range(2):
                    mm = pe.transpose(avp[:, P * (2 + q):P * (2 + q) + P], av_sb[:, q, :], ident[:, :])
                mm.then_inc(out_turned, 1)

            for g in range(AHEAD):
                product(0, g, 0)
                product(0, g, 1)
            pe.wait_ge(w_split, 2)

            def body(t, odd, ahead, earlier):
                for g in range(GPT):
                    u, v = divmod(g + AHEAD, GPT)
                    more = u == 0 or ahead
                    if more:
                        product(t + u, v, 0)
                    turn(t, g, 0)
                    turn(t, g, 1)
                    if more:
                        product(t + u, v, 1)
                    if g == len(PARTS) - 1 and earlier:
                        value_product(t - 1, not odd, g)
                    turn(t, g, 2)
                    turn(t, g, 3)
                    if g < len(PARTS) - 1 and earlier:
                        value_product(t - 1, not odd, g)
                    if g == AVG + 1 and earlier:
                        turn_out(t - 1)
                    if g == GPT - 1 and ahead and earlier:
                        pe.wait_ge(scaled, t)
                    if g >= GPT - 2 and not ahead:
                        if g == GPT - 2:
                            pe.wait_ge(scaled, t)
                        half_product(0, range(8 * (g - GPT + 2), 8 * (g - GPT + 2) + 8))
            tiles(pe, body)
            half_product(1, range(NT)).then_inc(av_part, 1)
            turn_out(NT - 1)


def stack_k(sp, g, ks, k_hi, k_lo, k_in):
    for j in range(2):
        rows = slice(NKV * HD * j + HD * g, NKV * HD * j + HD * g + HD)
        for part, src in enumerate((k_hi, k_hi, k_lo)):
            dst = ks[HD * part:HD * part + HD, g, :].rearrange("p (c j n) -> p j c n", c=2, j=2)
            sp.dma_start(dst[:, j, :, :].bitcast(F32), src[rows, :, :].bitcast(F32)).then_inc(k_in[g], 16)


def stack_q(sp, g, c, qs, q_hi, q_lo, q_in):
    for h in (2 * g, 2 * g + 1):
        rows, cols = slice(HD * h, HD * h + HD), slice(2 * TC * c, 2 * TC * c + 2 * TC)
        for part, src in enumerate((q_hi, q_lo, q_hi)):
            sp.dma_start(qs[HD * part:HD * part + HD, h, cols].bitcast(F32),
                         src[rows, 2 * c:2 * c + 2, :].rearrange("p q n -> p (q n)").bitcast(F32)).then_inc(q_in[g][c], 16)


def block_input(nc, d, x_sb, y, ident, gstat, qs, ks, vx, identb, cutb, stat, q_hi, q_lo, k_hi, k_lo, k_in, q_in):
    KR = NKV * HD
    with ExitStack() as ctx:
        m = Names(nc, ctx)
        h = m.sb("bi_h", [P, NT, C])
        eps = m.sb("bi_eps", [P, 2])
        ht = m.sb("bi_ht", [P, N])
        ln1 = m.sb("bi_ln1", [P, 1])
        wq = m.sb("bi_wq", [P, 2, NH * HD])
        wk = m.sb("bi_wk", [P, 2, KR])
        wv = m.sb("bi_wv", [P, KR])
        cos = m.sb("bi_cos", [P, N])
        sin = m.sb("bi_sin", [P, N])
        cosk = m.sb("bi_cosk", [P, 2, TC])
        sink = m.sb("bi_sink", [P, 2, TC])
        rot = m.sb("bi_rot", [P, 2, 2, TC])
        full = m.sb("bi_full", [P, 2, TC])
        cut = m.sb("bi_cut", [P, 2, P])
        ps = m.ps("bi_ps", [P, 8, 512])
        tables_k = m.sem("bi_tables_k")
        loaded, tables, cut_in = m.sem("bi_loaded"), m.sem("bi_tables"), m.sem("bi_cut_in")
        link_s, fixed = m.sem("bi_link"), m.sem("bi_fixed")
        sum_ready, std_ready, scale_ready = m.sem("bi_sum"), m.sem("bi_std"), m.sem("bi_scale")
        h_ready = m.sem("bi_h_s")
        ht_ps, ht_ready, v_ps, v_done = m.sem("bi_ht_ps"), m.sem("bi_ht_s"), m.sem("bi_v_ps"), m.sem("bi_v_s")
        unit_ps = m.sem("bi_unit_ps")
        by_cos, by_sin, rotated = m.sem("bi_by_cos"), m.sem("bi_by_sin"), m.sem("bi_rotated")
        high, low = m.sem("bi_high"), m.sem("bi_low")
        block = ctx.enter_context(nc.Block())
        units = [(0, 0), (1, 0)] + [(c, i) for c in range(2) for i in (1, 2)]

        def tables_of(c, i):
            if i == 0:
                return cosk[:, c, :], sink[:, c, :], k_hi[:, c, :], k_lo[:, c, :]
            q = 2 * c + i - 1
            cols = slice(TC * q, TC * q + TC)
            return cos[:, cols], sin[:, cols], q_hi[:, q, :], q_lo[:, q, :]

        @block.sync
        def _(sp):
            sp.dma_start(ln1[:, :], d["ln1"]).then_inc(loaded, 16)
            for k in range(2):
                sp.dma_start(wq[:, k, :], d["wqT"][k]).then_inc(loaded, 16)
                sp.dma_start(wk[:, k, :], d["wkT"][k]).then_inc(loaded, 16)
            sp.dma_start(wv[:, :], d["wvT"]).then_inc(loaded, 16)
            sp.dma_start(cosk[:, :, :], d["cosK"]).then_inc(tables_k, 16)
            sp.dma_start(sink[:, :, :], d["sinK"]).then_inc(tables_k, 16)
            sp.dma_start(cos[:, :], d["cosT"]).then_inc(tables, 16)
            sp.dma_start(sin[:, :], d["sinT"]).then_inc(tables, 16)
            sp.dma_start(cut[:, 0, :], d["causal_ts"]).then_inc(cut_in, 16)
            sp.dma_start(cut[:, 1, :], d["causal_st"]).then_inc(cut_in, 16)
            sp.wait_ge(low, 2)
            stack_k(sp, 0, ks, k_hi, k_lo, k_in)
            sp.wait_ge(low, 4)
            stack_q(sp, 0, 0, qs, q_hi, q_lo, q_in)

        @block.gpsimd
        def _(pool):
            link = chain(pool, fixed)
            link(pool.memset(ks[3 * HD:3 * HD + 1, :, :].bitcast(F32), 1.0))
            link(pool.memset(vx[:, :, :, :], 0.0))
            link(pool.memset(vx[:, :, :, HD:HD + 1], 1.0))
            link(pool.memset(cutb[:, :, :], 0.0))
            link(pool.tensor_copy(identb[:, :], ident[:, :]))
            pool.wait_ge(cut_in, 32)
            link(pool.tensor_copy(cutb[:, 0, TC - P:TC], cut[:, 0, :]))
            link(pool.tensor_copy(cutb[:, 1, 0:P], cut[:, 1, :]))

        @block.vector
        def _(dve):
            link = chain(dve, link_s)
            link(dve.memset(eps[:, 0:1], LN_EPS))
            link(dve.memset(eps[:, 1:2], RMS_EPS))
            moments(dve, link, gstat, stat)
            dve.sem_inc(sum_ready, 1)
            dve.wait_ge(std_ready, 1)
            link(dve.reciprocal(stat[:, 5, :], stat[:, 4, :]))
            link(dve.tensor_tensor(stat[:, 6, :], stat[:, 1, :], stat[:, 5, :], ALU.mult))
            dve.tensor_tensor(stat[:, 7, :], stat[:, 6, :], stat[:, 5, :], ALU.mult).then_inc(sum_ready, 1)
            dve.wait_ge(std_ready, 2)
            link(dve.reciprocal(stat[:, 9, :], stat[:, 8, :]))
            dve.tensor_tensor(stat[:, 6, :], stat[:, 5, :], stat[:, 9, :], ALU.mult).then_inc(scale_ready, 1)
            dve.wait_ge(scale_ready, 1)
            for t in range(NT):
                dve.tensor_scalar(h[:, t, :], x_sb[:, t, :], stat[:, 0, t:t + 1], stat[:, 6, t:t + 1], ALU.subtract,
                                  ALU.mult).then_inc(h_ready, 1)
            for u, (c, i) in enumerate(units):
                cs, sn, hi, lo = tables_of(c, i)
                bank, s = 2 + 2 * (u % 3), u % 2
                if i == 0:
                    dve.wait_ge(tables_k, 32)
                else:
                    dve.wait_ge(tables, 32)
                dve.wait_ge(unit_ps, u + 1)
                if u >= 2:
                    dve.wait_ge(rotated, u - 1)
                dve.tensor_tensor(rot[:, s, 0, :], ps[:, bank, :], cs, ALU.mult).then_inc(by_cos, 1)
                dve.tensor_tensor(rot[:, s, 1, :], ps[:, bank + 1, :], sn, ALU.mult).then_inc(by_sin, 1)
                if u:
                    pc, pi = units[u - 1]
                    _, _, phi, plo = tables_of(pc, pi)
                    dve.wait_ge(high, u)
                    dve.tensor_tensor(plo, full[:, 1 - s, :], phi.bitcast(F32), ALU.subtract).then_inc(low, 1)
                dve.wait_ge(by_cos, u + 1)
                dve.wait_ge(by_sin, u + 1)
                if u >= 2:
                    dve.wait_ge(low, u - 1)
                dve.tensor_tensor(full[:, s, :], rot[:, s, 0, :], rot[:, s, 1, :], ALU.add).then_inc(rotated, 1)
            _, _, phi, plo = tables_of(*units[-1])
            dve.wait_ge(high, len(units))
            dve.tensor_tensor(plo, full[:, 1, :], phi.bitcast(F32), ALU.subtract).then_inc(low, 1)

        @block.scalar
        def _(act):
            act.wait_ge(sum_ready, 1)
            act.activation(stat[:, 4, :], stat[:, 1, :], ACT.Sqrt, bias=eps[:, 0:1], scale=1.0 / C).then_inc(std_ready, 1)
            act.wait_ge(sum_ready, 2)
            act.activation(stat[:, 8, :], stat[:, 7, :], ACT.Sqrt, bias=eps[:, 1:2], scale=1.0 / C).then_inc(std_ready, 1)
            act.wait_ge(loaded, 96)
            for q in range(4):
                act.wait_ge(ht_ps, q + 1)
                act.activation(ht[:, TC * q:TC * q + TC], ps[:, q % 2, :], ACT.Copy, scale=ln1[:, 0:1]).then_inc(ht_ready, 1)
            for u, (c, i) in enumerate(units):
                act.wait_ge(rotated, u + 1)
                act.copy(tables_of(c, i)[2], full[:, u % 2, :]).then_inc(high, 1)
            act.wait_ge(fixed, 3)
            for q in range(2):
                act.wait_ge(v_ps, q + 1)
                act.copy(vx[:, 8 * q:8 * q + 8, :, 0:HD],
                         ps[:, q, :].rearrange("p (t g e) -> p t g e", t=8, g=NKV)).then_inc(v_done, 1)

        @block.tensor
        def _(pe):
            for q in range(4):
                pe.wait_ge(h_ready, 4 * q + 4)
                if q >= 2:
                    pe.wait_ge(ht_ready, q - 1)
                for k in range(4):
                    mm = pe.transpose(ps[:, q % 2, P * k:P * k + P], h[:, 4 * q + k, :], ident[:, :])
                mm.then_inc(ht_ps, 1)
            pe.wait_ge(loaded, 96)
            for u, (c, i) in enumerate(units):
                bank = 2 + 2 * (u % 3)
                pe.wait_ge(ht_ready, 2 * c + (2 if i != 1 else 1))
                if u >= 3:
                    pe.wait_ge(by_cos, u - 2)
                    pe.wait_ge(by_sin, u - 2)
                for r in range(2):
                    if i == 0:
                        for j in range(2):
                            q = 2 * c + j
                            mm = pe.matmul(ps[KR * j:KR * j + KR, bank + r, :], wk[:, r, :], ht[:, TC * q:TC * q + TC],
                                           start=True, stop=True)
                    else:
                        q = 2 * c + i - 1
                        mm = pe.matmul(ps[:, bank + r, :], wq[:, r, :], ht[:, TC * q:TC * q + TC], start=True, stop=True)
                mm.then_inc(unit_ps, 1)
            for q in range(2):
                for k in range(8):
                    t = 8 * q + k
                    mm = pe.matmul(ps[:, q, KR * k:KR * k + KR], ht[:, P * t:P * t + P], wv[:, :], start=True, stop=True)
                mm.then_inc(v_ps, 1)


def causal_attention(nc, d, x_sb, y, qs, ks, vx, ident, u_sb, identb, cutb, stat, q_hi, q_lo, k_hi, k_lo, k_in, q_in):
    K = 3 * HD
    chunks = [(g, tc) for g in range(NKV) for tc in range(N // TC)]
    tiles_c = TC // P
    ahead, rows_of = [], {}
    for c, (g, tc) in enumerate(chunks):
        for h in (2 * g, 2 * g + 1):
            for tt in range(tiles_c * tc, tiles_c * tc + tiles_c):
                for sc in range(tc + 1):
                    ahead.append((c, h, tt, sc))
        rows_of[c] = len(ahead)
    turn_after = {rows_of[c] + 1: c for c in rows_of}
    steps = []
    for i, unit in enumerate(ahead):
        steps.append(unit)
        if i in turn_after:
            steps.append((turn_after[i], None, None, None))
    steps.append((len(chunks) - 1, None, None, None))
    last_of = {c: max(i for i, u in enumerate(steps) if u[0] == c and u[1] is not None) for c in range(len(chunks))}
    stacks_from = [min(i for i, u in enumerate(steps) if u[0] == c) for c, (g, tc) in enumerate(chunks) if tc % 2 == 0]
    units = [(c, sj) for c, (g, tc) in enumerate(chunks) for sj in range(tiles_c * (tc + 1))]
    end_of = {c: max(i for i, u in enumerate(units) if u[0] == c) for c in range(len(chunks))}

    per_head = len(chunks) // NKV
    marks = [c for c in range(len(chunks)) if c < per_head or c == len(chunks) - 1]
    at = [min(i for i, u in enumerate(units) if u[0] == c) for c in marks]
    before = [max(i for i, u in enumerate(steps) if u[0] == c) + 1 + SLACK for c in marks]

    def due(n):
        return min(len(steps), int(np.ceil(np.interp(n, at, before))))

    with ExitStack() as ctx:
        m = Names(nc, ctx)
        probs = m.sb("ca_probs", [P, 3, 2, TC])
        mx = m.sb("ca_mx", [P, len(chunks), 2, tiles_c, NT // tiles_c])
        neg = m.sb("ca_neg", [P, len(chunks), 2, tiles_c])
        negt = m.sb("ca_negt", [2 * tiles_c, len(chunks), P], F32R)
        sps = m.ps("ca_sps", [P, 2, 512])
        tps = m.ps("ca_tps", [P, 2, 2, TC])
        ops = m.ps("ca_ops", [P, 2, TC])
        link_s = m.sem("ca_link")
        s_ready, s_used = m.sem("ca_s_ready"), m.sem("ca_s_used")
        neg_ready = m.sem("ca_neg_ready")
        neg_copied = m.sem("ca_neg_copied")
        neg_row = [m.sem(f"ca_neg_row{c}") for c in range(len(chunks))]
        t_ready, t_exp = m.sem("ca_t_ready"), m.sem("ca_t_exp")
        pv_done, o_moved = m.sem("ca_pv_done"), m.sem("ca_o_moved")
        y_done = m.sem("ca_y")
        block = ctx.enter_context(nc.Block())

        @block.gpsimd
        def _(pool):
            for t in range(NT):
                if t:
                    pool.wait_ge(y_done, t)
                pool.tensor_scalar(y[:, t, :], x_sb[:, t, :], stat[:, 0, t:t + 1], stat[:, 5, t:t + 1], ALU.subtract,
                                   ALU.mult).then_inc(y_done, 1)

        @block.sync
        def _(sp):
            stack_q(sp, 0, 1, qs, q_hi, q_lo, q_in)
            for c, (g, tc) in enumerate(chunks):
                sp.wait_ge(neg_copied, c + 1)
                for h in range(2):
                    dst = qs[K:K + 1, 2 * g + h, TC * tc:TC * tc + TC]
                    sp.dma_start(dst.bitcast(F32), negt[tiles_c * h:tiles_c * h + tiles_c, c, :].bitcast(F32)).then_inc(neg_row[c], 16)
                if c == 0:
                    stack_k(sp, 1, ks, k_hi, k_lo, k_in)
                elif c <= 2:
                    stack_q(sp, 1, c - 1, qs, q_hi, q_lo, q_in)

        @block.vector
        def _(dve):
            link = chain(dve, link_s)
            link(dve.memset(mx[:, :, :, :, :], -3e38))

            def take(n):
                c, h, tt, sc = steps[n]
                g, tc = chunks[c]
                dve.wait_ge(s_ready, n + 1)
                if h is None:
                    dve.tensor_copy(negt[:, c, :], sps[0:2 * tiles_c, n % 2, 0:P]).then_inc(s_used, 1)
                    dve.wait_ge(s_used, n + 1)
                    dve.sem_inc(neg_copied, 1)
                    return
                w = min(512, P * (tt + 1) - 512 * sc)
                dve.tensor_reduce(mx[:, c, h - 2 * g, tt - tiles_c * tc, sc:sc + 1], sps[:, n % 2, 0:w], AX.X,
                                  ALU.max).then_inc(s_used, 1)
                if n == last_of[c]:
                    dve.wait_ge(s_used, n + 1)
                    dve.tensor_reduce(neg[:, c, :, :], mx[:, c, :, :, :], AX.X, ALU.max, negate=True).then_inc(neg_ready, 1)

            def move_out(c):
                dve.wait_ge(pv_done, end_of[c] + 1)
                dve.tensor_copy(u_sb[:, chunks[c][0], TC * chunks[c][1]:TC * chunks[c][1] + TC], ops[:, c % 2, :]).then_inc(o_moved, 1)

            for n in range(due(0)):
                take(n)
            for u, (c, sj) in enumerate(units):
                for n in range(due(u), due(u + 1)):
                    take(n)
                if sj == 1 and c:
                    move_out(c - 1)
            move_out(len(chunks) - 1)

        @block.scalar
        def _(act):
            for u, (c, sj) in enumerate(units):
                off = max(0, P * sj - TC * chunks[c][1])
                act.wait_ge(t_ready, u + 1)
                if u >= 3:
                    act.wait_ge(pv_done, u - 2)
                act.activation(probs[:, u % 3, :, off:TC], tps[:, u % 2, :, off:TC], ACT.Exp,
                               scale=float(np.float32(1) / np.sqrt(np.float32(HD)))).then_inc(t_exp, 1)

        @block.tensor
        def _(pe):
            def by_target(n):
                c, h, tt, sc = steps[n]
                g, tc = chunks[c]
                if n >= 2:
                    pe.wait_ge(s_used, n - 1)
                if h is None:
                    pe.wait_ge(neg_ready, c + 1)
                    pe.transpose(sps[0:2 * tiles_c, n % 2, 0:P], neg[:, c, :, :].rearrange("p h t -> p (h t)"),
                                 ident[:, :]).then_inc(s_ready, 1)
                    return
                if n in stacks_from:
                    pe.wait_ge(k_in[g], 16 * 3 * 2)
                    pe.wait_ge(q_in[g][tc // 2], 16 * 3 * 2)
                w = min(512, P * (tt + 1) - 512 * sc)
                diag = sc == tc
                if diag:
                    pe.matmul(sps[:, n % 2, 0:w], identb[:, :], cutb[:, 0, TC - w:TC], start=True, stop=False)
                pe.matmul(sps[:, n % 2, 0:w], qs[0:K, h, P * tt:P * tt + P], ks[0:K, g, 512 * sc:512 * sc + w],
                          start=not diag, stop=True).then_inc(s_ready, 1)

            def by_source(u, h):
                c, sj = units[u]
                g, tc = chunks[c]
                off = max(0, P * sj - TC * tc)
                diag = sj >= tiles_c * tc
                if h == 0 and u >= 2:
                    pe.wait_ge(t_exp, u - 1)
                if h == 0 and sj == 0:
                    pe.wait_ge(neg_row[c], 32)
                if diag:
                    pe.matmul(tps[:, u % 2, h, off:TC], identb[:, :], cutb[:, 1, 0:TC - off], start=True, stop=False)
                mm = pe.matmul(tps[:, u % 2, h, off:TC], ks[0:K + 1, g, P * sj:P * sj + P],
                               qs[0:K + 1, 2 * g + h, TC * tc + off:TC * tc + TC], start=not diag, stop=True)
                if h == 1:
                    mm.then_inc(t_ready, 1)

            def values(u, h):
                c, sj = units[u]
                g, tc = chunks[c]
                off = max(0, P * sj - TC * tc)
                if h == 0:
                    pe.wait_ge(t_exp, u + 1)
                    if sj == 0 and c >= 2:
                        pe.wait_ge(o_moved, c - 1)
                mm = pe.matmul(ops[VW * h:VW * h + VW, c % 2, off:TC], vx[:, sj, g, :], probs[:, u % 3, h, off:TC],
                               start=(sj == 0), stop=(u == end_of[c]), skip_group_check=True)
                if h == 1:
                    mm.then_inc(pv_done, 1)

            for n in range(due(0)):
                by_target(n)
            for u in range(len(units)):
                between = list(range(due(u), due(u + 1)))
                by_source(u, 0)
                for n in between[0:1]:
                    by_target(n)
                by_source(u, 1)
                for n in between[1:2]:
                    by_target(n)
                if u:
                    values(u - 1, 0)
                for n in between[2:]:
                    by_target(n)
                if u:
                    values(u - 1, 1)
            for h in range(2):
                values(len(units) - 1, h)


def project(nc, d, y, u_sb, ident, ystat, weights_of):
    STEPS, W = NT // 4, 4
    raw, w_hi, w_lo, w_in, w_high, w_low = weights_of
    with ExitStack() as ctx:
        m = Names(nc, ctx)
        wo = m.sb("pj_wo", [P, C])
        rden = m.sb("pj_rden", [P, 2, W, NH])
        heads = m.sb("pj_heads", [P, 2, W, NH, HD])
        heads_t = m.sb("pj_heads_t", [P, 2, W * P])
        ups = m.ps("pj_ups", [P, 2, W, 2 * P])
        hps = m.ps("pj_hps", [P, 2, W * P])
        yps = m.ps("pj_yps", [P, 2, W, C])
        loaded = m.sem("pj_loaded")
        turned, inverted, divided = m.sem("pj_turned"), m.sem("pj_inverted"), m.sem("pj_divided")
        back, moved = m.sem("pj_back"), m.sem("pj_moved")
        projected, added, stats = m.sem("pj_projected"), m.sem("pj_added"), m.sem("pj_stats")
        block = ctx.enter_context(nc.Block())

        @block.sync
        def _(sp):
            sp.dma_start(wo[:, :], d["woT"]).then_inc(loaded, 16)
            for b in range(2):
                sp.dma_start(raw[:, b, :], d["experts"][b]).then_inc(w_in[b], 16)

        @block.gpsimd
        def _(pool):
            pool.wait_ge(w_high, 1)
            pool.tensor_tensor(w_lo[:, 0, :], raw[:, 0, :], w_hi[:, 0, :].bitcast(F32), ALU.subtract).then_inc(w_low, 1)

        @block.vector
        def _(dve):
            def divide(q):
                by_head = ups[:, q % 2, :, :].rearrange("p t (h e) -> p (t h) e", e=VW)
                dve.wait_ge(turned, q + 1)
                dve.reciprocal(rden[:, q % 2, :, :].rearrange("p t h -> p (t h)"), by_head[:, :, HD]).then_inc(inverted, 1)
                dve.wait_ge(inverted, q + 1)
                if q >= 2:
                    dve.wait_ge(back, q - 1)
                dve.tensor_tensor(heads[:, q % 2, :, :, :].rearrange("p t h e -> p (t h) e"), by_head[:, :, 0:HD],
                                  bc(rden[:, q % 2, :, :].rearrange("p t h -> p (t h)"), HD), ALU.mult).then_inc(divided, 1)

            def add(q):
                tiles = slice(W * q, W * q + W)
                dve.wait_ge(projected, q + 1)
                dve.tensor_tensor(y[:, tiles, :], y[:, tiles, :], yps[:, q % 2, :, :], ALU.add).then_inc(added, 1)
                dve.wait_ge(added, q + 1)
                for t in range(W * q, W * q + W):
                    dve.bn_stats(ystat[:, t, :], y[:, t, :]).then_inc(stats, 1)

            for q in range(STEPS):
                divide(q)
                if q:
                    add(q - 1)
            add(STEPS - 1)

        @block.scalar
        def _(act):
            act.wait_ge(w_in[0], 16)
            act.copy(w_hi[:, 0, :], raw[:, 0, :]).then_inc(w_high, 1)
            for q in range(STEPS):
                act.wait_ge(back, q + 1)
                if q >= 2:
                    act.wait_ge(projected, q - 1)
                act.copy(heads_t[:, q % 2, :], hps[:, q % 2, :]).then_inc(moved, 1)

        @block.tensor
        def _(pe):
            def turn(q):
                if q >= 2:
                    pe.wait_ge(divided, q - 1)
                for t in range(W):
                    for g in range(2):
                        mm = pe.transpose(ups[:, q % 2, t, P * g:P * g + P],
                                          u_sb[:, g, P * (W * q + t):P * (W * q + t) + P], ident[:, :])
                mm.then_inc(turned, 1)

            def turn_back(q):
                pe.wait_ge(divided, q + 1)
                if q >= 2:
                    pe.wait_ge(moved, q - 1)
                for t in range(W):
                    mm = pe.transpose(hps[:, q % 2, P * t:P * t + P],
                                      heads[:, q % 2, t, :, :].rearrange("p h e -> p (h e)"), ident[:, :])
                mm.then_inc(back, 1)

            def projection(q):
                pe.wait_ge(moved, q + 1)
                if q >= 2:
                    pe.wait_ge(added, q - 1)
                for t in range(W):
                    mm = pe.matmul(yps[:, q % 2, t, :], heads_t[:, q % 2, P * t:P * t + P], wo[:, :], start=True, stop=True)
                mm.then_inc(projected, 1)

            turn(0)
            pe.wait_ge(loaded, 16)
            for q in range(STEPS):
                if q + 1 < STEPS:
                    turn(q + 1)
                turn_back(q)
                if q:
                    projection(q - 1)
            projection(STEPS - 1)


def experts(nc, d, out, x_sb, y, ident, ystat, weights_of):
    UN, NCH = len(HK), N // TC
    raw, w_hi, w_lo, w_in, w_high, w_low = weights_of
    W1, W3, W2 = 0, HID, 2 * HID
    scratch = nc.dram_tensor("routing_rows", (NE, N), F32).ap()
    with ExitStack() as ctx:
        m = Names(nc, ctx)
        sq = m.sb("ex_sq", [P, NT, C])
        stat = m.sb("ex_stat", [P, 8, NT])
        eps = m.sb("ex_eps", [P, 1])
        ft = m.sb("ex_ft", [P, N])
        f_hi = m.sb("ex_f_hi", [P, N], F32R)
        f_lo = m.sb("ex_f_lo", [P, N], F32R)
        ln2 = m.sb("ex_ln2", [P, 1])
        rw = m.sb("ex_rw", [P, NE])
        desc = m.sb("ex_desc", [P, NE])
        pr = m.sb("ex_pr", [P, NT, NE])
        r = m.sb("ex_r", [P, 6, NT, NE])
        rs = m.sb("ex_rs", [P, 8, NT])
        wgt = m.sb("ex_wgt", [P, NT, NE])
        wgt_t = m.sb("ex_wgt_t", [P, P])
        wrow = m.sb("ex_wrow", [P, 2, N])
        gate = m.sb("ex_gate", [P, 2, TC])
        hid = m.sb("ex_hid", [P, 2, TC])
        h_hi = m.sb("ex_h_hi", [P, 2, UN, TC], F32R)
        h_lo = m.sb("ex_h_lo", [P, 2, UN, TC], F32R)
        part = m.sb("ex_part", [P, 2, TC])
        acc = m.sb("ex_acc", [P, N])
        aps = m.ps("ex_aps", [P, 2, TC])
        bps = m.ps("ex_bps", [P, 2, TC])
        ops = m.ps("ex_ops", [P, 2, TC])
        xps = m.ps("ex_xps", [P, 2, 512])
        loaded, link_s, zeroed = m.sem("ex_loaded"), m.sem("ex_link"), m.sem("ex_zeroed")
        sum_ready, std_ready, f_ready = m.sem("ex_sum"), m.sem("ex_std"), m.sem("ex_f")
        ft_ps, ft_ready, f_high, f_split = m.sem("ex_ft_ps"), m.sem("ex_ft_s"), m.sem("ex_f_high"), m.sem("ex_f_split")
        r_ps, shifted, r_exp = m.sem("ex_r_ps"), m.sem("ex_shifted"), m.sem("ex_r_exp")
        wgt_ready, wgt_ps, wgt_rows, wgt_dram = m.sem("ex_wgt_s"), m.sem("ex_wgt_ps"), m.sem("ex_wgt_rows"), m.sem("ex_wgt_dram")
        row_in = [m.sem(f"ex_row_in{b}") for b in range(2)]
        ab_ready = m.sem("ex_ab_ready")
        gated = m.sem("ex_gated")
        multiplied = m.sem("ex_multiplied")
        high, low = m.sem("ex_high"), m.sem("ex_low")
        o_ready = m.sem("ex_o_ready")
        weighted, combined = m.sem("ex_weighted"), m.sem("ex_combined")
        high_seen = m.sem("ex_high_seen")
        acc_ps, x_ready, total, stored = m.sem("ex_acc_ps"), m.sem("ex_x_ready"), m.sem("ex_total"), m.sem("ex_stored")
        block = ctx.enter_context(nc.Block())

        def pairs(engine, body):
            for b in range(2):
                body(b, b)
            with engine.Fori(1, NE // 2 - 1) as i:
                for b in range(2):
                    body(2 * i + b, b)
            for b in range(2):
                body(NE - 2 + b, b)

        def is_at(e, value):
            return isinstance(e, int) and e == value

        @block.sync
        def _(sp):
            sp.dma_start(ln2[:, :], d["ln2"]).then_inc(loaded, 16)
            sp.dma_start(rw[:, :], d["routerT"]).then_inc(loaded, 16)
            sp.dma_start(desc[:, :], d["descend"]).then_inc(loaded, 16)

            def weights(e, b):
                sp.wait_ge(w_low, e - 1)
                one = bass.ds(e if isinstance(e, int) else sp.snap(e), 1)
                sp.dma_start(raw[:, b, :], d["experts"][one].rearrange("o p k -> (o p) k")).then_inc(w_in[b], 16)

            def row(e, b):
                if not (isinstance(e, int) and e < 2):
                    sp.wait_ge(weighted, NCH * (e - 1))
                one = bass.ds(e if isinstance(e, int) else sp.snap(e), 1)
                sp.dma_start(wrow[:, b, :], scratch[one].to_broadcast([P, N])).then_inc(row_in[b], 16)

            sp.wait_ge(wgt_rows, 1)
            sp.dma_start(scratch.rearrange("e (t p) -> t e p", p=P), wgt_t[:, :]).then_inc(wgt_dram, 16)
            sp.wait_ge(wgt_dram, 16)
            for b in range(2):
                row(b, b)
            with sp.Fori(1, NE // 2) as i:
                for b in range(2):
                    weights(2 * i + b, b)
                    row(2 * i + b, b)
            out_t = out.rearrange("(t p) c -> p t c", p=P)
            for q in range(NCH):
                sp.wait_ge(total, q + 1)
                sp.dma_start(out_t[:, 4 * q:4 * q + 4, :], x_sb[:, 4 * q:4 * q + 4, :]).then_inc(stored, 16)
            sp.wait_ge(stored, 16 * NCH)

        @block.gpsimd
        def _(pool):
            pool.memset(acc[:, :], 0.0).then_inc(zeroed, 1)
            pool.wait_ge(zeroed, 1)
            pool.tensor_tensor(x_sb[:, :, :], x_sb[:, :, :], y[:, :, :], ALU.add).then_inc(x_ready, 1)

            def split_low(e, b):
                pool.wait_ge(w_high, e + 1)
                pool.sem_inc(high_seen, 1)
                pool.tensor_tensor(w_lo[:, b, :], raw[:, b, :], w_hi[:, b, :].bitcast(F32), ALU.subtract).then_inc(w_low, 1)

            def body(e, b):
                if not is_at(e, NE - 1):
                    split_low(e + 1, 1 - b)
            pairs(pool, body)

        @block.vector
        def _(dve):
            link = chain(dve, link_s)
            link(dve.memset(eps[:, :], RMS_EPS))
            moments(dve, link, ystat, stat)
            link(dve.tensor_tensor(stat[:, 2, :], stat[:, 0, :], stat[:, 0, :], ALU.mult))
            dve.scalar_tensor_tensor(stat[:, 3, :], stat[:, 2, :], float(C), stat[:, 1, :], ALU.mult, ALU.add).then_inc(sum_ready, 1)
            dve.wait_ge(std_ready, 1)
            link(dve.reciprocal(stat[:, 5, :], stat[:, 4, :]))
            for t in range(NT):
                dve.tensor_scalar(sq[:, t, :], y[:, t, :], stat[:, 5, t:t + 1], None, ALU.mult).then_inc(f_ready, 1)
            for q in range(4):
                cols = slice(512 * q, 512 * q + 512)
                dve.wait_ge(f_high, q + 1)
                dve.tensor_tensor(f_lo[:, cols], ft[:, cols], f_hi[:, cols].bitcast(F32), ALU.subtract).then_inc(f_split, 1)

            marks = desc[:, :].rearrange("p (o e) -> p o e", o=1).to_broadcast([P, NT, NE])

            def first_largest(src, largest, mark, hot):
                link(dve.tensor_reduce(rs[:, largest, :], src, AX.X, ALU.max))
                link(dve.tensor_tensor(r[:, 0, :, :], src, bc(rs[:, largest, :], NE), ALU.is_ge))
                link(dve.tensor_tensor(r[:, 1, :, :], r[:, 0, :, :], marks, ALU.mult))
                link(dve.tensor_reduce(rs[:, mark, :], r[:, 1, :, :], AX.X, ALU.max))
                link(dve.tensor_tensor(r[:, hot, :, :], r[:, 1, :, :], bc(rs[:, mark, :], NE), ALU.is_equal))

            def routing(stage):
                if stage == 0:
                    dve.wait_ge(r_ps, 1)
                    link(dve.tensor_copy(r[:, 0, :, :], xps[:, 0, 0:NT * NE].rearrange("p (t e) -> p t e", e=NE)))
                    link(dve.tensor_reduce(rs[:, 0, :], r[:, 0, :, :], AX.X, ALU.max))
                    dve.tensor_tensor(r[:, 1, :, :], r[:, 0, :, :], bc(rs[:, 0, :], NE), ALU.subtract).then_inc(shifted, 1)
                elif stage == 1:
                    dve.wait_ge(r_exp, 1)
                    link(dve.tensor_reduce(rs[:, 1, :], r[:, 2, :, :], AX.X, ALU.add))
                    link(dve.reciprocal(rs[:, 2, :], rs[:, 1, :]))
                    link(dve.tensor_tensor(pr[:, :, :], r[:, 2, :, :], bc(rs[:, 2, :], NE), ALU.mult))
                elif stage == 2:
                    first_largest(pr[:, :, :], 3, 4, 3)
                elif stage == 3:
                    link(dve.scalar_tensor_tensor(r[:, 5, :, :], r[:, 3, :, :], -2.0, pr[:, :, :], ALU.mult, ALU.add))
                    first_largest(r[:, 5, :, :], 5, 4, 4)
                elif stage == 4:
                    link(dve.scalar_tensor_tensor(rs[:, 6, :], rs[:, 3, :], 1e-9, rs[:, 5, :], ALU.add, ALU.add))
                    link(dve.reciprocal(rs[:, 7, :], rs[:, 6, :]))
                    link(dve.tensor_tensor(r[:, 0, :, :], r[:, 3, :, :], r[:, 4, :, :], ALU.add))
                    link(dve.tensor_tensor(r[:, 1, :, :], r[:, 0, :, :], pr[:, :, :], ALU.mult))
                    dve.tensor_tensor(wgt[:, :, :], r[:, 1, :, :], bc(rs[:, 7, :], NE), ALU.mult).then_inc(wgt_ready, 1)

            def routing_rows():
                dve.wait_ge(wgt_ps, 1)
                dve.tensor_copy(wgt_t[:, :], xps[:, 1, 0:P]).then_inc(wgt_rows, 1)

            def combine(e, b, tc):
                n = NCH * e + tc
                cols = slice(TC * tc, TC * tc + TC)
                if tc == 0:
                    dve.wait_ge(row_in[b], 16 * (e // 2 + 1) if isinstance(e, int) else 8 * (e - b + 2))
                dve.wait_ge(o_ready, n + 1)
                if not (is_at(e, 0) and tc < 2):
                    dve.wait_ge(combined, n - 1)
                dve.tensor_tensor(part[:, tc % 2, :], ops[:, tc % 2, :], wrow[:, b, cols], ALU.mult).then_inc(weighted, 1)
                dve.wait_ge(weighted, n + 1)
                if not is_at(e, 0):
                    dve.wait_ge(combined, n - NCH + 1)
                dve.tensor_tensor(acc[:, cols], acc[:, cols], part[:, tc % 2, :], ALU.add).then_inc(combined, 1)

            def multiply(e, tc, k):
                u = (NCH * e + tc) * UN + k
                rows, s = HK[k][1], (tc * UN + k) % 2
                dve.wait_ge(gated, u + 1)
                if not (is_at(e, 0) and tc == 0 and k < 2):
                    dve.wait_ge(low, u - 1)
                dve.tensor_tensor(hid[0:rows, s, :], gate[0:rows, s, :], bps[0:rows, s, :], ALU.mult).then_inc(multiplied, 1)

            def split_hidden(e, tc, k):
                u = (NCH * e + tc) * UN + k
                rows, s = HK[k][1], (tc * UN + k) % 2
                dve.wait_ge(high, u + 1)
                dve.tensor_tensor(h_lo[0:rows, tc % 2, k, :], hid[0:rows, s, :], h_hi[0:rows, tc % 2, k, :].bitcast(F32),
                                  ALU.subtract).then_inc(low, 1)

            def body(e, b):
                for tc in range(NCH):
                    for k in range(UN):
                        multiply(e, tc, k)
                        if k:
                            split_hidden(e, tc, k - 1)
                        elif tc:
                            split_hidden(e, tc - 1, UN - 1)
                        elif not is_at(e, 0):
                            split_hidden(e - 1, NCH - 1, UN - 1)
                        if is_at(e, 0) and UN * tc + k <= 4:
                            routing(UN * tc + k)
                        if is_at(e, 0) and UN * tc + k == 5:
                            routing_rows()
                            dve.wait_ge(zeroed, 1)
                    if is_at(e, 0):
                        if tc == 2:
                            combine(e, b, 0)
                        elif tc == 3:
                            combine(e, b, 1)
                            combine(e, b, 2)
                    elif tc:
                        combine(e, b, tc - 1)
                    else:
                        combine(e - 1, 1 - b, NCH - 1)
            pairs(dve, body)
            split_hidden(NE - 1, NCH - 1, UN - 1)
            combine(NE - 1, 1, NCH - 1)
            dve.wait_ge(x_ready, 1)
            for q in range(NCH):
                dve.wait_ge(acc_ps, q + 1)
                xq = x_sb[:, 4 * q:4 * q + 4, :].rearrange("p t c -> p (t c)")
                dve.tensor_tensor(xq, xq, xps[:, q % 2, :], ALU.add).then_inc(total, 1)

        @block.scalar
        def _(act):
            def split_high(e, b):
                act.wait_ge(w_in[b], 16 * (e // 2 + 1) if isinstance(e, int) else 8 * (e - b + 2))
                if not (isinstance(e, int) and e < 2):
                    act.wait_ge(o_ready, NCH * (e - 1))
                act.copy(w_hi[:, b, :], raw[:, b, :]).then_inc(w_high, 1)

            act.wait_ge(sum_ready, 1)
            act.activation(stat[:, 4, :], stat[:, 3, :], ACT.Sqrt, bias=eps[:, 0:1], scale=1.0 / C).then_inc(std_ready, 1)
            act.wait_ge(loaded, 48)
            for q in range(4):
                cols = slice(512 * q, 512 * q + 512)
                act.wait_ge(ft_ps, q + 1)
                act.activation(ft[:, cols], xps[:, q % 2, :], ACT.Copy, scale=ln2[:, 0:1]).then_inc(ft_ready, 1)
                act.wait_ge(ft_ready, q + 1)
                act.copy(f_hi[:, cols], ft[:, cols]).then_inc(f_high, 1)
            def silu(e, tc, k):
                u = (NCH * e + tc) * UN + k
                rows, s = HK[k][1], (tc * UN + k) % 2
                act.wait_ge(ab_ready, u + 1)
                if not (is_at(e, 0) and tc == 0 and k < 2):
                    act.wait_ge(multiplied, u - 1)
                act.activation(gate[0:rows, s, :], aps[0:rows, s, :], ACT.Silu).then_inc(gated, 1)

            def round_hidden(e, tc, k):
                n = NCH * e + tc
                rows, s = HK[k][1], (tc * UN + k) % 2
                act.wait_ge(multiplied, n * UN + k + 1)
                if k == 0 and not (is_at(e, 0) and tc < 2):
                    act.wait_ge(o_ready, n - 1)
                act.copy(h_hi[0:rows, tc % 2, k, :], hid[0:rows, s, :]).then_inc(high, 1)

            def body(e, b):
                for tc in range(NCH):
                    for k in range(UN):
                        silu(e, tc, k)
                        if k:
                            round_hidden(e, tc, k - 1)
                        elif tc:
                            round_hidden(e, tc - 1, UN - 1)
                        elif not is_at(e, 0):
                            round_hidden(e - 1, NCH - 1, UN - 1)
                        if is_at(e, 0) and tc == 0 and k == 0:
                            act.wait_ge(shifted, 1)
                            act.activation(r[:, 2, :, :], r[:, 1, :, :], ACT.Exp).then_inc(r_exp, 1)
                    if tc == 1 and not is_at(e, NE - 1):
                        split_high(e + 1, 1 - b)
            pairs(act, body)
            round_hidden(NE - 1, NCH - 1, UN - 1)

        @block.tensor
        def _(pe):
            for q in range(4):
                pe.wait_ge(f_ready, 4 * q + 4)
                if q >= 2:
                    pe.wait_ge(ft_ready, q - 1)
                for k in range(4):
                    mm = pe.transpose(xps[:, q % 2, P * k:P * k + P], sq[:, 4 * q + k, :], ident[:, :])
                mm.then_inc(ft_ps, 1)

            def router():
                pe.wait_ge(ft_ready, 4)
                pe.wait_ge(loaded, 48)
                for t in range(NT):
                    mm = pe.matmul(xps[:, 0, NE * t:NE * t + NE], ft[:, P * t:P * t + P], rw[:, :], start=True, stop=True)
                mm.then_inc(r_ps, 1)

            def product(dst, terms):
                for i, (col, width, b, rows, hi, lo) in enumerate(terms):
                    for j, (w, x) in enumerate(((w_hi, hi), (w_hi, lo), (w_lo, hi))):
                        mm = pe.matmul(dst, w[0:rows, b, col:col + width], x, start=(i == 0 and j == 0),
                                       stop=(i == len(terms) - 1 and j == 2))
                return mm

            def hidden(e, b, tc, k):
                u = (NCH * e + tc) * UN + k
                (k0, rows), s = HK[k], (tc * UN + k) % 2
                cols = slice(TC * tc, TC * tc + TC)
                if not (is_at(e, 0) and tc == 0 and k < 2):
                    pe.wait_ge(multiplied, u - 1)
                product(aps[0:rows, s, :], [(W1 + k0, rows, b, P, f_hi[:, cols], f_lo[:, cols])])
                product(bps[0:rows, s, :], [(W3 + k0, rows, b, P, f_hi[:, cols], f_lo[:, cols])]).then_inc(ab_ready, 1)

            def output(e, b, tc):
                n = NCH * e + tc
                pe.wait_ge(low, UN * (n + 1))
                if not (is_at(e, 0) and tc < 2):
                    pe.wait_ge(weighted, n - 1)
                product(ops[:, tc % 2, :], [(W2 + C * k, C, b, rows, h_hi[0:rows, tc % 2, k, :], h_lo[0:rows, tc % 2, k, :])
                                            for k, (_, rows) in enumerate(HK)]).then_inc(o_ready, 1)

            def body(e, b):
                pe.wait_ge(w_low, e + 1)
                for tc in range(NCH):
                    if is_at(e, 0):
                        pe.wait_ge(f_split, tc + 1)
                    for k in range(UN):
                        hidden(e, b, tc, k)
                        if is_at(e, 0) and tc == 0 and k == 0:
                            router()
                    if tc:
                        output(e, b, tc - 1)
                        if is_at(e, 0) and tc == 1:
                            pe.wait_ge(wgt_ready, 1)
                            pe.transpose(xps[:, 1, 0:P], wgt[:, :, :].rearrange("p t e -> p (t e)"), ident[:, :]).then_inc(wgt_ps, 1)
                    elif not is_at(e, 0):
                        output(e - 1, 1 - b, NCH - 1)
            pairs(pe, body)
            output(NE - 1, 1, NCH - 1)
            for q in range(NCH):
                pe.wait_ge(combined, NCH * (NE - 1) + q + 1)
                if q >= 2:
                    pe.wait_ge(total, q - 1)
                for k in range(4):
                    j = 4 * q + k
                    mm = pe.transpose(xps[:, q % 2, P * k:P * k + P], acc[:, P * j:P * j + P], ident[:, :])
                mm.then_inc(acc_ps, 1)


def program(nc, d, out, stop_after=None):
    with ExitStack() as ctx:
        m = Names(nc, ctx)
        x_sb = m.sb("x_sb", [P, NT, C])
        ident = m.sb("ident_sb", [P, P])
        gstat = m.sb("gstat", [P, NT, 6])
        with ExitStack() as gctx:
            g = Names(nc, gctx)
            values = g.sb("g_values", [P, NT, HV * (H - 1) + HW])
            er08 = g.sb("g_er08", [P, N])
            cj = g.sb("g_cj", [FR, N])
            ci = g.sb("g_ci", [FR, GROUPS])
            el08 = g.sb("g_el08", [P, GROUPS])
            feat = g.sb("g_feat", [P, 2, N])
            wlog = g.sb("g_wlog", [P, P])
            mask = g.sb("g_mask", [P, 2, N])
            args = (nc, d, x_sb, values, er08, cj, ci, el08, feat, wlog, ident, mask)
            graph_setup(*args)
            graph_attention(*args, gstat)
        if stop_after == "graph":
            done = m.sem("dbg")
            block = ctx.enter_context(nc.Block())

            @block.sync
            def _(sp):
                sp.dma_start(out.rearrange("(t p) c -> p t c", p=P), x_sb[:, :, :]).then_inc(done, 16)
                sp.wait_ge(done, 16)
            return
        y = m.sb("y_sb", [P, NT, C])
        ystat = m.sb("ystat", [P, NT, 6])
        weights_of = (m.sb("ex_raw", [P, 2, WCOLS]), m.sb("ex_w_hi", [P, 2, WCOLS], F32R), m.sb("ex_w_lo", [P, 2, WCOLS], F32R),
                      [m.sem(f"ex_w_in{b}") for b in range(2)], m.sem("ex_w_high"), m.sem("ex_w_low"))
        with ExitStack() as actx:
            a = Names(nc, actx)
            u_sb = a.sb("u_sb", [P, NKV, N])
            with ExitStack() as qctx:
                q = Names(nc, qctx)
                qs = q.sb("q_stack", [3 * HD + 1, NH, N], F32R)
                ks = q.sb("k_stack", [3 * HD + 1, NKV, N], F32R)
                vx = q.sb("v_values", [P, NT, NKV, VW])
                identb = q.sb("identb", [P, P], BF16)
                cutb = q.sb("cutb", [P, 2, TC], BF16)
                stat = q.sb("bi_stat", [P, 10, NT])
                q_hi, q_lo = q.sb("bi_q_hi", [P, 4, TC], F32R), q.sb("bi_q_lo", [P, 4, TC], F32R)
                k_hi, k_lo = q.sb("bi_k_hi", [P, 2, TC], F32R), q.sb("bi_k_lo", [P, 2, TC], F32R)
                k_in = [q.sem(f"k_in{g}") for g in range(NKV)]
                q_in = [[q.sem(f"q_in{g}{c}") for c in range(2)] for g in range(NKV)]
                shared = (identb, cutb, stat, q_hi, q_lo, k_hi, k_lo, k_in, q_in)
                block_input(nc, d, x_sb, y, ident, gstat, qs, ks, vx, *shared)
                causal_attention(nc, d, x_sb, y, qs, ks, vx, ident, u_sb, *shared)
            project(nc, d, y, u_sb, ident, ystat, weights_of)
        experts(nc, d, out, x_sb, y, ident, ystat, weights_of)


def lay_out(x, adj, L0_gnn_positions, L0_gnn_curv_feats, L0_gnn_W, L0_gnn_a_l, L0_gnn_a_r, L0_gnn_Wc, L0_gnn_gate,
            L0_ffn_ln1_w, L0_ffn_ln2_w, L0_ffn_wq, L0_ffn_wk, L0_ffn_wv, L0_ffn_wo, L0_ffn_router_w, L0_ffn_w1,
            L0_ffn_w2, L0_ffn_w3):
    a = np.asarray
    curv = a(L0_gnn_curv_feats)
    wc = a(L0_gnn_Wc)
    curvw = np.ones((P, P), np.float32)
    curvw[:FR] = np.tile(wc.T, (GI, GI))
    curvw[CJ_ROW:PAD_ROW] = np.tile(wc.T, (1, GI))
    arrays = {
        "x": a(x), "adj": a(adj),
        "WT": a(L0_gnn_W).T,
        "a_rl": np.stack([a(L0_gnn_a_r).reshape(-1), a(L0_gnn_a_l).reshape(-1)], 1),
        "curvw": curvw, "curvT": curv.T, "curv_i": curv.reshape(GROUPS, FR).T,
        "gate": a(L0_gnn_gate).reshape(1, 1),
        "ln1": a(L0_ffn_ln1_w).reshape(C, 1), "ln2": a(L0_ffn_ln2_w).reshape(C, 1),
        "wvT": a(L0_ffn_wv).T, "woT": a(L0_ffn_wo).T, "routerT": a(L0_ffn_router_w).T,
    }
    w2t = np.zeros((NE, len(HK) * P, C), np.float32)
    w2t[:, :HID] = a(L0_ffn_w2).transpose(0, 2, 1)
    w2t = w2t.reshape(NE, len(HK), P, C).transpose(0, 2, 1, 3).reshape(NE, P, len(HK) * C)
    arrays["experts"] = np.concatenate([a(L0_ffn_w1).transpose(0, 2, 1), a(L0_ffn_w3).transpose(0, 2, 1), w2t], 2)
    for name, w in (("wqT", a(L0_ffn_wq)), ("wkT", a(L0_ffn_wk))):
        partner = w.reshape(-1, 2, HD // 2, C)[:, ::-1].reshape(w.shape)
        arrays[name] = np.stack([w.T, partner.T])
    arrays.update(constants())
    return {k: np.ascontiguousarray(v) for k, v in arrays.items()}


def kernel(**inputs):
    import concourse.bacc as bacc
    from concourse.bass_utils import run_bass_kernel_spmd

    nc = bacc.Bacc("TRN2", target_bir_lowering=False, num_devices=1)
    arrays = lay_out(**inputs)
    aps = {name: nc.dram_tensor(f"in_{name}", a.shape, mybir.dt.from_np(a.dtype), kind="ExternalInput").ap()
           for name, a in arrays.items()}
    out = nc.dram_tensor("out", (N, C), F32, kind="ExternalOutput").ap()
    program(nc, aps, out)
    r = run_bass_kernel_spmd(nc, [{f"in_{name}": a for name, a in arrays.items()}], core_ids=[0])
    return r.results[0]["out"]
```
